# Optimizing a Trainium2 kernel written in Bass

```python
import numpy as np
import jax
import jax.numpy as jnp

def _softmax(x, axis=-1):
    return jax.nn.softmax(x, axis=axis)
def _gelu(x):
    return jax.nn.gelu(x, approximate=True)
def _silu(x):
    return jax.nn.silu(x)
def _sigmoid(x):
    return jax.nn.sigmoid(x)
def _layernorm(x, axis=-1, eps=1e-5):
    m = jnp.mean(x, axis=axis, keepdims=True)
    v = jnp.var(x, axis=axis, keepdims=True)
    return (x - m) / jnp.sqrt(v + eps)
def _scatter_add(tgt, idx, src, axis=0):
    return tgt.at[idx].add(src)
def _segment_sum(src, seg, n):
    return jax.ops.segment_sum(src, seg, n)

kernel_name = 'mk_conv_attn_hybrid_d2_conv_nhwc128_8b78d5'

def setup_inputs(seed: int = 0):
    np.random.seed(seed)
    _w = jnp.asarray
    def _rec_inputs():
        import jax
        import jax.numpy as jnp
        _gk = jax.random.key(seed)
        x = -0.0005207 + 1.001 * jax.random.normal(jax.random.fold_in(_gk, 1), (4, 32, 128, 128), jnp.float32)
        return x
    x = _rec_inputs()
    def _L0_conv_setup():
        import jax, jax.numpy as jnp
        import numpy as np
        N_HEADS = 16
        TEMPERATURE = 1.0
        EPS = 1e-05

        def _gelu(z):
            return jax.nn.gelu(z, approximate=False)

        def instance_norm(x, g, b):
            mu = jnp.mean(x, axis=(-2, -1), keepdims=True)
            var = jnp.var(x, axis=(-2, -1), keepdims=True)
            return (x - mu) * jax.lax.rsqrt(var + EPS) * g[:, None, None] + b[:, None, None]

        def conv1x1(x, w, b):
            return jnp.einsum('bihw,io->bohw', x, w) + b[None, :, None, None]

        def fourier_resample(x, out_shape):
            if tuple(x.shape[-2:]) == tuple(out_shape):
                return x
            Ho, Wo = out_shape
            xft = jnp.fft.rfftn(x, axes=(-2, -1), norm='forward')
            out = jnp.zeros(x.shape[:-2] + (Ho, Wo // 2 + 1), dtype=xft.dtype)
            hk = min(x.shape[-2], Ho) // 2
            wk = min(xft.shape[-1], Wo // 2 + 1)
            out = out.at[..., :hk, :wk].set(xft[..., :hk, :wk])
            out = out.at[..., -hk:, :wk].set(xft[..., -hk:, :wk])
            return jnp.fft.irfftn(out, s=out_shape, axes=(-2, -1), norm='forward')

        def spectral_conv(x, w, out_shape):
            wc = w[..., 0] + 1j * w[..., 1]
            mh = wc.shape[2] // 2
            mw = wc.shape[3]
            Ho, Wo = out_shape
            xft = jnp.fft.rfftn(x, axes=(-2, -1), norm='forward')
            top = jnp.einsum('bihw,iohw->bohw', xft[:, :, :mh, :mw], wc[:, :, :mh])
            bot = jnp.einsum('bihw,iohw->bohw', xft[:, :, -mh:, :mw], wc[:, :, mh:])
            out_ft = jnp.zeros((x.shape[0], wc.shape[1], Ho, Wo // 2 + 1), dtype=xft.dtype)
            out_ft = out_ft.at[:, :, :mh, :mw].set(top)
            out_ft = out_ft.at[:, :, -mh:, :mw].set(bot)
            return jnp.fft.irfftn(out_ft, s=out_shape, axes=(-2, -1), norm='forward')

        def fno_layer(x, spec_w, skip_w, skip_b, out_shape, norm=None, act=None):
            xs = fourier_resample(conv1x1(x, skip_w, skip_b), out_shape)
            xf = spectral_conv(x, spec_w, out_shape)
            if norm is not None:
                xf = instance_norm(xf, *norm)
            y = xf + xs
            return act(y) if act is not None else y

        def codano_forward(x, key_w, key_skip_w, key_skip_b, query_w, query_skip_w, query_skip_b, value_w, value_skip_w, value_skip_b, proj_w, proj_skip_w, proj_skip_b, norm1_g, norm1_b, attn_norm_g, attn_norm_b, norm2_g, norm2_b, mixer_w1, mixer_skip_w1, mixer_skip_b1, mixer_norm_g1, mixer_norm_b1, mixer_w2, mixer_skip_w2, mixer_skip_b2, mixer_norm_g2, mixer_norm_b2, mixer_out_g, mixer_out_b):
            b, t, H, W = x.shape
            tokens = x.reshape(b * t, 1, H, W)
            tokens_norm = instance_norm(tokens, norm1_g, norm1_b)
            Hs, Ws = (H // 2, W // 2)
            k = fno_layer(tokens_norm, key_w, key_skip_w, key_skip_b, (Hs, Ws))
            q = fno_layer(tokens_norm, query_w, query_skip_w, query_skip_b, (Hs, Ws))
            v = fno_layer(tokens_norm, value_w, value_skip_w, value_skip_b, (H, W))

            def heads_flat(z):
                hh, ww = z.shape[-2:]
                return z.reshape(b, t, N_HEADS, hh * ww).transpose(0, 2, 1, 3)
            kf, qf, vf = (heads_flat(k), heads_flat(q), heads_flat(v))
            scale = jnp.sqrt(jnp.asarray(kf.shape[-1], jnp.float32)) * TEMPERATURE
            dprod = jax.nn.softmax(jnp.einsum('bhtd,bhsd->bhts', qf, kf) / scale, axis=-1)
            attn = jnp.einsum('bhts,bhsd->bhtd', dprod, vf)
            attn = attn.transpose(0, 2, 1, 3).reshape(b * t, N_HEADS, H, W)
            attn = fno_layer(attn, proj_w, proj_skip_w, proj_skip_b, (H, W))
            attn = instance_norm(attn + tokens, attn_norm_g, attn_norm_b)
            m = instance_norm(attn, norm2_g, norm2_b)
            m = fno_layer(m, mixer_w1, mixer_skip_w1, mixer_skip_b1, (H, W), norm=(mixer_norm_g1, mixer_norm_b1), act=_gelu)
            m = fno_layer(m, mixer_w2, mixer_skip_w2, mixer_skip_b2, (H, W), norm=(mixer_norm_g2, mixer_norm_b2))
            out = instance_norm(m, mixer_out_g, mixer_out_b) + attn
            return out.reshape(b, t, H, W)
        key = jax.random.key(seed)
        ks = list(jax.random.split(key, 32))
        f32 = jnp.float32

        def W_(k, shape, s=0.02):
            return (s * jax.random.normal(k, shape)).astype(f32)
        B, T, H, Wd = (4, 32, 128, 128)
        mh_s, mw_s = (16, 9)
        mh_f, mw_f = (32, 17)
        return {'x': jax.random.normal(ks[0], (B, T, H, Wd), dtype=f32), 'key_w': W_(ks[1], (1, N_HEADS, mh_s, mw_s, 2)), 'key_skip_w': W_(ks[2], (1, N_HEADS), 0.5), 'key_skip_b': W_(ks[3], (N_HEADS,)), 'query_w': W_(ks[4], (1, N_HEADS, mh_s, mw_s, 2)), 'query_skip_w': W_(ks[5], (1, N_HEADS), 0.5), 'query_skip_b': W_(ks[6], (N_HEADS,)), 'value_w': W_(ks[7], (1, N_HEADS, mh_s, mw_s, 2)), 'value_skip_w': W_(ks[8], (1, N_HEADS), 0.5), 'value_skip_b': W_(ks[9], (N_HEADS,)), 'proj_w': W_(ks[10], (N_HEADS, 1, mh_f, mw_f, 2)), 'proj_skip_w': W_(ks[11], (N_HEADS, 1), 0.25), 'proj_skip_b': W_(ks[12], (1,)), 'norm1_g': jnp.ones((1,), f32), 'norm1_b': jnp.zeros((1,), f32), 'attn_norm_g': jnp.ones((1,), f32), 'attn_norm_b': jnp.zeros((1,), f32), 'norm2_g': jnp.ones((1,), f32), 'norm2_b': jnp.zeros((1,), f32), 'mixer_w1': W_(ks[13], (1, 1, mh_f, mw_f, 2)), 'mixer_skip_w1': W_(ks[14], (1, 1), 0.5), 'mixer_skip_b1': W_(ks[15], (1,)), 'mixer_norm_g1': jnp.ones((1,), f32), 'mixer_norm_b1': jnp.zeros((1,), f32), 'mixer_w2': W_(ks[16], (1, 1, mh_f, mw_f, 2)), 'mixer_skip_w2': W_(ks[17], (1, 1), 0.5), 'mixer_skip_b2': W_(ks[18], (1,)), 'mixer_norm_g2': jnp.ones((1,), f32), 'mixer_norm_b2': jnp.zeros((1,), f32), 'mixer_out_g': jnp.ones((1,), f32), 'mixer_out_b': jnp.zeros((1,), f32)}
    _L0_conv_all = _L0_conv_setup()
    _L0_conv_in = {k: v for k, v in _L0_conv_all.items() if k in ('key_w', 'key_skip_w', 'key_skip_b', 'query_w', 'query_skip_w', 'query_skip_b', 'value_w', 'value_skip_w', 'value_skip_b', 'proj_w', 'proj_skip_w', 'proj_skip_b', 'norm1_g', 'norm1_b', 'attn_norm_g', 'attn_norm_b', 'norm2_g', 'norm2_b', 'mixer_w1', 'mixer_skip_w1', 'mixer_skip_b1', 'mixer_norm_g1', 'mixer_norm_b1', 'mixer_w2', 'mixer_skip_w2', 'mixer_skip_b2', 'mixer_norm_g2', 'mixer_norm_b2', 'mixer_out_g', 'mixer_out_b', )}
    del _L0_conv_all

    def _L1_attn_setup():
        import jax, jax.numpy as jnp
        import numpy as np
        EMBED_DIM = 128
        GAMMA = 1.0
        B, S = (4, 4096)
        key = jax.random.key(seed)
        ks = jax.random.split(key, 6)
        return {'inputs': jax.random.normal(ks[0], (B, S, EMBED_DIM), dtype=jnp.float32), 'rotation_params': jax.random.normal(ks[1], (EMBED_DIM * EMBED_DIM,), dtype=jnp.float32), 'entangle_params': jax.random.normal(ks[2], (EMBED_DIM * EMBED_DIM,), dtype=jnp.float32), 'Wq': jax.random.normal(ks[3], (EMBED_DIM, EMBED_DIM), dtype=jnp.float32) / np.sqrt(EMBED_DIM), 'Wk': jax.random.normal(ks[4], (EMBED_DIM, EMBED_DIM), dtype=jnp.float32) / np.sqrt(EMBED_DIM), 'Wv': jax.random.normal(ks[5], (EMBED_DIM, EMBED_DIM), dtype=jnp.float32) / np.sqrt(EMBED_DIM)}
    _L1_attn_all = _L1_attn_setup()
    _L1_attn_in = {k: v for k, v in _L1_attn_all.items() if k in ('rotation_params', 'entangle_params', 'Wq', 'Wk', 'Wv', )}
    del _L1_attn_all

    def _L1_ffn_setup():
        import jax, jax.numpy as jnp
        import numpy as np
        B, N, D, C, E, K = (8, 8192, 128, 128, 8, 2)
        key = jax.random.key(seed)
        k0, k1, k2 = jax.random.split(key, 3)
        x = jax.random.normal(k0, (B, N, D), dtype=jnp.float32)
        router_w = jax.random.normal(k1, (D, E), dtype=jnp.float32) * 0.05
        router_b = jnp.zeros((E,), dtype=jnp.float32)
        expert_w = jax.random.normal(k2, (E, D, C), dtype=jnp.float32) * (1.0 / np.sqrt(D))
        expert_b = jnp.zeros((E, C), dtype=jnp.float32)
        return {'x': x, 'router_w': router_w, 'router_b': router_b, 'expert_w': expert_w, 'expert_b': expert_b}
    _L1_ffn_all = _L1_ffn_setup()
    _L1_ffn_in = {k: v for k, v in _L1_ffn_all.items() if k in ('router_w', 'router_b', 'expert_w', 'expert_b', )}
    del _L1_ffn_all

    return {
        "x": x,
        "L0_conv_key_w": _L0_conv_in["key_w"],
        "L0_conv_key_skip_w": _L0_conv_in["key_skip_w"],
        "L0_conv_key_skip_b": _L0_conv_in["key_skip_b"],
        "L0_conv_query_w": _L0_conv_in["query_w"],
        "L0_conv_query_skip_w": _L0_conv_in["query_skip_w"],
        "L0_conv_query_skip_b": _L0_conv_in["query_skip_b"],
        "L0_conv_value_w": _L0_conv_in["value_w"],
        "L0_conv_value_skip_w": _L0_conv_in["value_skip_w"],
        "L0_conv_value_skip_b": _L0_conv_in["value_skip_b"],
        "L0_conv_proj_w": _L0_conv_in["proj_w"],
        "L0_conv_proj_skip_w": _L0_conv_in["proj_skip_w"],
        "L0_conv_proj_skip_b": _L0_conv_in["proj_skip_b"],
        "L0_conv_norm1_g": _L0_conv_in["norm1_g"],
        "L0_conv_norm1_b": _L0_conv_in["norm1_b"],
        "L0_conv_attn_norm_g": _L0_conv_in["attn_norm_g"],
        "L0_conv_attn_norm_b": _L0_conv_in["attn_norm_b"],
        "L0_conv_norm2_g": _L0_conv_in["norm2_g"],
        "L0_conv_norm2_b": _L0_conv_in["norm2_b"],
        "L0_conv_mixer_w1": _L0_conv_in["mixer_w1"],
        "L0_conv_mixer_skip_w1": _L0_conv_in["mixer_skip_w1"],
        "L0_conv_mixer_skip_b1": _L0_conv_in["mixer_skip_b1"],
        "L0_conv_mixer_norm_g1": _L0_conv_in["mixer_norm_g1"],
        "L0_conv_mixer_norm_b1": _L0_conv_in["mixer_norm_b1"],
        "L0_conv_mixer_w2": _L0_conv_in["mixer_w2"],
        "L0_conv_mixer_skip_w2": _L0_conv_in["mixer_skip_w2"],
        "L0_conv_mixer_skip_b2": _L0_conv_in["mixer_skip_b2"],
        "L0_conv_mixer_norm_g2": _L0_conv_in["mixer_norm_g2"],
        "L0_conv_mixer_norm_b2": _L0_conv_in["mixer_norm_b2"],
        "L0_conv_mixer_out_g": _L0_conv_in["mixer_out_g"],
        "L0_conv_mixer_out_b": _L0_conv_in["mixer_out_b"],
        "L1_attn_rotation_params": _L1_attn_in["rotation_params"],
        "L1_attn_entangle_params": _L1_attn_in["entangle_params"],
        "L1_attn_Wq": _L1_attn_in["Wq"],
        "L1_attn_Wk": _L1_attn_in["Wk"],
        "L1_attn_Wv": _L1_attn_in["Wv"],
        "L1_ffn_router_w": _L1_ffn_in["router_w"],
        "L1_ffn_router_b": _L1_ffn_in["router_b"],
        "L1_ffn_expert_w": _L1_ffn_in["expert_w"],
        "L1_ffn_expert_b": _L1_ffn_in["expert_b"],
    }

def reference(x, L0_conv_key_w, L0_conv_key_skip_w, L0_conv_key_skip_b, L0_conv_query_w, L0_conv_query_skip_w, L0_conv_query_skip_b, L0_conv_value_w, L0_conv_value_skip_w, L0_conv_value_skip_b, L0_conv_proj_w, L0_conv_proj_skip_w, L0_conv_proj_skip_b, L0_conv_norm1_g, L0_conv_norm1_b, L0_conv_attn_norm_g, L0_conv_attn_norm_b, L0_conv_norm2_g, L0_conv_norm2_b, L0_conv_mixer_w1, L0_conv_mixer_skip_w1, L0_conv_mixer_skip_b1, L0_conv_mixer_norm_g1, L0_conv_mixer_norm_b1, L0_conv_mixer_w2, L0_conv_mixer_skip_w2, L0_conv_mixer_skip_b2, L0_conv_mixer_norm_g2, L0_conv_mixer_norm_b2, L0_conv_mixer_out_g, L0_conv_mixer_out_b, L1_attn_rotation_params, L1_attn_entangle_params, L1_attn_Wq, L1_attn_Wk, L1_attn_Wv, L1_ffn_router_w, L1_ffn_router_b, L1_ffn_expert_w, L1_ffn_expert_b):
    import jax
    import jax.numpy as jnp
    def _L0_conv_ref(x, key_w, key_skip_w, key_skip_b, query_w, query_skip_w, query_skip_b, value_w, value_skip_w, value_skip_b, proj_w, proj_skip_w, proj_skip_b, norm1_g, norm1_b, attn_norm_g, attn_norm_b, norm2_g, norm2_b, mixer_w1, mixer_skip_w1, mixer_skip_b1, mixer_norm_g1, mixer_norm_b1, mixer_w2, mixer_skip_w2, mixer_skip_b2, mixer_norm_g2, mixer_norm_b2, mixer_out_g, mixer_out_b):
        import jax, jax.numpy as jnp
        import numpy as np
        N_HEADS = 16
        TEMPERATURE = 1.0
        EPS = 1e-05

        def _gelu(z):
            return jax.nn.gelu(z, approximate=False)

        def instance_norm(x, g, b):
            mu = jnp.mean(x, axis=(-2, -1), keepdims=True)
            var = jnp.var(x, axis=(-2, -1), keepdims=True)
            return (x - mu) * jax.lax.rsqrt(var + EPS) * g[:, None, None] + b[:, None, None]

        def conv1x1(x, w, b):
            return jnp.einsum('bihw,io->bohw', x, w) + b[None, :, None, None]

        def fourier_resample(x, out_shape):
            if tuple(x.shape[-2:]) == tuple(out_shape):
                return x
            Ho, Wo = out_shape
            xft = jnp.fft.rfftn(x, axes=(-2, -1), norm='forward')
            out = jnp.zeros(x.shape[:-2] + (Ho, Wo // 2 + 1), dtype=xft.dtype)
            hk = min(x.shape[-2], Ho) // 2
            wk = min(xft.shape[-1], Wo // 2 + 1)
            out = out.at[..., :hk, :wk].set(xft[..., :hk, :wk])
            out = out.at[..., -hk:, :wk].set(xft[..., -hk:, :wk])
            return jnp.fft.irfftn(out, s=out_shape, axes=(-2, -1), norm='forward')

        def spectral_conv(x, w, out_shape):
            wc = w[..., 0] + 1j * w[..., 1]
            mh = wc.shape[2] // 2
            mw = wc.shape[3]
            Ho, Wo = out_shape
            xft = jnp.fft.rfftn(x, axes=(-2, -1), norm='forward')
            top = jnp.einsum('bihw,iohw->bohw', xft[:, :, :mh, :mw], wc[:, :, :mh])
            bot = jnp.einsum('bihw,iohw->bohw', xft[:, :, -mh:, :mw], wc[:, :, mh:])
            out_ft = jnp.zeros((x.shape[0], wc.shape[1], Ho, Wo // 2 + 1), dtype=xft.dtype)
            out_ft = out_ft.at[:, :, :mh, :mw].set(top)
            out_ft = out_ft.at[:, :, -mh:, :mw].set(bot)
            return jnp.fft.irfftn(out_ft, s=out_shape, axes=(-2, -1), norm='forward')

        def fno_layer(x, spec_w, skip_w, skip_b, out_shape, norm=None, act=None):
            xs = fourier_resample(conv1x1(x, skip_w, skip_b), out_shape)
            xf = spectral_conv(x, spec_w, out_shape)
            if norm is not None:
                xf = instance_norm(xf, *norm)
            y = xf + xs
            return act(y) if act is not None else y

        def codano_forward(x, key_w, key_skip_w, key_skip_b, query_w, query_skip_w, query_skip_b, value_w, value_skip_w, value_skip_b, proj_w, proj_skip_w, proj_skip_b, norm1_g, norm1_b, attn_norm_g, attn_norm_b, norm2_g, norm2_b, mixer_w1, mixer_skip_w1, mixer_skip_b1, mixer_norm_g1, mixer_norm_b1, mixer_w2, mixer_skip_w2, mixer_skip_b2, mixer_norm_g2, mixer_norm_b2, mixer_out_g, mixer_out_b):
            b, t, H, W = x.shape
            tokens = x.reshape(b * t, 1, H, W)
            tokens_norm = instance_norm(tokens, norm1_g, norm1_b)
            Hs, Ws = (H // 2, W // 2)
            k = fno_layer(tokens_norm, key_w, key_skip_w, key_skip_b, (Hs, Ws))
            q = fno_layer(tokens_norm, query_w, query_skip_w, query_skip_b, (Hs, Ws))
            v = fno_layer(tokens_norm, value_w, value_skip_w, value_skip_b, (H, W))

            def heads_flat(z):
                hh, ww = z.shape[-2:]
                return z.reshape(b, t, N_HEADS, hh * ww).transpose(0, 2, 1, 3)
            kf, qf, vf = (heads_flat(k), heads_flat(q), heads_flat(v))
            scale = jnp.sqrt(jnp.asarray(kf.shape[-1], jnp.float32)) * TEMPERATURE
            dprod = jax.nn.softmax(jnp.einsum('bhtd,bhsd->bhts', qf, kf) / scale, axis=-1)
            attn = jnp.einsum('bhts,bhsd->bhtd', dprod, vf)
            attn = attn.transpose(0, 2, 1, 3).reshape(b * t, N_HEADS, H, W)
            attn = fno_layer(attn, proj_w, proj_skip_w, proj_skip_b, (H, W))
            attn = instance_norm(attn + tokens, attn_norm_g, attn_norm_b)
            m = instance_norm(attn, norm2_g, norm2_b)
            m = fno_layer(m, mixer_w1, mixer_skip_w1, mixer_skip_b1, (H, W), norm=(mixer_norm_g1, mixer_norm_b1), act=_gelu)
            m = fno_layer(m, mixer_w2, mixer_skip_w2, mixer_skip_b2, (H, W), norm=(mixer_norm_g2, mixer_norm_b2))
            out = instance_norm(m, mixer_out_g, mixer_out_b) + attn
            return out.reshape(b, t, H, W)
        return codano_forward(x, key_w, key_skip_w, key_skip_b, query_w, query_skip_w, query_skip_b, value_w, value_skip_w, value_skip_b, proj_w, proj_skip_w, proj_skip_b, norm1_g, norm1_b, attn_norm_g, attn_norm_b, norm2_g, norm2_b, mixer_w1, mixer_skip_w1, mixer_skip_b1, mixer_norm_g1, mixer_norm_b1, mixer_w2, mixer_skip_w2, mixer_skip_b2, mixer_norm_g2, mixer_norm_b2, mixer_out_g, mixer_out_b)

    def _L1_attn_ref(inputs, rotation_params, entangle_params, Wq, Wk, Wv):
        import jax, jax.numpy as jnp
        import numpy as np
        EMBED_DIM = 128
        GAMMA = 1.0
        B, S = (4, 4096)
        D = EMBED_DIM
        rot = rotation_params.reshape(D, -1)
        ent = entangle_params.reshape(D, -1)
        rotated = jnp.einsum('bsd,de->bse', inputs, rot)
        entangled = jnp.einsum('bsd,de->bse', inputs, ent)
        Q = jnp.einsum('bsd,ed->bse', rotated, Wq)
        K = jnp.einsum('bsd,ed->bse', entangled, Wk)
        V = jnp.einsum('bsd,ed->bse', inputs, Wv)
        q2 = jnp.sum(Q * Q, axis=-1)
        k2 = jnp.sum(K * K, axis=-1)
        qk = jnp.einsum('bqd,bkd->bqk', Q, K)
        dist2 = q2[:, :, None] + k2[:, None, :] - 2.0 * qk
        scores = jnp.exp(-GAMMA * dist2)
        attn = jax.nn.softmax(scores, axis=-1)
        return jnp.einsum('bqk,bkd->bqd', attn, V)

    def _L1_ffn_ref(x, router_w, router_b, expert_w, expert_b):
        import jax, jax.numpy as jnp
        import numpy as np
        B, N, D, C, E, K = (8, 8192, 128, 128, 8, 2)
        router_probs = jax.nn.softmax(x @ router_w + router_b, axis=-1)
        top_p, top_i = jax.lax.top_k(router_probs, K)
        top_p = top_p / jnp.sum(top_p, axis=-1, keepdims=True)
        expert_out = jnp.einsum('bnd,edc->bnec', x, expert_w) + expert_b
        gathered = jnp.take_along_axis(expert_out, top_i[..., None], axis=2)
        return jnp.einsum('bnk,bnkc->bnc', top_p, gathered)

    def _gn(v, G=32, eps=1e-5):
        B_, H_, W_, C_ = v.shape
        g = v.reshape(B_, H_, W_, G, C_ // G)
        m = jnp.mean(g, axis=(1, 2, 4), keepdims=True)
        s = jnp.var(g, axis=(1, 2, 4), keepdims=True)
        return ((g - m) / jnp.sqrt(s + eps)).reshape(v.shape)

    def _ln_c(v, eps=1e-6):
        m = jnp.mean(v, axis=-1, keepdims=True)
        s = jnp.var(v, axis=-1, keepdims=True)
        return (v - m) / jnp.sqrt(s + eps)

    def _ln_t(v, eps=1e-5):
        m = jnp.mean(v, axis=-1, keepdims=True)
        s = jnp.var(v, axis=-1, keepdims=True)
        return (v - m) / jnp.sqrt(s + eps)

    def _to_tokens(v):
        B_, H_, W_, C_ = v.shape
        return v.reshape(B_, H_ * W_, C_)
    def _from_tokens(t, like):
        return t.reshape(like.shape)

    x = x + _L0_conv_ref(_gn(x), L0_conv_key_w, L0_conv_key_skip_w, L0_conv_key_skip_b, L0_conv_query_w, L0_conv_query_skip_w, L0_conv_query_skip_b, L0_conv_value_w, L0_conv_value_skip_w, L0_conv_value_skip_b, L0_conv_proj_w, L0_conv_proj_skip_w, L0_conv_proj_skip_b, L0_conv_norm1_g, L0_conv_norm1_b, L0_conv_attn_norm_g, L0_conv_attn_norm_b, L0_conv_norm2_g, L0_conv_norm2_b, L0_conv_mixer_w1, L0_conv_mixer_skip_w1, L0_conv_mixer_skip_b1, L0_conv_mixer_norm_g1, L0_conv_mixer_norm_b1, L0_conv_mixer_w2, L0_conv_mixer_skip_w2, L0_conv_mixer_skip_b2, L0_conv_mixer_norm_g2, L0_conv_mixer_norm_b2, L0_conv_mixer_out_g, L0_conv_mixer_out_b)
    t = _to_tokens(x)
    t = t + _L1_attn_ref(_ln_t(t), L1_attn_rotation_params, L1_attn_entangle_params, L1_attn_Wq, L1_attn_Wk, L1_attn_Wv)
    t = t + _L1_ffn_ref(_ln_t(t), L1_ffn_router_w, L1_ffn_router_b, L1_ffn_expert_w, L1_ffn_expert_b)
    x = _from_tokens(t, x)
    return x


_drawn_inputs = setup_inputs


def setup_inputs(seed=0):
    import zlib

    import numpy as np

    out = dict(_drawn_inputs(seed))
    spreads = {'L1_ffn_router_b': (0.0, 0.1), 'L1_ffn_expert_b': (0.0, 0.268)}
    factors = {'L0_conv_key_w': 64.0,
     'L0_conv_key_skip_b': 64.0,
     'L0_conv_query_w': 64.0,
     'L0_conv_query_skip_b': 64.0,
     'L0_conv_value_w': 4.207,
     'L0_conv_value_skip_b': 64.0,
     'L1_attn_Wv': 2.762}
    for name, (base, spread) in spreads.items():
        noise = np.random.default_rng([zlib.crc32(name.encode()), seed]).standard_normal(out[name].shape)
        drawn = base * np.exp(spread * noise) if base else spread * noise
        out[name] = jnp.asarray(drawn.astype(out[name].dtype))
    for name, factor in factors.items():
        out[name] = (out[name] * factor).astype(out[name].dtype)
    return out
```

```python
from contextlib import ExitStack

import numpy as np
import concourse.bass as bass
from concourse import mybir

F32 = mybir.dt.float32
ALU = mybir.AluOpType
ACT = mybir.ActivationFunctionType
AX = mybir.AxisListType

P = 128
NB, NT, NH, NW = 4, 32, 128, 128
NI = NB * NT
HEADS = 16
K33 = 33
FQ = 2 * K33
K17 = 17
FM = 2 * K17
ROWS = 2 * K17
NM = ROWS * K17
MT = [(m, min(P, NM - m)) for m in range(0, NM, P)]
LOWT = 4
HC = 34
GRP = 4
NG = NI // GRP
UN = 4
PIX = NH * NW
EPS = 1e-5
D = 128
SEQ = NT * NH
KT = SEQ // P
QC = 512
NQC = SEQ // QC
EXPERTS = 8
SCALARS = ['L0_conv_norm1_g', 'L0_conv_norm1_b', 'L0_conv_attn_norm_g', 'L0_conv_attn_norm_b',
           'L0_conv_norm2_g', 'L0_conv_norm2_b', 'L0_conv_mixer_skip_w1', 'L0_conv_mixer_skip_b1',
           'L0_conv_mixer_norm_g1', 'L0_conv_mixer_norm_b1', 'L0_conv_mixer_skip_w2',
           'L0_conv_mixer_skip_b2', 'L0_conv_mixer_norm_g2', 'L0_conv_mixer_norm_b2',
           'L0_conv_mixer_out_g', 'L0_conv_mixer_out_b', 'L0_conv_proj_skip_b']


def tables():
    n = np.arange(P)[:, None]
    k = np.arange(K33)[None, :]
    dft = np.concatenate([np.cos(2 * np.pi * n * k / P), np.sin(2 * np.pi * n * k / P)], 1) / P
    dft[:, K33] = 0.0
    k = np.arange(K17)[:, None]
    idft = np.zeros((P, P))
    idft[:K17] = np.cos(2 * np.pi * k * n.T / P)
    idft[K17:FM] = np.sin(2 * np.pi * k * n.T / P)
    twice = np.where(np.arange(P) % K17 > 0, 2.0, 1.0)[:, None]
    batch = np.kron(np.eye(NB), np.ones((NT, NT))) / NT
    low = np.zeros((ROWS, K17))
    low[0:8, 1:9] = 2
    low[K17 + 1:K17 + 9, 1:9] = 2
    low[1:9, 0] = 2
    low[0, 0] = 1
    lowm = np.zeros(P * len(MT))
    lowm[:NM] = 64 * low.ravel()
    var = np.zeros((2, K17, 2, K17))
    var[:, 1:, :, 1:] = 1
    var[0, 0, :, 1:] = 2
    var[:, 1:, 0, 0] = 0.5
    tie = np.arange(EXPERTS)[None, :] < np.arange(EXPERTS)[:, None]

    def on_all(a):
        return np.broadcast_to(a.reshape(1, -1), (P, a.size))
    parts = [('ident', np.eye(P)), ('tie', on_all(tie)), ('dft', dft), ('rows', idft), ('cols', idft * twice),
             ('batch', batch), ('low', lowm.reshape(len(MT), P).T), ('var', on_all(var))]
    at, where = 0, {}
    for name, a in parts:
        where[name] = (at, at + a.shape[1])
        at += a.shape[1]
    return np.concatenate([a for _, a in parts], 1).astype(np.float32), where


class Names(dict):

    def __getattr__(self, name):
        return self[name]


class Views:
    pass


class Chain:

    def __init__(self, eng, sem):
        self.eng, self.sem, self.n, self.off = eng, sem, 0, 0

    def step(self, ins):
        ins.then_inc(self.sem, 1)
        self.n += 1
        self.eng.wait_ge(self.sem, self.off + self.n)

    def enter(self, it, per):
        self.before, self.per = self.n, per
        self.off = it * per

    def leave(self, count):
        assert self.n - self.before == self.per, (self.n - self.before, self.per)
        self.n = self.before + self.per * count
        self.off = 0


def reached(eng, sem, value):
    if not (isinstance(value, int) and value <= 0):
        eng.wait_ge(sem, value)


def over(ap, axis, n):
    shape = list(ap.shape)
    return ap.unsqueeze(axis).to_broadcast(shape[:axis] + [n] + shape[axis:])


def semaphores(nc, held, stage, names):
    made = {n: nc.alloc_semaphore(f"{stage}_{n}") for n in names.split()}
    held.extend(made.values())
    return Names(made)


def memory(nc, ctx, where):
    m = Views()

    def sb(scope, name, shape):
        return scope.enter_context(nc.sbuf_tensor(name, shape, F32))

    m.a = sb(ctx, "images_a", [P, NI, NW])
    m.b = sb(ctx, "images_b", [P, NI, NW])
    keep = sb(ctx, "keep", [P, where['tie'][1]])
    m.keep = keep
    m.ident = keep[:, 0:P]
    m.tie = keep[:, P:].rearrange("p (i j) -> p i j", i=EXPERTS)
    small = sb(ctx, "small", [P, 208])
    m.sc = small[:, 0:len(SCALARS)]
    m.skips = small[:, 32:96]
    m.biases = small[:, 96:144]
    m.col = small[:, 144:176]
    m.gram = small[:, 176:208]
    m.ps = [ctx.enter_context(nc.psum_tensor(f"bank{i}", [P, 512], F32)) for i in range(8)]

    with ExitStack() as l0:
        c0 = where['dft'][0]
        m.tab = sb(l0, "table", [P, where['var'][1] - c0])

        def tab(name, rows=P):
            lo, hi = where[name]
            return m.tab[0:rows, lo - c0:hi - c0]
        m.dft = tab('dft')
        m.dft17 = m.dft.rearrange("p (s k) -> p s k", s=2)[:, :, 0:K17]
        m.rows, m.cols, m.batch, m.low, m.var = tab('rows', FM), tab('cols', FM), tab('batch'), tab('low'), tab('var')
        pair = sb(l0, "pair", [P, 2, 2 * NM])
        m.wraw = pair[0:64, 0, :].rearrange("p (r k c) -> p r k c", r=ROWS, c=2)
        m.weff = pair[0:64, 1, :].rearrange("p (c m) -> p c m", c=2)
        m.feat = pair[:, 0, :].rearrange("p (x y) -> p x y", x=FM)
        m.coef = pair[:, 1, :].rearrange("p (x y) -> p x y", x=FM)
        mixw = sb(l0, "mixer_weights", [P, 2 * NM])
        m.mixw = mixw[:, :].rearrange("p (r k c) -> p r k c", r=ROWS, c=2)
        f = sb(l0, "features", [P, FQ * FQ])
        m.ft = f[:, :].rearrange("p (x y) -> p x y", x=FQ)
        m.half17 = f[:, 0:P * FM].rearrange("p (t x) -> p t x", t=P)
        g = sb(l0, "spare", [P, HC * P])
        m.spare = g[:, :]
        m.gramT = g[:, :].rearrange("p (c t) -> p c t", c=HC)
        m.coefT = g[0:FM, :].rearrange("p (x t) -> p x t", x=FM)
        m.modes = sb(l0, "modes", [P, 2, NM])
        r = sb(l0, "transposed", [P, 1920])
        m.turned = r[:, :]
        m.modesT = r[:, 0:1280].rearrange("p (k c t) -> p k c t", k=5, c=2)
        m.wT = r[:, 1280:1920].rearrange("p (k c h) -> p k c h", k=5, c=2)
        m.stat = r[:, 0:768].rearrange("p (t s) -> p t s", t=P)
        m.aff = r[:, 768:768 + 8 * P].rearrange("p (k t) -> p k t", k=8)
        m.stage = sb(l0, "coef_stage", [P, 2, (GRP - 1) * FM + P])
        m.half = sb(l0, "half_inverse", [P, 2, GRP * NW])
        m.ust = sb(l0, "image_stage", [P, 2, GRP, NW])
        m.tmp = m.modes[:, :, 0:GRP * NW].rearrange("p s (t w) -> p s t w", t=GRP)

    b = m.b[:, :, :].rearrange("p a b -> p (a b)")
    m.half33 = b[:, 0:P * FQ].rearrange("p (t x) -> p t x", t=P)
    m.load = b[:, 12804:12804 + 2048].rearrange("p (s t w) -> p s t w", s=4, t=GRP)
    m.prod = b[:, 0:8192].rearrange("p (k h t) -> p k h t", k=4, h=HEADS)
    m.hg = b[:, 8448:8448 + FQ * FQ]
    m.probT = b[:, 8448:10496].rearrange("p (h t) -> p h t", h=HEADS)
    m.probD = b[:, 0:2048].rearrange("p (h t) -> p h t", h=HEADS)
    m.mixD = b[:, 2048:2176]
    m.mixT = b[:, 2176:2304]
    m.mixA = b[:, 2304:2432]
    m.score, m.expo, m.prob = (b[:, 10496 + 512 * i:11008 + 512 * i].rearrange("p (h s) -> p h s", h=HEADS)
                               for i in range(3))
    m.dcq = b[0:1, 12804:13316].rearrange("p (h s) -> p h s", h=HEADS)
    m.dck = b[0:1, 13316:15364].rearrange("p (h t) -> p h t", h=HEADS)
    m.wk = b[:, 15364:16384]
    m.zprod = b[:, 0:4096].rearrange("p (s k h t) -> p s k h t", s=2, k=4, h=4)
    m.zsum = b[:, 4096:8192].rearrange("p (c h t) -> p c h t", c=2, h=HEADS)

    m.st = sb(ctx, "row_stats", [P, NI, 6])
    with ExitStack() as l1:
        m.kT = sb(l1, "keys_T", [P, SEQ])
        m.qT = sb(l1, "queries_T", [P, SEQ])
        m.q2 = sb(l1, "query_norms", [P, SEQ])
        m.v = sb(l1, "values", [P, KT, D + 1])
        m.dist = sb(l1, "distances", [P, 2, QC])
        m.prb = sb(l1, "weights", [P, 2, QC])
        m.maps = sb(l1, "maps", [P, 3, D])
        m.k2 = sb(l1, "key_norms", [P, KT])
        m.rden = sb(l1, "reciprocals", [P, 8])
        m.halves = sb(l1, "halves", [P, P])
    with ExitStack() as l2:
        m.ln = sb(l2, "normed", [P, 2, GRP, D])
        m.w8 = sb(l2, "expert_weights", [P, EXPERTS * D])
        m.lnT = sb(l2, "normed_T", [P, 2, GRP, P])
        m.rw = sb(l2, "router_weights", [P, EXPERTS])
        m.rb = sb(l2, "router_biases", [P, EXPERTS])
        m.eb = sb(l2, "expert_biases", [EXPERTS, D])
        m.gT = sb(l2, "gates_T", [EXPERTS, 2, GRP, P])
        m.pa = sb(l2, "scaled_a", [P, 2, 4, D])
        m.pb = sb(l2, "scaled_b", [P, 2, 4, D])
        m.pc = sb(l2, "scaled_sum", [P, 2, 4, D])
        m.y = sb(l2, "group_result", [P, 2, GRP, D])
        m.rk = sb(l2, "ranks", [P, 2, GRP, EXPERTS, EXPERTS])
        m.gt = sb(l2, "gates", [P, 2, 6, GRP, EXPERTS])
        m.g1 = sb(l2, "gate_sums", [P, 4, GRP])
        m.fac = sb(l2, "row_factors", [P, 4, NI])
    return m



def stage_tokens(nc, held, m, ins, tok, const):
    s = semaphores(nc, held, "tokens", "tables x weights cleared scalars v sums averaged added rooted stored ready")
    x = ins['x'].rearrange("b t h w -> (b t) h w")
    Q = NH // 4
    nt = m.keep.shape[1]

    with nc.Block() as block:
        @block.sync
        def _(sp):
            for q in range(4):
                sp.dma_start(m.a[:, q * Q:q * Q + Q, :], x[:, q * Q:q * Q + Q, :]).then_inc(s.x, 16)
            sp.wait_ge(s.ready, 1)
            for q in range(4):
                sp.dma_start(tok[:, q * Q:q * Q + Q, :], m.a[:, q * Q:q * Q + Q, :]).then_inc(s.stored, 16)
            sp.wait_ge(s.stored, 64)

        @block.gpsimd
        def _(pool):
            pool.memset(m.wraw, 0.0).then_inc(s.cleared, 1)
            pool.memset(m.mixw, 0.0).then_inc(s.cleared, 1)
            pool.memset(m.turned, 0.0)

        @block.scalar
        def _(act):
            act.dma_start(m.keep[:, :], const[:, 0:nt]).then_inc(s.tables, 16)
            act.dma_start(m.tab[:, :], const[:, nt:]).then_inc(s.tables, 16)
            act.wait_ge(s.cleared, 2)
            with nc.allow_non_contiguous_dma(reason="skip weights and biases, a few numbers"):
                for i, n in enumerate(SCALARS):
                    src = ins[n]
                    if len(src.shape) == 2:
                        src = src.rearrange("a b -> (a b)")
                    act.dma_start(m.sc[:, i:i + 1], src.partition_broadcast(P)).then_inc(s.scalars, 16)
                for i, n in enumerate(['query', 'key', 'value', 'proj']):
                    w = ins[f'L0_conv_{n}_skip_w'].rearrange("a b -> (a b)")
                    act.dma_start(m.skips[:, 16 * i:16 * i + 16], w.partition_broadcast(P)).then_inc(s.scalars, 16)
                    if n == 'proj':
                        w = ins['L0_conv_proj_w'][:, 0]
                        act.dma_start(m.wraw[48:64, 0:16], w[:, 0:16]).then_inc(s.weights, 16)
                        act.dma_start(m.wraw[48:64, K17 + 1:ROWS], w[:, 31:15:-1]).then_inc(s.weights, 16)
                        continue
                    act.dma_start(m.biases[:, 16 * i:16 * i + 16],
                                  ins[f'L0_conv_{n}_skip_b'].partition_broadcast(P)).then_inc(s.scalars, 16)
                    w = ins[f'L0_conv_{n}_w'][0]
                    act.dma_start(m.wraw[16 * i:16 * i + 16, 0:8, 0:9], w[:, 0:8]).then_inc(s.weights, 16)
                    act.dma_start(m.wraw[16 * i:16 * i + 16, K17 + 1:K17 + 9, 0:9], w[:, 15:7:-1])\
                        .then_inc(s.weights, 16)
                load_mixer(act, m, ins, 1, s.weights)
            act.wait_ge(s.added, 1)
            act.activation(m.spare[:, 320:352], m.spare[:, 320:352], ACT.Sqrt).then_inc(s.rooted, 1)
            act.wait_ge(s.added, 2)
            act.activation(m.col[:, 4:5], m.col[:, 3:4], ACT.Sqrt).then_inc(s.rooted, 1)
            act.wait_ge(s.tables, 32)
            act.wait_ge(s.weights, 16 * 10)
            act.wait_ge(s.scalars, 16 * (len(SCALARS) + 7))

        @block.tensor
        def _(pe):
            pe.wait_ge(s.tables, 32)
            pe.wait_ge(s.sums, 1)
            pe.matmul(m.ps[0][:, 0:32], m.batch, m.spare[:, 192:224], start=True, stop=True).then_inc(s.averaged, 1)
            pe.wait_ge(s.sums, 2)
            pe.matmul(m.ps[1][:, 0:32], m.batch, m.spare[:, 352:384], start=True, stop=True).then_inc(s.averaged, 1)

        @block.vector
        def _(vec):
            c = Chain(vec, s.v)
            gs = m.spare[:, 0:192].rearrange("p (g k) -> p g k", g=32)
            two, mean, var, rstd, work = (m.spare[:, 192 + 32 * i:224 + 32 * i] for i in (0, 1, 5, 4, 6))
            dev = m.spare[:, 384:448].rearrange("p (g k) -> p g k", g=32)
            sq = m.spare[:, 448:512].rearrange("p (g k) -> p g k", g=32)
            vec.wait_ge(s.x, 64)
            with vec.Fori(0, 32) as g:
                c.enter(g, 1)
                c.step(vec.bn_stats(gs[:, g, :], m.a[:, :, bass.ds(g * 4, 4)]))
            c.leave(32)
            vec.tensor_tensor(two, gs[:, :, 1], gs[:, :, 4], ALU.add).then_inc(s.sums, 1)
            vec.wait_ge(s.averaged, 1)
            c.step(vec.tensor_scalar(mean, m.ps[0][:, 0:32], 0.5, None, ALU.mult))
            c.step(vec.tensor_tensor(dev, gs[:, :, 1::3], over(mean, 2, 2), ALU.subtract))
            c.step(vec.tensor_tensor(sq, dev, dev, ALU.mult))
            c.step(vec.tensor_reduce(work, sq, AX.X, ALU.add))
            c.step(vec.tensor_scalar(work, work, 0.5, None, ALU.mult))
            c.step(vec.tensor_tensor(var, gs[:, :, 2], gs[:, :, 5], ALU.add))
            vec.scalar_tensor_tensor(out=var, in0=var, scalar=1.0 / 512, in1=work, op0=ALU.mult, op1=ALU.add)\
                .then_inc(s.sums, 1)
            vec.wait_ge(s.averaged, 2)
            vec.tensor_scalar(rstd, m.ps[1][:, 0:32], EPS, None, ALU.add).then_inc(s.added, 1)
            vec.wait_ge(s.rooted, 1)
            c.step(vec.reciprocal(rstd, rstd))
            with vec.Fori(0, 32) as g:
                c.enter(g, 1)
                c.step(vec.tensor_scalar(m.a[:, :, bass.ds(g * 4, 4)], m.a[:, :, bass.ds(g * 4, 4)],
                                         mean[:, bass.ds(g, 1)], rstd[:, bass.ds(g, 1)], ALU.subtract, ALU.mult))
            c.leave(32)
            vec.drain().then_inc(s.ready, 1)
            with vec.Fori(0, 32) as g:
                c.enter(g, 1)
                c.step(vec.bn_stats(gs[:, g, :], m.a[:, bass.ds(g * 4, 4), :].rearrange("p a b -> p (a b)")))
            c.leave(32)
            c.step(vec.bn_aggr(m.col[:, 2:4], m.spare[:, 0:192]))
            vec.tensor_scalar(m.col[:, 3:4], m.col[:, 3:4], EPS, None, ALU.add).then_inc(s.added, 1)
            vec.wait_ge(s.rooted, 2)
            vec.wait_ge(s.scalars, 16 * (len(SCALARS) + 7))
            c.step(vec.reciprocal(m.col[:, 4:5], m.col[:, 4:5]))
            c.step(vec.tensor_tensor(m.col[:, 0:1], m.col[:, 4:5], m.sc[:, 0:1], ALU.mult))
            c.step(vec.tensor_tensor(m.col[:, 5:6], m.col[:, 0:1], m.col[:, 2:3], ALU.mult))
            c.step(vec.tensor_tensor(m.col[:, 1:2], m.sc[:, 1:2], m.col[:, 5:6], ALU.subtract))


def load_mixer(eng, m, ins, i, sem):
    w = ins[f'L0_conv_mixer_w{i}'][0, 0]
    eng.dma_start(m.mixw[:, 0:16], w[0:16].partition_broadcast(P)).then_inc(sem, 16)
    eng.dma_start(m.mixw[:, K17 + 1:ROWS], w[31:15:-1].partition_broadcast(P)).then_inc(sem, 16)


def stage_forward(nc, held, m, tok):
    s = semaphores(nc, held, "forward", "in0 in1 in2 in3 first copied second scaled v")
    arrived = [s.in0, s.in1, s.in2, s.in3]
    tok_img = tok.rearrange("t h w -> h t w")
    per = 6
    rounds = FQ // per

    with nc.Block() as block:
        @block.sync
        def _(sp):
            def body(it):
                for u in range(UN):
                    g = it * UN + u
                    reached(sp, s.first, g - UN + 1)
                    sp.dma_start(m.load[:, u], tok_img[:, bass.ds(g * GRP, GRP), :]).then_inc(arrived[u], 16)
            body(0)
            with sp.Fori(1, NG // UN) as it:
                body(it)

        @block.tensor
        def _(pe):
            def body(it):
                for u in range(UN):
                    g = it * UN + u
                    pe.wait_ge(arrived[u], (it + 1) * 16)
                    reached(pe, s.copied, g - 1)
                    for j in range(GRP):
                        mm = pe.matmul(m.ps[u % 2][:, j * FQ:j * FQ + FQ], m.load[:, u, j, :], m.dft,
                                       start=True, stop=True)
                    mm.then_inc(s.first, 1)
            body(0)
            with pe.Fori(1, NG // UN) as it:
                body(it)
            pe.wait_ge(s.copied, NG)
            for r in range(rounds):
                reached(pe, s.scaled, r - 3)
                for j in range(per):
                    mm = pe.matmul(m.ps[4 + r % 4][:, j * FQ:j * FQ + FQ], m.half33[:, :, r * per + j], m.dft,
                                   start=True, stop=True)
                mm.then_inc(s.second, 1)

        @block.scalar
        def _(act):
            with act.Fori(0, NG // UN) as it:
                for u in range(UN):
                    g = it * UN + u
                    act.wait_ge(s.first, g + 1)
                    act.copy(m.half33[:, bass.ds(g * GRP, GRP), :],
                             m.ps[u % 2][:, 0:GRP * FQ].rearrange("p (t x) -> p t x", t=GRP)).then_inc(s.copied, 1)

        @block.vector
        def _(vec):
            c = Chain(vec, s.v)
            for r in range(rounds):
                vec.wait_ge(s.second, r + 1)
                vec.tensor_scalar(m.ft[:, r * per:r * per + per, :].rearrange("p x y -> p (x y)"),
                                  m.ps[4 + r % 4][:, 0:per * FQ], m.col[:, 0:1], None, ALU.mult)\
                    .then_inc(s.scaled, 1)
            vec.wait_ge(s.scaled, rounds)
            c.step(vec.tensor_scalar(m.ft[:, 0, 0:1], m.ft[:, 0, 0:1], m.col[:, 1:2], None, ALU.add))


def form_modes(vec, c, feat, modes, k):
    f = feat.rearrange("p (a x) (b y) -> p a x b y", a=2, b=2)
    cc, cs, sc, ss = (f[:, a, 0:K17, b, 0:K17] for a in (0, 1) for b in (0, 1))
    re, im = (modes[:, i].rearrange("p (r k) -> p r k", r=ROWS) for i in (0, 1))
    vec.tensor_tensor(re[:, 0:K17], cc, ss, ALU.subtract)
    vec.tensor_tensor(re[:, K17:ROWS], cc, ss, ALU.add)
    vec.tensor_tensor(im[:, K17:ROWS], sc, cs, ALU.subtract)
    c.step(vec.scalar_tensor_tensor(out=im[:, 0:K17], in0=sc, scalar=-1.0, in1=cs, op0=ALU.mult, op1=ALU.subtract))


def stage_modes(nc, held, m):
    s = semaphores(nc, held, "modes", "v modes weights high turned copied gram")
    R2 = 2.0 ** 0.5
    wt = m.weff.rearrange("p c (r k) -> p c r k", r=ROWS)
    jobs = []
    for k, (m0, n) in enumerate(MT):
        jobs += [(m.weff[:, cpt, m0:m0 + n], n, m.wT[0:n, k, cpt, :], 64, 'weights') for cpt in (0, 1)]
    for k, (m0, n) in enumerate(MT):
        jobs += [(m.modes[:, cpt, m0:m0 + n], n, m.modesT[0:n, k, cpt, :], P, 'modes') for cpt in (0, 1)]
    banks = [jobs[i:i + 2] for i in range(0, len(jobs), 2)]
    hbanks = [list(range(i, min(HC, i + 4))) for i in range(0, HC, 4)]
    NBK = 6

    with nc.Block() as block:
        @block.vector
        def _(vec):
            c = Chain(vec, s.v)
            wre, wim = wt[:, 0], wt[:, 1]
            vec.tensor_copy(wre, m.wraw[:, :, :, 0])
            c.step(vec.tensor_copy(wim, m.wraw[:, :, :, 1]))
            pr, nr = wre[0:48, 1:9, 0], wre[0:48, K17 + 1:K17 + 9, 0]
            pi, ni = wim[0:48, 1:9, 0], wim[0:48, K17 + 1:K17 + 9, 0]
            even, odd = m.spare[0:48, 0:8], m.spare[0:48, 8:16]
            vec.tensor_tensor(even, pr, nr, ALU.add)
            c.step(vec.tensor_tensor(odd, pi, ni, ALU.subtract))
            vec.tensor_scalar(pr, even, 0.5, None, ALU.mult)
            vec.tensor_scalar(nr, even, 0.5, None, ALU.mult)
            vec.tensor_scalar(pi, odd, 0.5, None, ALU.mult)
            vec.tensor_scalar(ni, odd, -0.5, None, ALU.mult)
            c.step(vec.memset(wim[0:48, 0:1, 0], 0.0))
            vec.drain().then_inc(s.weights, 1)
            form_modes(vec, c, m.ft, m.modes, K33)
            vec.drain().then_inc(s.modes, 1)
            h, f = m.hg.rearrange("p (x y) -> p x y", x=FQ), m.ft
            c.step(vec.tensor_scalar(m.hg, m.ft.rearrange("p x y -> p (x y)"), 2.0, None, ALU.mult))
            c.step(vec.tensor_scalar(h[:, :, 0:K33:32], f[:, :, 0:K33:32], R2, None, ALU.mult))
            c.step(vec.tensor_scalar(h[:, 0, :], f[:, 0, :], R2, None, ALU.mult))
            c.step(vec.tensor_copy(h[:, 0, 0:K33:32], f[:, 0, 0:K33:32]))
            c.step(vec.memset(h[:, 32:66:33, :], 0.0))
            a1, a2, a3, a4 = (m.spare[:, 16 + 32 * i:48 + 32 * i] for i in range(4))
            vec.tensor_tensor(a1, f[:, 32, 1:33], f[:, 65, 34:66], ALU.add)
            c.step(vec.tensor_tensor(a2, f[:, 65, 1:33], f[:, 32, 34:66], ALU.subtract))
            vec.tensor_scalar(h[:, 32, 1:32], a1[:, 0:31], R2, None, ALU.mult)
            vec.tensor_scalar(h[:, 65, 1:32], a2[:, 0:31], R2, None, ALU.mult)
            vec.tensor_copy(h[:, 32, 0:1], f[:, 32, 0:1])
            vec.tensor_copy(h[:, 32, 32:33], a1[:, 31:32])
            hv = m.hg.rearrange("p (x b y) -> p x b y", x=FQ, b=2)
            vec.memset(hv[:, 0:9, :, 0:9], 0.0)
            vec.memset(hv[:, K33:K33 + 9, :, 0:9], 0.0)
            vec.tensor_tensor(a3[:, 0:8], f[:, 8, 1:9], f[:, 41, 34:42], ALU.subtract)
            c.step(vec.tensor_tensor(a4[:, 0:8], f[:, 41, 1:9], f[:, 8, 34:42], ALU.add))
            vec.tensor_scalar(h[:, 8, 1:9], a3[:, 0:8], R2, None, ALU.mult)
            vec.tensor_scalar(h[:, 41, 1:9], a4[:, 0:8], R2, None, ALU.mult)
            c.step(vec.memset(h[:, :, 65:66], 0.0))
            vec.drain().then_inc(s.high, 1)
            vec.wait_ge(s.gram, 1)
            for b in range(NB):
                q = slice(NT * b, NT * b + NT)
                vec.tensor_copy(m.gram[q, :], m.ps[7][q, NT * b:NT * b + NT])

        @block.tensor
        def _(pe):
            for i, bank in enumerate(banks):
                if i == 0:
                    pe.wait_ge(s.weights, 1)
                if bank[0][4] == 'modes':
                    pe.wait_ge(s.modes, 1)
                reached(pe, s.copied, i - NBK + 1)
                for j, (src, n, _, wide, _) in enumerate(bank):
                    mm = pe.transpose(m.ps[i % NBK][0:n, j * P:j * P + wide], src, m.ident[0:wide, 0:wide])
                mm.then_inc(s.turned, 1)
            pe.wait_ge(s.high, 1)
            for r, cs in enumerate(hbanks):
                i = len(banks) + r
                reached(pe, s.copied, i - NBK + 1)
                for j, k in enumerate(cs):
                    mm = pe.transpose(m.ps[i % NBK][:, j * P:j * P + P], m.hg[:, k * P:k * P + P], m.ident)
                mm.then_inc(s.turned, 1)
            for k in range(HC):
                pe.wait_ge(s.copied, len(banks) + k // 4 + 1)
                mm = pe.matmul(m.ps[7][:, 0:P], m.gramT[:, k, :], m.gramT[:, k, :], start=(k == 0), stop=(k == HC - 1))
            mm.then_inc(s.gram, 1)

        @block.scalar
        def _(act):
            for i, bank in enumerate(banks):
                act.wait_ge(s.turned, i + 1)
                for j, (_, n, dst, wide, _) in enumerate(bank):
                    ins = act.copy(dst, m.ps[i % NBK][0:n, j * P:j * P + wide])
                ins.then_inc(s.copied, 1)
            for r, cs in enumerate(hbanks):
                i = len(banks) + r
                act.wait_ge(s.turned, i + 1)
                act.copy(m.gramT[:, cs[0]:cs[-1] + 1, :].rearrange("p c t -> p (c t)"),
                         m.ps[i % NBK][:, 0:P * len(cs)]).then_inc(s.copied, 1)


def stage_weights(nc, held, m):
    s = semaphores(nc, held, "weights", "v")
    w = weight_views(m)

    with nc.Block() as block:
        @block.vector
        def _(vec):
            c = Chain(vec, s.v)
            sk = m.skips
            n5 = len(MT)
            c.step(vec.tensor_tensor(w.sum, m.wT[:, :, 0, 0:48], over(sk[:, 0:48], 1, n5), ALU.add))
            qr, kr, vr = w.sum[:, :, 0:16], w.sum[:, :, 16:32], w.sum[:, :, 32:48]
            qi, ki, vi, pi = (m.wT[:, :, 1, 16 * i:16 * i + 16] for i in range(4))
            v0, pr = m.wT[:, :, 0, 32:48], m.wT[:, :, 0, 48:64]
            low = over(m.low, 2, HEADS)
            vec.tensor_tensor(w.t1, qr, kr, ALU.mult)
            vec.tensor_tensor(w.t2, qi, ki, ALU.mult)
            vec.tensor_tensor(w.t3, qi, kr, ALU.mult)
            c.step(vec.tensor_tensor(w.t4, qr, ki, ALU.mult))
            vec.tensor_tensor(w.t1, w.t1, w.t2, ALU.add)
            c.step(vec.tensor_tensor(w.t3, w.t3, w.t4, ALU.subtract))
            vec.tensor_tensor(w.ar, w.t1, low, ALU.mult)
            c.step(vec.tensor_tensor(w.ai, w.t3, low, ALU.mult))
            c.step(vec.tensor_scalar(w.an, w.ai, -1.0, None, ALU.mult))
            pw = over(sk[:, 48:64], 1, n5)
            vec.tensor_tensor(w.t1, v0, pw, ALU.mult)
            vec.tensor_tensor(w.t2, pr, vr, ALU.mult)
            vec.tensor_tensor(w.t3, pi, vi, ALU.mult)
            c.step(vec.tensor_tensor(w.t4, pr, pw, ALU.add))
            vec.tensor_tensor(w.t1, w.t1, w.t2, ALU.add)
            c.step(vec.tensor_tensor(w.t4, w.t4, vi, ALU.mult))
            vec.tensor_tensor(w.ur, w.t1, w.t3, ALU.subtract)
            c.step(vec.tensor_tensor(w.t2, pi, vr, ALU.mult))
            c.step(vec.tensor_tensor(w.ui, w.t4, w.t2, ALU.add))
            c.step(vec.tensor_tensor(w.t1[:, 0, :], pr[:, 0, :], sk[:, 48:64], ALU.add))
            c.step(vec.tensor_tensor(w.t1[:, 0, :], w.t1[:, 0, :], m.biases[:, 32:48], ALU.mult))
            c.step(vec.tensor_reduce(m.col[:, 8:9], w.t1[:, 0, :], AX.X, ALU.add))
            c.step(vec.tensor_tensor(m.col[:, 8:9], m.col[:, 8:9], m.sc[:, 16:17], ALU.add))
            c.step(vec.tensor_tensor(w.cg, sk[:, 0:16], sk[:, 16:32], ALU.mult))
            vec.tensor_scalar(w.cg, w.cg, 64.0, None, ALU.mult)
            c.step(vec.tensor_tensor(w.cm, sk[:, 32:48], sk[:, 48:64], ALU.mult))
            aq, ak = w.sum[0:1, 0, 0:16], w.sum[0:1, 0, 16:32]
            bq, bk = m.biases[0:1, 0:16], m.biases[0:1, 16:32]
            c.step(vec.scalar_tensor_tensor(out=w.r1[0:1], in0=aq, scalar=64.0, in1=bk, op0=ALU.mult, op1=ALU.mult))
            c.step(vec.scalar_tensor_tensor(out=w.r2[0:1], in0=ak, scalar=64.0, in1=bq, op0=ALU.mult, op1=ALU.mult))
            c.step(vec.scalar_tensor_tensor(out=w.r3[0:1], in0=bq, scalar=64.0, in1=bk, op0=ALU.mult, op1=ALU.mult))
            vec.tensor_copy(m.dcq, over(w.r1[0:1], 2, NT))
            c.step(vec.tensor_tensor(m.dck, over(m.modesT[0:1, 0, 0, :], 1, HEADS), over(w.r2[0:1], 2, P), ALU.mult))
            c.step(vec.tensor_tensor(m.dck, m.dck, over(w.r3[0:1], 2, P), ALU.add))
            c.step(vec.memset(w.one[0:1], 1.0))


def weight_views(m):
    w = Views()
    w.sum = m.wk[:, 0:240].rearrange("p (k h) -> p k h", k=5)
    big = [m.wk[:, 240 + 80 * i:320 + 80 * i].rearrange("p (k h) -> p k h", k=5) for i in range(9)]
    w.ar, w.ai, w.an, w.ur, w.ui, w.t1, w.t2, w.t3, w.t4 = big
    w.cg, w.cm = m.wk[:, 960:976], m.wk[:, 976:992]
    w.r1, w.mix = m.wk[:, 640:656], m.wk[:, 656:688]
    w.r2, w.r3, w.one = m.wk[:, 720:736], m.wk[:, 800:816], m.wk[:, 880:912]
    return w


def stage_scores(nc, held, m):
    s = semaphores(nc, held, "scores", "v a p0 p1 p2 p3 used done sub exp cleared probs turned copied mixed mixc")
    w = weight_views(m)
    ready = [s.p0, s.p1, s.p2, s.p3]
    left = [(w.ar, 0), (w.ai, 1), (w.ar, 1), (w.an, 0)]

    with nc.Block() as block:
        def operands(k, j):
            a, part = left[j]
            return over(m.modesT[:, k, part, :], 1, HEADS), over(a[:, k, :], 2, P)

        @block.vector
        def _(vec):
            c = Chain(vec, s.v)
            for k in range(LOWT):
                for j in (0, 1):
                    if k:
                        vec.wait_ge(s.used, 4 * (k - 1) + j + 1)
                    x, a = operands(k, j)
                    vec.tensor_tensor(m.prod[:, j], x, a, ALU.mult).then_inc(ready[j], 1)
            sh = [HEADS, NT]
            gram = over(m.gram, 1, HEADS)
            c.step(vec.tensor_tensor(m.score, gram, over(w.cg, 2, NT), ALU.mult))
            vec.wait_ge(s.done, 1)
            c.step(vec.tensor_tensor(m.score, m.ps[0][:, :].rearrange("p (h s) -> p h s", h=HEADS), m.score, ALU.add))
            c.step(vec.tensor_reduce(w.r1, m.score, AX.X, ALU.max))
            vec.tensor_tensor(m.score, m.score, over(w.r1, 2, NT), ALU.subtract).then_inc(s.sub, 1)
            vec.wait_ge(s.exp, 1)
            c.step(vec.tensor_reduce(w.r1, m.expo, AX.X, ALU.add))
            c.step(vec.reciprocal(w.r1, w.r1))
            c.step(vec.tensor_tensor(m.prob, m.expo, over(w.r1, 2, NT), ALU.mult))
            vec.wait_ge(s.cleared, 2)
            for b in range(NB):
                q = slice(NT * b, NT * b + NT)
                ins = vec.tensor_copy(m.probD[q, :, NT * b:NT * b + NT], m.prob[q])
            ins.then_inc(s.probs, 1)
            c.step(vec.tensor_tensor(m.score, m.prob, over(w.cm, 2, NT), ALU.mult))
            c.step(vec.tensor_reduce(w.mix, m.score.rearrange("p h s -> p s h"), AX.X, ALU.add))
            for b in range(NB):
                q = slice(NT * b, NT * b + NT)
                ins = vec.tensor_copy(m.mixD[q, NT * b:NT * b + NT], w.mix[q])
            ins.then_inc(s.probs, 1)
            vec.wait_ge(s.mixed, 1)
            c.step(vec.tensor_copy(m.mixT, m.ps[5][:, 0:P]))
            vec.scalar_tensor_tensor(out=m.mixA, in0=m.ps[5][:, 0:P], scalar=m.col[:, 0:1], in1=m.ident,
                                     op0=ALU.mult, op1=ALU.add).then_inc(s.mixc, 1)
            vec.wait_ge(s.mixed, 2)
            c.step(vec.tensor_copy(m.col[:, 9:10], m.ps[6][:, 0:1]))

        @block.gpsimd
        def _(pool):
            for k in range(LOWT):
                if k:
                    pool.wait_ge(s.used, 4 * (k - 1) + 3)
                x, a = operands(k, 2)
                pool.tensor_tensor(m.prod[:, 2], x, a, ALU.mult).then_inc(ready[2], 1)
            pool.wait_ge(s.done, 1)
            pool.memset(m.probD, 0.0).then_inc(s.cleared, 1)
            pool.memset(m.mixD, 0.0).then_inc(s.cleared, 1)

        @block.scalar
        def _(act):
            for k in range(LOWT):
                if k:
                    act.wait_ge(s.used, 4 * (k - 1) + 4)
                a, part = left[3]
                for h in range(HEADS):
                    ins = act.activation(m.prod[:, 3, h, :], m.modesT[:, k, part, :], ACT.Copy, scale=a[:, k, h:h + 1])
                ins.then_inc(ready[3], 1)
            act.wait_ge(s.sub, 1)
            act.activation(m.expo, m.score, ACT.Exp).then_inc(s.exp, 1)
            for i in range(4):
                act.wait_ge(s.turned, i + 1)
                act.copy(m.probT[:, 4 * i:4 * i + 4, :].rearrange("p h t -> p (h t)"), m.ps[1 + i][:, :])\
                    .then_inc(s.copied, 1)

        @block.tensor
        def _(pe):
            for k in range(LOWT):
                for j in range(4):
                    pe.wait_ge(ready[j], k + 1)
                    for b in range(NB):
                        q = slice(NT * b, NT * b + NT)
                        mm = pe.matmul(m.ps[0][q, :], m.modesT[:, k, j // 2, q], m.prod[:, j, :, q],
                                       start=(k == 0 and j == 0), stop=False)
                    mm.then_inc(s.used, 1)
            for b in range(NB):
                q = slice(NT * b, NT * b + NT)
                pe.matmul(m.ps[0][q, :], m.modesT[0:1, 0, 0, q], m.dcq, start=False, stop=False)
                mm = pe.matmul(m.ps[0][q, :], w.one[0:1], m.dck[:, :, q], start=False, stop=True)
            mm.then_inc(s.done, 1)
            pe.wait_ge(s.probs, 1)
            for h in range(HEADS):
                mm = pe.transpose(m.ps[1 + h // 4][:, (h % 4) * P:(h % 4) * P + P], m.probD[:, h, :], m.ident)
                if h % 4 == 3:
                    mm.then_inc(s.turned, 1)
            pe.wait_ge(s.probs, 2)
            pe.transpose(m.ps[5][:, 0:P], m.mixD, m.ident).then_inc(s.mixed, 1)
            pe.wait_ge(s.mixc, 1)
            pe.matmul(m.ps[6][:, 0:1], m.mixT, m.col[:, 1:2], start=True, stop=True).then_inc(s.mixed, 1)


def stage_mix(nc, held, m, mix):
    s = semaphores(nc, held, "mix", "v mixed added stored xm used summed free reduced dc turned copied coef")
    w = weight_views(m)
    NCH = PIX // 512
    steps = [(k, q) for k in range(len(MT)) for q in range(4)]
    a = m.a[:, :, :].rearrange("p a b -> p (a b)")

    with nc.Block() as block:
        @block.tensor
        def _(pe):
            def body(it):
                for u in range(4):
                    i = it * 4 + u
                    reached(pe, s.added, i - 3)
                    pe.matmul(m.ps[u][:, :], m.mixA, a[:, bass.ds(i * 512, 512)], start=True, stop=True)\
                        .then_inc(s.mixed, 1)
            body(0)
            with pe.Fori(1, NCH // 4) as it:
                body(it)
            for i, (k, q) in enumerate(steps):
                m0, n = MT[k]
                if i < 2:
                    pe.wait_ge(s.added, NCH)
                reached(pe, s.used, i - 2)
                for part in (0, 1):
                    mm = pe.matmul(m.ps[2 * (i % 3) + part][0:n, :], m.modes[:, part, m0:m0 + n],
                                   m.probT[:, 4 * q:4 * q + 4, :], start=True, stop=True)
                mm.then_inc(s.xm, 1)
            for k, (m0, n) in enumerate(MT):
                pe.wait_ge(s.reduced, k + 1)
                if k == 0:
                    pe.wait_ge(s.dc, 1)
                    pe.wait_ge(s.used, len(steps))
                reached(pe, s.copied, k - 2)
                for part in (0, 1):
                    mm = pe.transpose(m.ps[k % 3][:, part * P:part * P + n], m.modesT[0:n, k, part, :], m.ident[0:n, 0:n])
                mm.then_inc(s.turned, 1)
            turn_coefficients(pe, m, s, len(MT))

        @block.scalar
        def _(act):
            for k, (m0, n) in enumerate(MT):
                act.wait_ge(s.turned, k + 1)
                src = m.ps[k % 3][:, 0:2 * P].rearrange("p (c n) -> p c n", c=2)[:, :, 0:n]
                act.copy(m.modes[:, :, m0:m0 + n], src).then_inc(s.copied, 1)
            copy_coefficients(act, m, s, len(MT))

        @block.sync
        def _(sp):
            sp.wait_ge(s.added, NCH)
            for q in range(4):
                sp.dma_start(mix[:, 32 * q:32 * q + 32, :], m.a[:, 32 * q:32 * q + 32, :]).then_inc(s.stored, 16)
            sp.wait_ge(s.stored, 64)

        @block.vector
        def _(vec):
            c = Chain(vec, s.v)
            with vec.Fori(0, NCH // 4) as it:
                for u in range(4):
                    i = it * 4 + u
                    vec.wait_ge(s.mixed, i + 1)
                    vec.tensor_scalar(a[:, bass.ds(i * 512, 512)], m.ps[u][:, :], m.col[:, 9:10], None, ALU.add)\
                        .then_inc(s.added, 1)
            for i, (k, q) in enumerate(steps):
                n = MT[k][1]
                vec.wait_ge(s.xm, i + 1)
                reached(vec, s.summed, i - 1)
                for j, (part, u) in enumerate([(0, w.ur), (1, w.ui), (0, w.ui), (1, w.ur)]):
                    src = m.ps[2 * (i % 3) + part][0:n, :].rearrange("p (h t) -> p h t", h=4)
                    ins = vec.tensor_tensor(m.zprod[0:n, i % 2, j], src, over(u[0:n, k, 4 * q:4 * q + 4], 2, P), ALU.mult)
                ins.then_inc(s.used, 1)
                if q == 3:
                    vec.wait_ge(s.summed, i + 1)
                    for part in (0, 1):
                        ins = vec.tensor_reduce(m.modesT[0:n, k, part, :], m.zsum[0:n, part].rearrange("p h t -> p t h"),
                                                AX.X, ALU.add)
                    ins.then_inc(s.reduced, 1)
            vec.wait_ge(s.reduced, len(MT))
            vec.tensor_scalar(m.modesT[0:1, 0, 0, :], m.modesT[0:1, 0, 0, :], m.col[0:1, 8:9], None, ALU.add)\
                .then_inc(s.dc, 1)
            vec.wait_ge(s.copied, len(MT))
            form_coefficients(vec, m, m.modes[:, 0], m.modes[:, 1])
            vec.drain().then_inc(s.coef, 1)

        @block.gpsimd
        def _(pool):
            for i, (k, q) in enumerate(steps):
                n = MT[k][1]
                pool.wait_ge(s.used, i + 1)
                if q == 0:
                    reached(pool, s.reduced, k)
                pool.tensor_tensor(m.zsum[0:n, 0, 4 * q:4 * q + 4], m.zprod[0:n, i % 2, 0], m.zprod[0:n, i % 2, 1], ALU.subtract)
                pool.tensor_tensor(m.zsum[0:n, 1, 4 * q:4 * q + 4], m.zprod[0:n, i % 2, 2], m.zprod[0:n, i % 2, 3], ALU.add)\
                    .then_inc(s.summed, 1)


def form_coefficients(vec, m, re, im):
    g = m.coef.rearrange("p (a x) (b y) -> p a x b y", a=2, b=2)
    re, im = (v.rearrange("p (r k) -> p r k", r=ROWS) for v in (re, im))
    rp, rn, ip, im_ = re[:, 0:K17], re[:, K17:ROWS], im[:, 0:K17], im[:, K17:ROWS]
    vec.tensor_tensor(g[:, 0, :, 0], rp, rn, ALU.add)
    vec.tensor_tensor(g[:, 1, :, 1], rn, rp, ALU.subtract)
    vec.tensor_tensor(g[:, 1, :, 0], im_, ip, ALU.subtract)
    return vec.scalar_tensor_tensor(out=g[:, 0, :, 1], in0=ip, scalar=-1.0, in1=im_, op0=ALU.mult, op1=ALU.subtract)


COEF_BANKS = [list(range(i, min(FM, i + 4))) for i in range(0, FM, 4)]


def turn_coefficients(pe, m, s, base):
    pe.wait_ge(s.coef, 1)
    for r, xs in enumerate(COEF_BANKS):
        if r > 2:
            pe.wait_ge(s.copied, base + r - 2)
        for j, xf in enumerate(xs):
            mm = pe.transpose(m.ps[3 + r % 3][0:FM, j * P:j * P + P], m.coef[:, xf, :], m.ident)
        mm.then_inc(s.turned, 1)


def copy_coefficients(act, m, s, base):
    for r, xs in enumerate(COEF_BANKS):
        act.wait_ge(s.turned, base + r + 1)
        act.copy(m.coefT[:, xs[0]:xs[-1] + 1, :].rearrange("p x t -> p (x t)"),
                 m.ps[3 + r % 3][0:FM, 0:P * len(xs)]).then_inc(s.copied, 1)


def sweep(eng, step, lag):
    for u in range(UN):
        step(u, u)
    with eng.Fori(1, NG // UN) as it:
        for u in range(UN):
            step(it * UN + u, u)
    for u in range(lag):
        step(NG + u, u)


def live(g):
    return not isinstance(g, int) or 0 <= g < NG


def group(images, g):
    return images[:, bass.ds(g * GRP, GRP), :]


def banked(m, bank):
    return m.ps[bank][:, :].rearrange("p (t w) -> p t w", t=GRP)


def stage_inverse(nc, held, m, kind, mix=None, ins=None):
    s = semaphores(nc, held, "inverse_" + kind, "in0 in1 in2 in3 staged cols colsc rows used stats "
                   "lin pre ready saved first copied weights")
    arrived = [s.in0, s.in1, s.in2, s.in3]
    dest = m.a if kind == 'mix2' else m.b

    with nc.Block() as block:
        @block.sync
        def _(sp):
            if kind == 'proj':
                mix_img = mix.rearrange("t h w -> h t w")

                def load(t, u):
                    reached(sp, s.used, t - UN + 1)
                    sp.dma_start(group(m.b, t), mix_img[:, bass.ds(t * GRP, GRP), :]).then_inc(arrived[u], 16)
                sweep(sp, load, 0)
            if kind == 'mix1':
                load_mixer(sp, m, ins, 2, s.weights)
                sp.wait_ge(s.weights, 32)

        @block.gpsimd
        def _(pool):
            pool.memset(m.stage[:, :, GRP * FM:], 0.0)

            def step(t, u):
                if live(t):
                    reached(pool, s.cols, t - 1)
                    pool.tensor_copy(m.stage[0:FM, u % 2, 0:GRP * FM].rearrange("p (t x) -> p t x", t=GRP),
                                     m.coefT[:, :, bass.ds(t * GRP, GRP)].rearrange("p x t -> p t x"))\
                        .then_inc(s.staged, 1)
                g = t - 2
                if kind == 'mix1' and live(g):
                    pool.wait_ge(s.ready, g + 1)
                    pool.tensor_copy(group(m.a, g), m.ust[:, u % 2]).then_inc(s.saved, 1)
            sweep(pool, step, 2 if kind == 'mix1' else 0)

        @block.tensor
        def _(pe):
            def step(t, u):
                if live(t):
                    pe.wait_ge(s.staged, t + 1)
                    reached(pe, s.colsc, t - 1)
                    for j in range(GRP):
                        mm = pe.matmul(m.ps[u % 2][:, j * NW:j * NW + NW],
                                       m.stage[0:FM, u % 2, j * FM:j * FM + P], m.cols, start=True, stop=True)
                    mm.then_inc(s.cols, 1)
                g = t - 1
                if live(g):
                    pe.wait_ge(s.colsc, g + 1)
                    reached(pe, s.pre if kind == 'mix1' else s.used, g - 1)
                    pe.matmul(m.ps[2 + (u - 1) % 2][:, :], m.rows, m.half[0:FM, (u - 1) % 2, :], start=True, stop=True)\
                        .then_inc(s.rows, 1)
                g = t - 3
                if kind == 'mix1' and live(g):
                    pe.wait_ge(s.ready, g + 1)
                    reached(pe, s.copied, g - 1)
                    for j in range(GRP):
                        mm = pe.matmul(m.ps[4 + (u - 3) % 2][:, j * FM:j * FM + FM], m.ust[:, (u - 3) % 2, j, :],
                                       m.dft17, start=True, stop=True)
                    mm.then_inc(s.first, 1)
            sweep(pe, step, 3 if kind == 'mix1' else 1)

        @block.scalar
        def _(act):
            def step(t, u):
                if live(t):
                    act.wait_ge(s.cols, t + 1)
                    reached(act, s.rows, t - 1)
                    act.copy(m.half[0:FM, u % 2, :], m.ps[u % 2][0:FM, :]).then_inc(s.colsc, 1)
                g = t - 2
                if kind == 'mix1' and live(g):
                    act.wait_ge(s.pre, g + 1)
                    reached(act, s.first, g - 1)
                    reached(act, s.saved, g - 1)
                    act.activation(m.ust[:, u % 2], m.tmp[:, u % 2], ACT.Gelu).then_inc(s.ready, 1)
                g = t - 3
                if kind == 'mix1' and live(g):
                    act.wait_ge(s.first, g + 1)
                    act.copy(m.half17[:, bass.ds(g * GRP, GRP), :],
                             m.ps[4 + (u - 3) % 2][:, 0:GRP * FM].rearrange("p (t x) -> p t x", t=GRP))\
                        .then_inc(s.copied, 1)
            sweep(act, step, 3 if kind == 'mix1' else 0)

        @block.vector
        def _(vec):
            def step(t, u, it):
                if kind == 'mix1' and live(t):
                    reached(vec, s.ready, t - 1)
                    for j in range(GRP):
                        img = t * GRP + j
                        e = vec.tensor_scalar(m.tmp[:, u % 2, j, :], m.b[:, bass.ds(img, 1), :],
                                              m.aff[:, 4, bass.ds(img, 1)], m.aff[:, 5, bass.ds(img, 1)],
                                              ALU.mult, ALU.add)
                    e.then_inc(s.lin, 1)
                g = t - 1
                if live(g):
                    if kind != 'mix1':
                        reached(vec, s.used, g)
                    vec.wait_ge(s.rows, g + 1)
                    y = banked(m, 2 + (u - 1) % 2)
                    if kind == 'proj':
                        vec.wait_ge(arrived[(u - 1) % UN], (it + (1 if u else 0)) * 16)
                        vec.tensor_tensor(group(m.b, g), group(m.b, g), y, ALU.add).then_inc(s.used, 1)
                    elif kind == 'mix1':
                        vec.wait_ge(s.lin, g + 1)
                        vec.tensor_tensor(m.tmp[:, (u - 1) % 2], m.tmp[:, (u - 1) % 2], y, ALU.add).then_inc(s.pre, 1)
                    else:
                        vec.scalar_tensor_tensor(out=group(m.a, g), in0=group(m.a, g), scalar=m.sc[:, 10:11], in1=y,
                                                 op0=ALU.mult, op1=ALU.add).then_inc(s.used, 1)
                g = t - 2
                if kind != 'mix1' and live(g):
                    if isinstance(g, int) and g == NG - 1:
                        vec.wait_ge(s.used, NG)
                    for j in range(GRP):
                        img = g * GRP + j
                        vec.bn_stats(m.stat[:, bass.ds(img, 1), :], dest[:, bass.ds(img, 1), :])

            for u in range(UN):
                step(u, u, 0)
            with vec.Fori(1, NG // UN) as it:
                for u in range(UN):
                    step(it * UN + u, u, it)
            for u in range(2):
                step(NG + u, u, NG // UN)


def stage_factors(nc, held, m, kind):
    s = semaphores(nc, held, "factors_" + kind, "v ones sums summed added rooted")
    half = m.spare[:, 128:2176]
    ones, total, mean, var = m.spare[:, 0:P], half[:, 0:128], half[:, 128:256], half[:, 256:384]
    root, root2, t = half[:, 384:512], half[:, 512:640], half[:, 640:768]
    dev = half[:, 768:1024].rearrange("p (t k) -> p t k", k=2)
    sc1, bi1, sc2, bi2, sa, sb = (m.aff[:, i, :] for i in range(6))

    def scalar(i):
        return m.sc[:, i:i + 1]

    with nc.Block() as block:
        @block.tensor
        def _(pe):
            pe.wait_ge(s.ones, 1)
            for i, src in enumerate([total, t]):
                pe.wait_ge(s.sums, i + 1)
                pe.matmul(m.ps[i][:, 0:P], ones, src, start=True, stop=True).then_inc(s.summed, 1)

        @block.scalar
        def _(act):
            for i, (dst, src) in enumerate([(root, var), (root2, t)][:2 if kind == 'proj' else 1]):
                act.wait_ge(s.added, i + 1)
                act.activation(dst, src if i else root, ACT.Sqrt).then_inc(s.rooted, 1)

        @block.vector
        def _(vec):
            c = Chain(vec, s.v)
            vec.memset(ones, 1.0).then_inc(s.ones, 1)
            vec.tensor_tensor(total, m.stat[:, :, 1], m.stat[:, :, 4], ALU.add).then_inc(s.sums, 1)
            vec.wait_ge(s.summed, 1)
            c.step(vec.tensor_scalar(mean, m.ps[0][:, 0:P], 1.0 / (2 * P), None, ALU.mult))
            c.step(vec.tensor_tensor(dev, m.stat[:, :, 1::3], over(mean, 2, 2), ALU.subtract))
            c.step(vec.tensor_tensor(dev, dev, dev, ALU.mult))
            c.step(vec.tensor_tensor(t, dev[:, :, 0], dev[:, :, 1], ALU.add))
            c.step(vec.tensor_tensor(var, m.stat[:, :, 2], m.stat[:, :, 5], ALU.add))
            vec.scalar_tensor_tensor(out=t, in0=t, scalar=float(NW // 2), in1=var, op0=ALU.mult, op1=ALU.add)\
                .then_inc(s.sums, 1)
            vec.wait_ge(s.summed, 2)
            c.step(vec.tensor_scalar(var, m.ps[1][:, 0:P], 1.0 / PIX, None, ALU.mult))
            vec.tensor_scalar(root, var, EPS, None, ALU.add).then_inc(s.added, 1)
            vec.wait_ge(s.rooted, 1)
            g, b = (2, 3) if kind == 'proj' else (14, 15)
            c.step(vec.reciprocal(root, root))
            c.step(vec.tensor_scalar(sc1, root, scalar(g), None, ALU.mult))
            c.step(vec.tensor_tensor(t, mean, sc1, ALU.mult))
            c.step(vec.tensor_scalar(bi1, t, -1.0, scalar(b), ALU.mult, ALU.add))
            if kind == 'proj':
                c.step(vec.tensor_tensor(t, sc1, sc1, ALU.mult))
                c.step(vec.tensor_tensor(t, t, var, ALU.mult))
                vec.tensor_scalar(t, t, EPS, None, ALU.add).then_inc(s.added, 1)
                vec.wait_ge(s.rooted, 2)
                c.step(vec.reciprocal(root2, root2))
                c.step(vec.tensor_scalar(sc2, root2, scalar(4), None, ALU.mult))
                c.step(vec.tensor_scalar(t, sc2, scalar(3), None, ALU.mult))
                c.step(vec.tensor_scalar(bi2, t, -1.0, scalar(5), ALU.mult, ALU.add))
                vec.tensor_scalar(sa, sc2, scalar(6), None, ALU.mult)
                vec.tensor_scalar(sb, bi2, scalar(6), None, ALU.mult)


def stage_attended(nc, held, m):
    s = semaphores(nc, held, "attended", "normed staged first copied")

    with nc.Block() as block:
        @block.vector
        def _(vec):
            def step(t, u):
                if live(t):
                    for j in range(GRP):
                        img = bass.ds(t * GRP + j, 1)
                        e = vec.tensor_scalar(m.b[:, img, :], m.b[:, img, :], m.aff[:, 0, img], m.aff[:, 1, img],
                                              ALU.mult, ALU.add)
                    e.then_inc(s.normed, 1)
                g = t - 2
                if live(g):
                    vec.wait_ge(s.first, g + 1)
                    vec.tensor_copy(m.half17[:, bass.ds(g * GRP, GRP), :],
                                    m.ps[u % 2][:, 0:GRP * FM].rearrange("p (t x) -> p t x", t=GRP))\
                        .then_inc(s.copied, 1)
            sweep(vec, step, 2)

        @block.scalar
        def _(act):
            def step(t, u):
                act.wait_ge(s.normed, t + 1)
                reached(act, s.first, t - 1)
                for j in range(GRP):
                    img = bass.ds(t * GRP + j, 1)
                    e = act.activation(m.ust[:, u % 2, j, :], m.b[:, img, :].rearrange("p a w -> p (a w)"), ACT.Identity,
                                       scale=m.aff[:, 2, img], bias=m.aff[:, 3, img])
                e.then_inc(s.staged, 1)
            sweep(act, step, 0)

        @block.tensor
        def _(pe):
            def step(t, u):
                pe.wait_ge(s.staged, t + 1)
                reached(pe, s.copied, t - 1)
                for j in range(GRP):
                    mm = pe.matmul(m.ps[u % 2][:, j * FM:j * FM + FM], m.ust[:, u % 2, j, :], m.dft17,
                                   start=True, stop=True)
                mm.then_inc(s.first, 1)
            sweep(pe, step, 0)


def stage_mixer(nc, held, m, i):
    s = semaphores(nc, held, f"mixer{i}", "v second added rooted coef turned copied")
    rounds = [(0, 12), (12, 24), (24, 34)]
    zr, zi, t1, t2 = (m.spare[:, NM * k:NM * k + NM] for k in range(4))
    wide = m.spare[:, 4 * NM:4 * NM + FM * FM]
    prod = m.spare[:, 0:FM * FM]
    k0 = 6 if i == 1 else 10
    var, root, fac, con = (m.col[:, 16 + j:17 + j] for j in range(4))

    with nc.Block() as block:
        @block.tensor
        def _(pe):
            for r, (lo, hi) in enumerate(rounds):
                for xf in range(lo, hi):
                    mm = pe.matmul(m.ps[r][:, (xf - lo) * FM:(xf - lo) * FM + FM], m.half17[:, :, xf], m.dft17,
                                   start=True, stop=True)
                mm.then_inc(s.second, 1)
            turn_coefficients(pe, m, s, 0)

        @block.scalar
        def _(act):
            act.wait_ge(s.added, 1)
            act.activation(root, var, ACT.Sqrt).then_inc(s.rooted, 1)
            copy_coefficients(act, m, s, 0)

        @block.vector
        def _(vec):
            c = Chain(vec, s.v)
            for r, (lo, hi) in enumerate(rounds):
                vec.wait_ge(s.second, r + 1)
                e = vec.tensor_copy(m.feat[:, lo:hi, :].rearrange("p x y -> p (x y)"), m.ps[r][:, 0:(hi - lo) * FM])
                if r == 2:
                    c.step(e)
            form_modes(vec, c, m.feat, m.modes, K17)
            wr, wi = (m.mixw[:, :, :, k].rearrange("p r k -> p (r k)") for k in (0, 1))
            xr, xi = m.modes[:, 0], m.modes[:, 1]
            vec.tensor_tensor(zr, xr, wr, ALU.mult)
            vec.tensor_tensor(t1, xi, wi, ALU.mult)
            vec.tensor_tensor(zi, xr, wi, ALU.mult)
            c.step(vec.tensor_tensor(t2, xi, wr, ALU.mult))
            vec.tensor_tensor(zr, zr, t1, ALU.subtract)
            c.step(vec.tensor_tensor(zi, zi, t2, ALU.add))
            c.step(form_coefficients(vec, m, zr, zi))
            g = m.coef.rearrange("p x y -> p (x y)")
            c.step(vec.tensor_tensor(wide, g, m.var, ALU.mult))
            c.step(vec.tensor_tensor_reduce(prod, wide, g, 1.0, 0.0, ALU.mult, ALU.add, var))
            vec.tensor_scalar(var, var, EPS, None, ALU.add).then_inc(s.added, 1)
            vec.wait_ge(s.rooted, 1)
            c.step(vec.reciprocal(root, root))
            c.step(vec.tensor_tensor(fac, root, m.sc[:, k0 + 2:k0 + 3], ALU.mult))
            c.step(vec.tensor_tensor(con, m.sc[:, k0 + 1:k0 + 2], m.sc[:, k0 + 3:k0 + 4], ALU.add))
            c.step(vec.tensor_scalar(g, g, fac, None, ALU.mult))
            vec.tensor_copy(g[:, 0:1], con).then_inc(s.coef, 1)


def stage_residual(nc, held, m, ins):
    s = semaphores(nc, held, "residual", "in0 in1 in2 in3 normed partly whole")
    arrived = [s.in0, s.in1, s.in2, s.in3]
    x_img = ins['x'].rearrange("b t h w -> h (b t) w")
    load = m.spare[:, 0:4 * 512].rearrange("p (s t w) -> p s t w", s=4, t=GRP)

    with nc.Block() as block:
        @block.sync
        def _(sp):
            def body(it):
                for u in range(UN):
                    g = it * UN + u
                    reached(sp, s.whole, g - UN + 1)
                    sp.dma_start(load[:, u], x_img[:, bass.ds(g * GRP, GRP), :]).then_inc(arrived[u], 16)
            body(0)
            with sp.Fori(1, NG // UN) as it:
                body(it)

        @block.scalar
        def _(act):
            def step(t, u):
                for j in range(GRP):
                    img = bass.ds(t * GRP + j, 1)
                    a = m.a[:, img, :].rearrange("p a w -> p (a w)")
                    e = act.activation(a, a, ACT.Identity, scale=m.aff[:, 0, img], bias=m.aff[:, 1, img])
                e.then_inc(s.normed, 1)
            sweep(act, step, 0)

        @block.gpsimd
        def _(pool):
            def body(it):
                for u in range(UN):
                    g = it * UN + u
                    pool.wait_ge(arrived[u], (it + 1) * 16)
                    pool.tensor_tensor(group(m.b, g), group(m.b, g), load[:, u], ALU.add).then_inc(s.partly, 1)
            with pool.Fori(0, NG // UN) as it:
                body(it)

        @block.vector
        def _(vec):
            def step(t, u):
                if live(t):
                    reached(vec, s.whole, t)
                    vec.wait_ge(s.normed, t + 1)
                    vec.wait_ge(s.partly, t + 1)
                    vec.tensor_tensor(group(m.b, t), group(m.b, t), group(m.a, t), ALU.add).then_inc(s.whole, 1)
                g = t - 1
                if live(g):
                    if isinstance(g, int) and g == NG - 1:
                        vec.wait_ge(s.whole, NG)
                    for j in range(GRP):
                        img = bass.ds(g * GRP + j, 1)
                        vec.bn_stats(m.stat[:, img, :], m.b[:, img, :])
            sweep(vec, step, 1)



def row_factors(vec, c, st, fac, factor, rooted):
    mean, dev, t, q = (fac[:, i, :] for i in range(4))
    vec.tensor_tensor(t, st[:, :, 1], st[:, :, 4], ALU.add)
    c.step(vec.tensor_tensor(dev, st[:, :, 1], st[:, :, 4], ALU.subtract))
    vec.tensor_scalar(mean, t, 0.5, None, ALU.mult)
    c.step(vec.tensor_scalar(dev, dev, 0.5, None, ALU.mult))
    c.step(vec.tensor_tensor(dev, dev, dev, ALU.mult))
    c.step(vec.tensor_tensor(q, st[:, :, 2], st[:, :, 5], ALU.add))
    c.step(vec.scalar_tensor_tensor(out=dev, in0=q, scalar=1.0 / D, in1=dev, op0=ALU.mult, op1=ALU.add))
    vec.tensor_scalar(dev, dev, EPS, None, ALU.add).then_inc(factor, 1)
    vec.wait_ge(rooted, 1)
    c.step(vec.reciprocal(dev, dev))


def stage_normed(nc, held, m, ins):
    s = semaphores(nc, held, "normed", "v loaded turned mapsc maps done rooted factor staged turnedr copied")
    names = ['L1_attn_rotation_params', 'L1_attn_entangle_params', 'L1_attn_Wq', 'L1_attn_Wk', 'L1_attn_Wv']
    raw = m.kT[:, 0:640].rearrange("p (k d) -> p k d", k=5)
    rawT = m.kT[:, 640:1280].rearrange("p (k d) -> p k d", k=5)
    fac = m.kT[:, 1280:1280 + 4 * NI].rearrange("p (k t) -> p k t", k=4)
    ln = m.qT[:, 0:1024].rearrange("p (s t w) -> p s t w", s=2, t=GRP)

    with nc.Block() as block:
        @block.sync
        def _(sp):
            for i, n in enumerate(names):
                src = ins[n]
                if len(src.shape) == 1:
                    src = src.rearrange("(d e) -> d e", d=D)
                sp.dma_start(raw[:, i, :], src).then_inc(s.loaded, 16)

        @block.tensor
        def _(pe):
            pe.wait_ge(s.loaded, 80)
            for i in range(5):
                mm = pe.transpose(m.ps[4 + i // 4][:, (i % 4) * D:(i % 4) * D + D], raw[:, i, :], m.ident)
            mm.then_inc(s.turned, 1)
            pe.wait_ge(s.mapsc, 1)
            for i in (0, 1):
                mm = pe.matmul(m.ps[6][:, i * D:i * D + D], rawT[:, i, :], rawT[:, 2 + i, :], start=True, stop=True)
            mm.then_inc(s.maps, 1)

            def step(t, u):
                pe.wait_ge(s.staged, t + 1)
                reached(pe, s.copied, t - 1)
                for j in range(GRP):
                    mm = pe.transpose(m.ps[u % 2][:, j * P:j * P + P], ln[:, u % 2, j, :], m.ident)
                mm.then_inc(s.turnedr, 1)
            sweep(pe, step, 0)

        @block.scalar
        def _(act):
            act.wait_ge(s.factor, 1)
            act.activation(fac[:, 1], fac[:, 1], ACT.Sqrt).then_inc(s.rooted, 1)

            def step(t, u):
                act.wait_ge(s.turnedr, t + 1)
                act.copy(group(m.a, t), banked(m, u % 2)).then_inc(s.copied, 1)
            sweep(act, step, 0)

        @block.vector
        def _(vec):
            c = Chain(vec, s.v)
            row_factors(vec, c, m.stat, fac, s.factor, s.rooted)
            vec.memset(m.halves[:, :], 0.5)
            vec.memset(m.v[:, :, D:D + 1], 1.0)
            vec.wait_ge(s.turned, 1)
            vec.tensor_copy(rawT[:, 0:4, :].rearrange("p k d -> p (k d)"), m.ps[4][:, :])
            vec.tensor_copy(rawT[:, 4, :], m.ps[5][:, 0:D]).then_inc(s.mapsc, 1)
            vec.wait_ge(s.maps, 1)
            vec.wait_ge(s.mapsc, 1)
            vec.tensor_copy(m.maps[:, 0:2, :].rearrange("p k d -> p (k d)"), m.ps[6][:, 0:2 * D])
            vec.tensor_copy(m.maps[:, 2, :], rawT[:, 4, :])

            def step(t, u):
                reached(vec, s.turnedr, t - 1)
                for j in range(GRP):
                    img = t * GRP + j
                    e = vec.tensor_scalar(ln[:, u % 2, j, :], m.b[:, bass.ds(img, 1), :], fac[:, 0, bass.ds(img, 1)],
                                          fac[:, 1, bass.ds(img, 1)], ALU.subtract, ALU.mult)
                e.then_inc(s.staged, 1)
            sweep(vec, step, 0)


LEAD = 3


def stage_attention(nc, held, m):
    s = semaphores(nc, held, "attn", "proj_k proj_q proj_v k_copied k_squared q_copied q_squared v_copied q_norm k_norm "
                   "q_norm_copied k_norm_copied turned v_stored scores dist inner outer summed recip added")
    a = m.a[:, :, :].rearrange("p a b -> p (a b)")
    vst, sq = m.dist[:, 0, :], m.prb
    NC = SEQ // 512
    ONE = 1
    TILES = NQC * KT

    with nc.Block() as block:
        @block.tensor
        def _(pe):
            for sem in (s.k_norm, s.q_norm, s.turned, s.summed):
                pe.sem_inc(sem, ONE)
            with pe.Fori(0, NB) as b:
                pe.wait_ge(s.dist, ONE + b * TILES)
                pe.wait_ge(s.added, ONE + b * (NQC * 4))
                for ch in range(NC):
                    n = b * NC + ch
                    src = a[:, bass.ds(n * 512, 512)]
                    pe.wait_ge(s.k_copied, ONE + n)
                    pe.matmul(m.ps[0][:, :], m.maps[:, 1, :], src, start=True, stop=True).then_inc(s.proj_k, 1)
                    pe.wait_ge(s.q_copied, ONE + n)
                    pe.wait_ge(s.q_squared, ONE + n)
                    pe.matmul(m.ps[1][:, :], m.maps[:, 0, :], src, start=True, stop=True).then_inc(s.proj_q, 1)
                    pe.wait_ge(s.v_copied, ONE + n)
                    pe.matmul(m.ps[2][:, :], m.maps[:, 2, :], src, start=True, stop=True).then_inc(s.proj_v, 1)
                    pe.wait_ge(s.q_norm_copied, ONE + n)
                    pe.wait_ge(s.q_squared, ONE + n + 1)
                    pe.matmul(m.ps[3][:, :], m.halves[:, :], sq[:, 1, :], start=True, stop=True).then_inc(s.q_norm, 1)
                    pe.wait_ge(s.k_norm_copied, ONE + n)
                    pe.wait_ge(s.k_squared, ONE + n + 1)
                    for j in range(4):
                        mm = pe.matmul(m.ps[4][:, j:j + 1], sq[:, 0, j * P:j * P + P], m.halves[:, 0:1],
                                       start=True, stop=True)
                    mm.then_inc(s.k_norm, 1)
                    pe.wait_ge(s.v_stored, ONE + n)
                    pe.wait_ge(s.v_copied, ONE + n + 1)
                    for j in range(4):
                        mm = pe.transpose(m.ps[5][:, j * P:j * P + P], vst[:, j * P:j * P + P], m.ident)
                    mm.then_inc(s.turned, 1)
                for sem in (s.k_copied, s.q_copied, s.q_squared, s.v_stored, s.q_norm_copied, s.k_norm_copied):
                    pe.wait_ge(sem, ONE + (b + 1) * NC)

                def run(qc, first, last):
                    n0 = (b * NQC + qc) * KT

                    def scores(k):
                        if not first or k >= 4:
                            pe.wait_ge(s.dist, ONE + n0 + k - 3)
                        q = bass.ds((qc + k // KT) * QC, QC)
                        pe.matmul(m.ps[k % 4][:, :], m.kT[:, k % KT * P:k % KT * P + P], m.qT[:, q],
                                  start=True, stop=True).then_inc(s.scores, 1)
                    if first:
                        for k in range(LEAD):
                            scores(k)
                    for k in range(KT):
                        if k + LEAD < (KT if last else KT + LEAD):
                            scores(k + LEAD)
                        pe.wait_ge(s.outer, ONE + n0 + k + 1)
                        if k == 0 and not first:
                            pe.wait_ge(s.added, ONE + (b * NQC + qc) * 4)
                        for j in range(4):
                            mm = pe.matmul(m.ps[4 + j][:, 0:D + 1], m.prb[:, k % 2, j * P:j * P + P], m.v[:, k, :],
                                           start=(k == 0), stop=(k == KT - 1))
                        mm.then_inc(s.summed, 1)
                run(0, True, False)
                with pe.Fori(1, NQC - 1) as qc:
                    run(qc, False, False)
                run(NQC - 1, False, True)

        @block.vector
        def _(vec):
            for sem in (s.q_copied, s.q_norm_copied, s.k_norm_copied, s.v_stored, s.dist, s.added):
                vec.sem_inc(sem, ONE)
            with vec.Fori(0, NB) as b:
                for ch in range(NC):
                    n = b * NC + ch
                    vec.wait_ge(s.proj_q, n + 1)
                    vec.tensor_copy(m.qT[:, ch * 512:ch * 512 + 512], m.ps[1][:, :]).then_inc(s.q_copied, 1)
                    vec.wait_ge(s.q_norm, ONE + n + 1)
                    vec.tensor_copy(m.q2[:, ch * 512:ch * 512 + 512], m.ps[3][:, :]).then_inc(s.q_norm_copied, 1)
                    vec.wait_ge(s.k_norm, ONE + n + 1)
                    vec.tensor_copy(m.k2[:, 4 * ch:4 * ch + 4], m.ps[4][:, 0:4]).then_inc(s.k_norm_copied, 1)
                    vec.wait_ge(s.turned, ONE + n + 1)
                    vec.tensor_copy(m.v[:, 4 * ch:4 * ch + 4, 0:D], m.ps[5][:, :].rearrange("p (j d) -> p j d", j=4))\
                        .then_inc(s.v_stored, 1)
                vec.wait_ge(s.q_norm_copied, ONE + (b + 1) * NC)
                vec.wait_ge(s.k_norm_copied, ONE + (b + 1) * NC)

                def distances(qc, k, first):
                    n0 = (b * NQC + qc) * KT
                    vec.wait_ge(s.scores, n0 + k + 1)
                    vec.wait_ge(s.outer, ONE + (n0 + k - 1 if k >= 2 or not first else n0))
                    vec.scalar_tensor_tensor(out=m.dist[:, k % 2, :], in0=m.ps[k % 4][:, :], scalar=m.k2[:, k:k + 1],
                                             in1=m.q2[:, bass.ds(qc * QC, QC)], op0=ALU.subtract,
                                             op1=ALU.subtract).then_inc(s.dist, 1)

                def finish(qc):
                    c = b * NQC + qc
                    rows = [bass.ds(b * KT + qc * 4 + j, 1) for j in range(4)]
                    vec.wait_ge(s.summed, ONE + c * KT + KT)
                    for j in range(4):
                        e = vec.reciprocal(m.rden[:, j:j + 1], m.ps[4 + j][:, D:D + 1])
                    e.then_inc(s.recip, 1)
                    vec.wait_ge(s.recip, c + 1)
                    for j in range(4):
                        x = m.b[:, rows[j], :].rearrange("p a d -> p (a d)")
                        vec.scalar_tensor_tensor(out=x, in0=m.ps[4 + j][:, 0:D], scalar=m.rden[:, j:j + 1], in1=x,
                                                 op0=ALU.mult, op1=ALU.add).then_inc(s.added, 1)
                    vec.wait_ge(s.added, ONE + c * 4 + 4)
                    vec.tensor_copy(m.rden[:, 4:8], m.rden[:, 0:4])
                    for j in range(4):
                        vec.bn_stats(m.st[:, rows[j], :], m.b[:, rows[j], :])

                def run(qc, first):
                    for k in range(KT):
                        distances(qc, k, first)
                        if k == 1 and not first:
                            finish(qc - 1)
                run(0, True)
                with vec.Fori(1, NQC) as qc:
                    run(qc, False)
                finish(NQC - 1)

        @block.scalar
        def _(act):
            for sem in (s.k_copied, s.k_squared, s.q_squared, s.v_copied, s.outer):
                act.sem_inc(sem, ONE)
            with act.Fori(0, NB) as b:
                for ch in range(NC):
                    n = b * NC + ch
                    act.wait_ge(s.proj_k, n + 1)
                    act.wait_ge(s.k_norm, ONE + n)
                    act.activation(sq[:, 0, :], m.ps[0][:, :], ACT.Square).then_inc(s.k_squared, 1)
                    act.copy(m.kT[:, ch * 512:ch * 512 + 512], m.ps[0][:, :]).then_inc(s.k_copied, 1)
                    act.wait_ge(s.q_copied, ONE + n + 1)
                    act.wait_ge(s.q_norm, ONE + n)
                    act.activation(sq[:, 1, :], m.ps[1][:, :], ACT.Square).then_inc(s.q_squared, 1)
                    act.wait_ge(s.proj_v, n + 1)
                    act.wait_ge(s.turned, ONE + n)
                    act.copy(vst, m.ps[2][:, :]).then_inc(s.v_copied, 1)
                act.wait_ge(s.k_norm, ONE + (b + 1) * NC)
                with act.Fori(0, NQC) as qc:
                    n0 = (b * NQC + qc) * KT
                    for k in range(KT):
                        act.wait_ge(s.dist, ONE + n0 + k + 1)
                        act.activation(m.dist[:, k % 2, :], m.dist[:, k % 2, :], ACT.Exp, scale=2.0).then_inc(s.inner, 1)
                        act.wait_ge(s.inner, n0 + k + 1)
                        act.wait_ge(s.summed, ONE + (n0 + k - 1 if k >= 2 else n0))
                        act.activation(m.prb[:, k % 2, :], m.dist[:, k % 2, :], ACT.Exp).then_inc(s.outer, 1)


def stage_experts(nc, held, m, ins, out):
    s = semaphores(nc, held, "experts", "loaded v factor rooted normed turned copied logits shifted exp gates gates_turned "
                   "gates_copied biased tiles scaled_a scaled_b scaled_sum reduced partly result stored0 stored1")
    out_img = out.rearrange("b t h w -> h (b t) w")
    ONE = 1
    stored = [s.stored0, s.stored1]

    with nc.Block() as block:
        @block.sync
        def _(sp):
            with nc.allow_non_contiguous_dma(reason="weights of the experts, once"):
                sp.dma_start(m.w8[:, :].rearrange("p (e c) -> p e c", e=EXPERTS),
                             ins['L1_ffn_expert_w'].rearrange("e d c -> d e c")).then_inc(s.loaded, 16)
                sp.dma_start(m.rw[:, :], ins['L1_ffn_router_w']).then_inc(s.loaded, 16)
                sp.dma_start(m.rb[:, :], ins['L1_ffn_router_b'].partition_broadcast(P)).then_inc(s.loaded, 16)
                sp.dma_start(m.eb[:, :], ins['L1_ffn_expert_b']).then_inc(s.loaded, 16)
            with sp.Fori(0, NG // 2) as it:
                for u in (0, 1):
                    g = it * 2 + u
                    sp.wait_ge(s.result, g + 1)
                    sp.dma_start(out_img[:, bass.ds(g * GRP, GRP), :], m.y[:, u]).then_inc(stored[u], 16)
            for u in (0, 1):
                sp.wait_ge(stored[u], NG // 2 * 16)

        @block.tensor
        def _(pe):
            pe.wait_ge(s.loaded, 64)

            def experts(g, u, tiles):
                for j in tiles:
                    n = g * GRP + j
                    reached(pe, s.scaled_a, n - 1)
                    reached(pe, s.scaled_b, n - 1)
                    for h in (0, 1):
                        mm = pe.matmul(m.ps[4 + 2 * (j % 2) + h][:, :], m.lnT[:, u, j, :], m.w8[:, 512 * h:512 * h + 512],
                                       start=True, stop=True)
                    mm.then_inc(s.tiles, 1)

            def step(t, u):
                if live(t):
                    pe.wait_ge(s.normed, t + 1)
                    reached(pe, s.copied, t)
                    for j in range(GRP):
                        mm = pe.transpose(m.ps[0][:, j * P:j * P + P], m.ln[:, u % 2, j, :], m.ident)
                    mm.then_inc(s.turned, 1)
                g, v = t - 1, (u - 1) % 2
                if live(g):
                    pe.wait_ge(s.gates_copied, g + 1)
                    reached(pe, s.result, g)
                    for j in range(GRP):
                        mm = pe.matmul(m.ps[3][:, j * D:j * D + D], m.gT[:, v, j, :], m.eb[:, :], start=True, stop=True)
                    mm.then_inc(s.biased, 1)
                    experts(g, v, (0, 1))
                if live(t):
                    pe.wait_ge(s.copied, t + 1)
                    reached(pe, s.shifted, t)
                    for j in range(GRP):
                        mm = pe.matmul(m.ps[1][:, j * EXPERTS:j * EXPERTS + EXPERTS], m.lnT[:, u % 2, j, :], m.rw[:, :],
                                       start=True, stop=True)
                    mm.then_inc(s.logits, 1)
                if live(g):
                    experts(g, v, (2, 3))
                if live(t):
                    pe.wait_ge(s.gates, t + 1)
                    reached(pe, s.gates_copied, t)
                    for j in range(GRP):
                        mm = pe.transpose(m.ps[2][0:EXPERTS, j * P:j * P + P], m.gt[:, u % 2, 5, j, :], m.ident)
                    mm.then_inc(s.gates_turned, 1)
            sweep(pe, step, 1)

        @block.scalar
        def _(act):
            act.wait_ge(s.factor, 1)
            act.activation(m.fac[:, 1], m.fac[:, 1], ACT.Sqrt).then_inc(s.rooted, 1)

            def scale(g, u, tiles):
                for j in tiles:
                    n = g * GRP + j
                    act.wait_ge(s.tiles, n + 1)
                    reached(act, s.scaled_sum, n - 1)
                    for e in range(4):
                        o = act.activation(m.pb[:, j % 2, e, :], m.ps[5 + 2 * (j % 2)][:, e * D:e * D + D], ACT.Copy,
                                           scale=m.gt[:, u, 5, j, 4 + e:5 + e])
                    o.then_inc(s.scaled_b, 1)

            def step(t, u):
                if live(t):
                    act.wait_ge(s.turned, t + 1)
                    reached(act, s.tiles, (t - 1) * GRP)
                    act.copy(m.lnT[:, u % 2], banked(m, 0)).then_inc(s.copied, 1)
                g, v = t - 1, (u - 1) % 2
                if live(g):
                    scale(g, v, (0, 1))
                if live(t):
                    act.wait_ge(s.shifted, t + 1)
                    act.activation(m.gt[:, u % 2, 1], m.gt[:, u % 2, 1], ACT.Exp).then_inc(s.exp, 1)
                if live(g):
                    scale(g, v, (2, 3))
                if live(t):
                    act.wait_ge(s.gates_turned, t + 1)
                    act.copy(m.gT[:, u % 2], m.ps[2][0:EXPERTS, :].rearrange("p (t w) -> p t w", t=GRP))\
                        .then_inc(s.gates_copied, 1)
            sweep(act, step, 1)

        @block.gpsimd
        def _(pool):
            with pool.Fori(0, NI // 2) as it:
                for u in (0, 1):
                    n = it * 2 + u
                    pool.wait_ge(s.scaled_a, n + 1)
                    pool.wait_ge(s.scaled_b, n + 1)
                    pool.wait_ge(s.reduced, ONE + it * 2)
                    pool.tensor_tensor(m.pc[:, u], m.pa[:, u], m.pb[:, u], ALU.add).then_inc(s.scaled_sum, 1)

        @block.vector
        def _(vec):
            c = Chain(vec, s.v)
            vec.sem_inc(s.reduced, ONE)
            vec.wait_ge(s.loaded, 64)
            row_factors(vec, c, m.st, m.fac, s.factor, s.rooted)

            def normed(t, u):
                reached(vec, s.turned, t - 1)
                for j in range(GRP):
                    img = bass.ds(t * GRP + j, 1)
                    e = vec.tensor_scalar(m.ln[:, u % 2, j, :], m.b[:, img, :], m.fac[:, 0, img], m.fac[:, 1, img],
                                          ALU.subtract, ALU.mult)
                e.then_inc(s.normed, 1)

            def weigh(g, u, tiles, before):
                for j in tiles:
                    n = g * GRP + j
                    vec.wait_ge(s.tiles, n + 1)
                    reached(vec, s.scaled_sum, n - 1)
                    src = m.ps[4 + 2 * (j % 2)][:, :].rearrange("p (e c) -> p e c", e=4)
                    vec.tensor_tensor(m.pa[:, j % 2], src, over(m.gt[:, u, 5, j, 0:4], 2, D), ALU.mult)\
                        .then_inc(s.scaled_a, 1)
                for j in tiles:
                    n = g * GRP + j
                    if j == 0:
                        reached(vec, stored[u], before * 16)
                    vec.wait_ge(s.scaled_sum, n + 1)
                    vec.tensor_reduce(m.y[:, u, j, :], m.pc[:, j % 2].rearrange("p e c -> p c e"), AX.X, ALU.add)\
                        .then_inc(s.reduced, 1)

            def gates(t, u):
                logit, ex, sel, cnt, best, gate = (m.gt[:, u, i] for i in range(6))
                top, total = m.g1[:, 0], m.g1[:, 1]
                vec.wait_ge(s.logits, t + 1)
                c.step(vec.tensor_tensor(logit, m.ps[1][:, 0:GRP * EXPERTS].rearrange("p (t e) -> p t e", t=GRP),
                                         over(m.rb[:, :], 1, GRP), ALU.add))
                c.step(vec.tensor_reduce(top, logit, AX.X, ALU.max))
                vec.tensor_tensor(ex, logit, over(top, 2, EXPERTS), ALU.subtract).then_inc(s.shifted, 1)
                other, own = over(logit, 2, EXPERTS), over(logit, 3, EXPERTS)
                vec.tensor_tensor(m.rk[:, 0], other, own, ALU.is_gt)
                c.step(vec.tensor_tensor(m.rk[:, 1], other, own, ALU.is_equal))
                c.step(vec.tensor_tensor(m.rk[:, 1], m.rk[:, 1], over(m.tie, 1, GRP), ALU.mult))
                c.step(vec.tensor_tensor(m.rk[:, 0], m.rk[:, 0], m.rk[:, 1], ALU.add))
                c.step(vec.tensor_reduce(cnt, m.rk[:, 0], AX.X, ALU.add))
                c.step(vec.tensor_scalar(sel, cnt, 1.5, None, ALU.is_lt))
                vec.wait_ge(s.exp, t + 1)
                c.step(vec.tensor_tensor(best, ex, sel, ALU.mult))
                c.step(vec.tensor_reduce(total, best, AX.X, ALU.add))
                c.step(vec.reciprocal(total, total))
                vec.tensor_tensor(gate, best, over(total, 2, EXPERTS), ALU.mult).then_inc(s.gates, 1)
            PER = 10

            def step(t, u, it):
                if isinstance(t, int) and t == 0:
                    normed(0, 0)
                g, v = t - 1, (u - 1) % 2
                before = it * (UN // 2) + (u - 1) // 2
                if live(g):
                    weigh(g, v, (0, 1), before)
                if live(t):
                    gates(t, u % 2)
                if live(t + 1):
                    normed(t + 1, u + 1)
                if live(g):
                    weigh(g, v, (2, 3), before)
                    vec.wait_ge(s.biased, g + 1)
                    vec.wait_ge(s.reduced, ONE + (g + 1) * GRP)
                    vec.tensor_tensor(m.y[:, v], m.y[:, v], banked(m, 3), ALU.add).then_inc(s.partly, 1)
                    vec.wait_ge(s.partly, g + 1)
                    vec.tensor_tensor(m.y[:, v], m.y[:, v], group(m.b, g), ALU.add).then_inc(s.result, 1)
            for u in range(UN):
                step(u, u, 0)
            with vec.Fori(1, NG // UN - 1) as it:
                c.enter(it - 1, PER * UN)
                for u in range(UN):
                    step(it * UN + u, u, it)
            c.leave(NG // UN - 2)
            for u in range(UN + 1):
                step(NG - UN + u, u, NG // UN - 1)


def build(nc, ins, const, where, out, upto=99):
    with ExitStack() as ctx:
        tok = nc.dram_tensor("tokens_scratch", (NI, NH, NW), F32, kind="Internal").ap()
        mix = nc.dram_tensor("mixed_scratch", (NI, NH, NW), F32, kind="Internal").ap()
        m = memory(nc, ctx, where)
        held = []
        stages = [
            lambda: stage_tokens(nc, held, m, ins, tok, const),
            lambda: stage_forward(nc, held, m, tok),
            lambda: stage_modes(nc, held, m),
            lambda: stage_weights(nc, held, m),
            lambda: stage_scores(nc, held, m),
            lambda: stage_mix(nc, held, m, mix),
            lambda: stage_inverse(nc, held, m, 'proj', mix=mix),
            lambda: stage_factors(nc, held, m, 'proj'),
            lambda: stage_attended(nc, held, m),
            lambda: stage_mixer(nc, held, m, 1),
            lambda: stage_inverse(nc, held, m, 'mix1', ins=ins),
            lambda: stage_mixer(nc, held, m, 2),
            lambda: stage_inverse(nc, held, m, 'mix2'),
            lambda: stage_factors(nc, held, m, 'mix2'),
            lambda: stage_residual(nc, held, m, ins),
            lambda: stage_normed(nc, held, m, ins),
            lambda: stage_attention(nc, held, m),
            lambda: stage_experts(nc, held, m, ins, out),
        ]
        for i, stage in enumerate(stages[:upto]):
            if i == 8:
                nc.clear_and_free_semaphores(held)
                held.clear()
                nc.all_engine_barrier()
            stage()


NAMES = ['x'] + SCALARS + [
    'L0_conv_key_w', 'L0_conv_key_skip_w', 'L0_conv_key_skip_b', 'L0_conv_query_w', 'L0_conv_query_skip_w',
    'L0_conv_query_skip_b', 'L0_conv_value_w', 'L0_conv_value_skip_w', 'L0_conv_value_skip_b', 'L0_conv_proj_w',
    'L0_conv_proj_skip_w', 'L0_conv_mixer_w1', 'L0_conv_mixer_w2', 'L1_attn_rotation_params',
    'L1_attn_entangle_params', 'L1_attn_Wq', 'L1_attn_Wk', 'L1_attn_Wv', 'L1_ffn_router_w', 'L1_ffn_router_b',
    'L1_ffn_expert_w', 'L1_ffn_expert_b']


def kernel(**inputs):
    import concourse.bacc as bacc
    from concourse.bass_utils import run_bass_kernel_spmd

    nc = bacc.Bacc("TRN2", target_bir_lowering=False, num_devices=1)
    arrays, ins = {}, {}
    for name in NAMES:
        a = np.ascontiguousarray(inputs[name])
        arrays[f"in_{name}"] = a
        ins[name] = nc.dram_tensor(f"in_{name}", a.shape, mybir.dt.from_np(a.dtype), kind="ExternalInput").ap()
    table, where = tables()
    arrays["tables"] = table
    const = nc.dram_tensor("tables", table.shape, F32, kind="ExternalInput").ap()
    out = nc.dram_tensor("result", inputs['x'].shape, F32, kind="ExternalOutput").ap()
    build(nc, ins, const, where, out)
    got = run_bass_kernel_spmd(nc, [arrays], core_ids=[0])
    return got.results[0]["result"]
```

```python
from contextlib import ExitStack

import numpy as np
import concourse.bass as bass
from concourse import mybir

F32 = mybir.dt.float32
F32R = mybir.dt.float32r
F16 = mybir.dt.float16
ALU = mybir.AluOpType
ACT = mybir.ActivationFunctionType
AX = mybir.AxisListType

P = 128
NB, NT, NH, NW = 4, 32, 128, 128
NI = NB * NT
HEADS = 16
K33 = 33
FQ = 2 * K33
K17 = 17
FM = 2 * K17
ROWS = 2 * K17
NM = ROWS * K17
MT = [(m, min(P, NM - m)) for m in range(0, NM, P)]
LOWT = 4
HC = 34
GRP = 4
NG = NI // GRP
UN = 4
PIX = NH * NW
EPS = 1e-5
D = 128
SEQ = NT * NH
KT = SEQ // P
QC = 512
NQC = SEQ // QC
EXPERTS = 8
SCALARS = ['L0_conv_norm1_g', 'L0_conv_norm1_b', 'L0_conv_attn_norm_g', 'L0_conv_attn_norm_b',
           'L0_conv_norm2_g', 'L0_conv_norm2_b', 'L0_conv_mixer_skip_w1', 'L0_conv_mixer_skip_b1',
           'L0_conv_mixer_norm_g1', 'L0_conv_mixer_norm_b1', 'L0_conv_mixer_skip_w2',
           'L0_conv_mixer_skip_b2', 'L0_conv_mixer_norm_g2', 'L0_conv_mixer_norm_b2',
           'L0_conv_mixer_out_g', 'L0_conv_mixer_out_b', 'L0_conv_proj_skip_b']


def tables():
    n = np.arange(P)[:, None]
    k = np.arange(K33)[None, :]
    dft = np.concatenate([np.cos(2 * np.pi * n * k / P), np.sin(2 * np.pi * n * k / P)], 1) / P
    dft[:, K33] = 0.0
    k = np.arange(K17)[:, None]
    idft = np.zeros((P, P))
    idft[:K17] = np.cos(2 * np.pi * k * n.T / P)
    idft[K17:FM] = np.sin(2 * np.pi * k * n.T / P)
    twice = np.where(np.arange(P) % K17 > 0, 2.0, 1.0)[:, None]
    batch = np.kron(np.eye(NB), np.ones((NT, NT))) / NT
    low = np.zeros((ROWS, K17))
    low[0:8, 1:9] = 2
    low[K17 + 1:K17 + 9, 1:9] = 2
    low[1:9, 0] = 2
    low[0, 0] = 1
    lowm = np.zeros(P * len(MT))
    lowm[:NM] = 64 * low.ravel()
    var = np.zeros((2, K17, 2, K17))
    var[:, 1:, :, 1:] = 1
    var[0, 0, :, 1:] = 2
    var[:, 1:, 0, 0] = 0.5
    tie = np.arange(EXPERTS)[None, :] < np.arange(EXPERTS)[:, None]

    def on_all(a):
        return np.broadcast_to(a.reshape(1, -1), (P, a.size))
    parts = [('ident', np.eye(P)), ('tie', on_all(tie)), ('dft', dft), ('rows', idft), ('cols', idft * twice),
             ('batch', batch), ('low', lowm.reshape(len(MT), P).T), ('var', on_all(var))]
    at, where = 0, {}
    for name, a in parts:
        where[name] = (at, at + a.shape[1])
        at += a.shape[1]
    return np.concatenate([a for _, a in parts], 1).astype(np.float32), where


class Names(dict):

    def __getattr__(self, name):
        return self[name]


class Views:
    pass


class Chain:

    def __init__(self, eng, sem):
        self.eng, self.sem, self.n, self.off = eng, sem, 0, 0

    def step(self, ins):
        ins.then_inc(self.sem, 1)
        self.n += 1
        self.eng.wait_ge(self.sem, self.off + self.n)

    def enter(self, it, per):
        self.before, self.per = self.n, per
        self.off = it * per

    def leave(self, count):
        assert self.n - self.before == self.per, (self.n - self.before, self.per)
        self.n = self.before + self.per * count
        self.off = 0


def reached(eng, sem, value):
    if not (isinstance(value, int) and value <= 0):
        eng.wait_ge(sem, value)


def over(ap, axis, n):
    shape = list(ap.shape)
    return ap.unsqueeze(axis).to_broadcast(shape[:axis] + [n] + shape[axis:])


def semaphores(nc, held, stage, names):
    made = {n: nc.alloc_semaphore(f"{stage}_{n}") for n in names.split()}
    held.extend(made.values())
    return Names(made)


def memory(nc, ctx, where):
    m = Views()

    def sb(scope, name, shape, dtype=F32):
        return scope.enter_context(nc.sbuf_tensor(name, shape, dtype))

    m.a = sb(ctx, "images_a", [P, NI, NW])
    m.b = sb(ctx, "images_b", [P, NI, NW])
    keep = sb(ctx, "keep", [P, where['tie'][1]])
    m.keep = keep
    m.ident = keep[:, 0:P]
    m.tie = keep[:, P:].rearrange("p (i j) -> p i j", i=EXPERTS)
    small = sb(ctx, "small", [P, 208])
    m.sc = small[:, 0:len(SCALARS)]
    m.skips = small[:, 32:96]
    m.biases = small[:, 96:144]
    m.col = small[:, 144:176]
    m.gram = small[:, 176:208]
    m.ps = [ctx.enter_context(nc.psum_tensor(f"bank{i}", [P, 512], F32)) for i in range(8)]

    with ExitStack() as l0:
        c0 = where['dft'][0]
        m.tab = sb(l0, "table", [P, where['var'][1] - c0])

        def tab(name, rows=P):
            lo, hi = where[name]
            return m.tab[0:rows, lo - c0:hi - c0]
        m.dft = tab('dft')
        m.dft17 = m.dft.rearrange("p (s k) -> p s k", s=2)[:, :, 0:K17]
        m.rows, m.cols, m.batch, m.low, m.var = tab('rows', FM), tab('cols', FM), tab('batch'), tab('low'), tab('var')
        pair = sb(l0, "pair", [P, 2, 2 * NM])
        m.wraw = pair[0:64, 0, :].rearrange("p (r k c) -> p r k c", r=ROWS, c=2)
        m.weff = pair[0:64, 1, :].rearrange("p (c m) -> p c m", c=2)
        m.feat = pair[:, 0, :].rearrange("p (x y) -> p x y", x=FM)
        m.coef = pair[:, 1, :].rearrange("p (x y) -> p x y", x=FM)
        mixw = sb(l0, "mixer_weights", [P, 2 * NM])
        m.mixw = mixw[:, :].rearrange("p (r k c) -> p r k c", r=ROWS, c=2)
        f = sb(l0, "features", [P, FQ * FQ])
        m.ft = f[:, :].rearrange("p (x y) -> p x y", x=FQ)
        m.half17 = f[:, 0:P * FM].rearrange("p (t x) -> p t x", t=P)
        g = sb(l0, "spare", [P, HC * P])
        m.spare = g[:, :]
        m.gramT = g[:, :].rearrange("p (c t) -> p c t", c=HC)
        m.coefT = g[0:FM, :].rearrange("p (x t) -> p x t", x=FM)
        m.modes = sb(l0, "modes", [P, 2, NM])
        r = sb(l0, "transposed", [P, 1920])
        m.turned = r[:, :]
        m.modesT = r[:, 0:1280].rearrange("p (k c t) -> p k c t", k=5, c=2)
        m.wT = r[:, 1280:1920].rearrange("p (k c h) -> p k c h", k=5, c=2)
        m.stat = r[:, 0:768].rearrange("p (t s) -> p t s", t=P)
        m.aff = r[:, 768:768 + 8 * P].rearrange("p (k t) -> p k t", k=8)
        m.stage = sb(l0, "coef_stage", [P, 2, (GRP - 1) * FM + P])
        m.half = sb(l0, "half_inverse", [P, 2, GRP * NW])
        m.ust = sb(l0, "image_stage", [P, 2, GRP, NW])
        m.tmp = m.modes[:, :, 0:GRP * NW].rearrange("p s (t w) -> p s t w", t=GRP)

    b = m.b[:, :, :].rearrange("p a b -> p (a b)")
    m.half33 = b[:, 0:P * FQ].rearrange("p (t x) -> p t x", t=P)
    m.load = b[:, 12804:12804 + 2048].rearrange("p (s t w) -> p s t w", s=4, t=GRP)
    m.prod = b[:, 0:8192].rearrange("p (k h t) -> p k h t", k=4, h=HEADS)
    m.hg = b[:, 8448:8448 + FQ * FQ]
    m.probT = b[:, 8448:10496].rearrange("p (h t) -> p h t", h=HEADS)
    m.probD = b[:, 0:2048].rearrange("p (h t) -> p h t", h=HEADS)
    m.mixD = b[:, 2048:2176]
    m.mixT = b[:, 2176:2304]
    m.mixA = b[:, 2304:2432]
    m.score, m.expo, m.prob = (b[:, 10496 + 512 * i:11008 + 512 * i].rearrange("p (h s) -> p h s", h=HEADS)
                               for i in range(3))
    m.dcq = b[0:1, 12804:13316].rearrange("p (h s) -> p h s", h=HEADS)
    m.dck = b[0:1, 13316:15364].rearrange("p (h t) -> p h t", h=HEADS)
    m.wk = b[:, 15364:16384]
    m.zprod = b[:, 0:4096].rearrange("p (s k h t) -> p s k h t", s=2, k=4, h=4)
    m.zsum = b[:, 4096:8192].rearrange("p (c h t) -> p c h t", c=2, h=HEADS)

    m.st = sb(ctx, "row_stats", [P, NI, 6])
    with ExitStack() as l1:
        m.scratch = sb(l1, "normed_scratch", [P, 3072])
    with ExitStack() as l1:
        m.kH = sb(l1, "keys_high", [P, SEQ], F32R)
        m.kL = sb(l1, "keys_low", [P, SEQ], F32R)
        m.v = sb(l1, "values", [P, KT, 2 * D + 2], F16)
        m.qH = sb(l1, "queries_high", [P, 2, QC], F32R)
        m.qL = sb(l1, "queries_low", [P, 2, QC], F32R)
        m.q2 = sb(l1, "query_norms", [P, 2, QC])
        m.dist = sb(l1, "distances", [P, 2, QC])
        m.wt = sb(l1, "weights", [P, 2, QC])
        m.wH = sb(l1, "weights_high", [P, 2, QC], F16)
        m.wL = sb(l1, "weights_low", [P, 2, QC], F16)
        m.maps = sb(l1, "maps", [P, 3, D])
        m.unit = sb(l1, "value_units", [P, D])
        m.halves = sb(l1, "halves", [P, P])
        m.k2 = sb(l1, "key_norms", [P, KT])
        m.rden = sb(l1, "reciprocals", [P, 8])
        m.sums = sb(l1, "softmax_sums", [P, 4])
    with ExitStack() as l2:
        m.ln = sb(l2, "normed", [P, 2, GRP, D])
        m.w8 = sb(l2, "expert_weights", [P, EXPERTS * D])
        m.lnT = sb(l2, "normed_T", [P, 2, GRP, P])
        m.rw = sb(l2, "router_weights", [P, EXPERTS])
        m.rb = sb(l2, "router_biases", [P, EXPERTS])
        m.eb = sb(l2, "expert_biases", [EXPERTS, D])
        m.gT = sb(l2, "gates_T", [EXPERTS, 2, GRP, P])
        m.pa = sb(l2, "scaled_a", [P, 2, 4, D])
        m.pb = sb(l2, "scaled_b", [P, 2, 4, D])
        m.pc = sb(l2, "scaled_sum", [P, 2, 4, D])
        m.y = sb(l2, "group_result", [P, 2, GRP, D])
        m.rk = sb(l2, "ranks", [P, 2, GRP, EXPERTS, EXPERTS])
        m.gt = sb(l2, "gates", [P, 2, 6, GRP, EXPERTS])
        m.g1 = sb(l2, "gate_sums", [P, 4, GRP])
        m.fac = sb(l2, "row_factors", [P, 4, NI])
    return m



def stage_tokens(nc, held, m, ins, tok, const):
    s = semaphores(nc, held, "tokens", "tables x weights cleared scalars v sums averaged added rooted stored ready")
    x = ins['x'].rearrange("b t h w -> (b t) h w")
    Q = NH // 4
    nt = m.keep.shape[1]

    with nc.Block() as block:
        @block.sync
        def _(sp):
            for q in range(4):
                sp.dma_start(m.a[:, q * Q:q * Q + Q, :], x[:, q * Q:q * Q + Q, :]).then_inc(s.x, 16)
            sp.wait_ge(s.ready, 1)
            for q in range(4):
                sp.dma_start(tok[:, q * Q:q * Q + Q, :], m.a[:, q * Q:q * Q + Q, :]).then_inc(s.stored, 16)
            sp.wait_ge(s.stored, 64)

        @block.gpsimd
        def _(pool):
            pool.memset(m.wraw, 0.0).then_inc(s.cleared, 1)
            pool.memset(m.mixw, 0.0).then_inc(s.cleared, 1)
            pool.memset(m.turned, 0.0)

        @block.scalar
        def _(act):
            act.dma_start(m.keep[:, :], const[:, 0:nt]).then_inc(s.tables, 16)
            act.dma_start(m.tab[:, :], const[:, nt:]).then_inc(s.tables, 16)
            act.wait_ge(s.cleared, 2)
            with nc.allow_non_contiguous_dma(reason="skip weights and biases, a few numbers"):
                for i, n in enumerate(SCALARS):
                    src = ins[n]
                    if len(src.shape) == 2:
                        src = src.rearrange("a b -> (a b)")
                    act.dma_start(m.sc[:, i:i + 1], src.partition_broadcast(P)).then_inc(s.scalars, 16)
                for i, n in enumerate(['query', 'key', 'value', 'proj']):
                    w = ins[f'L0_conv_{n}_skip_w'].rearrange("a b -> (a b)")
                    act.dma_start(m.skips[:, 16 * i:16 * i + 16], w.partition_broadcast(P)).then_inc(s.scalars, 16)
                    if n == 'proj':
                        w = ins['L0_conv_proj_w'][:, 0]
                        act.dma_start(m.wraw[48:64, 0:16], w[:, 0:16]).then_inc(s.weights, 16)
                        act.dma_start(m.wraw[48:64, K17 + 1:ROWS], w[:, 31:15:-1]).then_inc(s.weights, 16)
                        continue
                    act.dma_start(m.biases[:, 16 * i:16 * i + 16],
                                  ins[f'L0_conv_{n}_skip_b'].partition_broadcast(P)).then_inc(s.scalars, 16)
                    w = ins[f'L0_conv_{n}_w'][0]
                    act.dma_start(m.wraw[16 * i:16 * i + 16, 0:8, 0:9], w[:, 0:8]).then_inc(s.weights, 16)
                    act.dma_start(m.wraw[16 * i:16 * i + 16, K17 + 1:K17 + 9, 0:9], w[:, 15:7:-1])\
                        .then_inc(s.weights, 16)
                load_mixer(act, m, ins, 1, s.weights)
            act.wait_ge(s.added, 1)
            act.activation(m.spare[:, 320:352], m.spare[:, 320:352], ACT.Sqrt).then_inc(s.rooted, 1)
            act.wait_ge(s.added, 2)
            act.activation(m.col[:, 4:5], m.col[:, 3:4], ACT.Sqrt).then_inc(s.rooted, 1)
            act.wait_ge(s.tables, 32)
            act.wait_ge(s.weights, 16 * 10)
            act.wait_ge(s.scalars, 16 * (len(SCALARS) + 7))

        @block.tensor
        def _(pe):
            pe.wait_ge(s.tables, 32)
            pe.wait_ge(s.sums, 1)
            pe.matmul(m.ps[0][:, 0:32], m.batch, m.spare[:, 192:224], start=True, stop=True).then_inc(s.averaged, 1)
            pe.wait_ge(s.sums, 2)
            pe.matmul(m.ps[1][:, 0:32], m.batch, m.spare[:, 352:384], start=True, stop=True).then_inc(s.averaged, 1)

        @block.vector
        def _(vec):
            c = Chain(vec, s.v)
            gs = m.spare[:, 0:192].rearrange("p (g k) -> p g k", g=32)
            two, mean, var, rstd, work = (m.spare[:, 192 + 32 * i:224 + 32 * i] for i in (0, 1, 5, 4, 6))
            dev = m.spare[:, 384:448].rearrange("p (g k) -> p g k", g=32)
            sq = m.spare[:, 448:512].rearrange("p (g k) -> p g k", g=32)
            vec.wait_ge(s.x, 64)
            with vec.Fori(0, 32) as g:
                c.enter(g, 1)
                c.step(vec.bn_stats(gs[:, g, :], m.a[:, :, bass.ds(g * 4, 4)]))
            c.leave(32)
            vec.tensor_tensor(two, gs[:, :, 1], gs[:, :, 4], ALU.add).then_inc(s.sums, 1)
            vec.wait_ge(s.averaged, 1)
            c.step(vec.tensor_scalar(mean, m.ps[0][:, 0:32], 0.5, None, ALU.mult))
            c.step(vec.tensor_tensor(dev, gs[:, :, 1::3], over(mean, 2, 2), ALU.subtract))
            c.step(vec.tensor_tensor(sq, dev, dev, ALU.mult))
            c.step(vec.tensor_reduce(work, sq, AX.X, ALU.add))
            c.step(vec.tensor_scalar(work, work, 0.5, None, ALU.mult))
            c.step(vec.tensor_tensor(var, gs[:, :, 2], gs[:, :, 5], ALU.add))
            vec.scalar_tensor_tensor(out=var, in0=var, scalar=1.0 / 512, in1=work, op0=ALU.mult, op1=ALU.add)\
                .then_inc(s.sums, 1)
            vec.wait_ge(s.averaged, 2)
            vec.tensor_scalar(rstd, m.ps[1][:, 0:32], EPS, None, ALU.add).then_inc(s.added, 1)
            vec.wait_ge(s.rooted, 1)
            c.step(vec.reciprocal(rstd, rstd))
            with vec.Fori(0, 32) as g:
                c.enter(g, 1)
                c.step(vec.tensor_scalar(m.a[:, :, bass.ds(g * 4, 4)], m.a[:, :, bass.ds(g * 4, 4)],
                                         mean[:, bass.ds(g, 1)], rstd[:, bass.ds(g, 1)], ALU.subtract, ALU.mult))
            c.leave(32)
            vec.drain().then_inc(s.ready, 1)
            with vec.Fori(0, 32) as g:
                c.enter(g, 1)
                c.step(vec.bn_stats(gs[:, g, :], m.a[:, bass.ds(g * 4, 4), :].rearrange("p a b -> p (a b)")))
            c.leave(32)
            c.step(vec.bn_aggr(m.col[:, 2:4], m.spare[:, 0:192]))
            vec.tensor_scalar(m.col[:, 3:4], m.col[:, 3:4], EPS, None, ALU.add).then_inc(s.added, 1)
            vec.wait_ge(s.rooted, 2)
            vec.wait_ge(s.scalars, 16 * (len(SCALARS) + 7))
            c.step(vec.reciprocal(m.col[:, 4:5], m.col[:, 4:5]))
            c.step(vec.tensor_tensor(m.col[:, 0:1], m.col[:, 4:5], m.sc[:, 0:1], ALU.mult))
            c.step(vec.tensor_tensor(m.col[:, 5:6], m.col[:, 0:1], m.col[:, 2:3], ALU.mult))
            c.step(vec.tensor_tensor(m.col[:, 1:2], m.sc[:, 1:2], m.col[:, 5:6], ALU.subtract))


def load_mixer(eng, m, ins, i, sem):
    w = ins[f'L0_conv_mixer_w{i}'][0, 0]
    eng.dma_start(m.mixw[:, 0:16], w[0:16].partition_broadcast(P)).then_inc(sem, 16)
    eng.dma_start(m.mixw[:, K17 + 1:ROWS], w[31:15:-1].partition_broadcast(P)).then_inc(sem, 16)


def stage_forward(nc, held, m, tok):
    s = semaphores(nc, held, "forward", "in0 in1 in2 in3 first copied second scaled v")
    arrived = [s.in0, s.in1, s.in2, s.in3]
    tok_img = tok.rearrange("t h w -> h t w")
    per = 6
    rounds = FQ // per

    with nc.Block() as block:
        @block.sync
        def _(sp):
            def body(it):
                for u in range(UN):
                    g = it * UN + u
                    reached(sp, s.first, g - UN + 1)
                    sp.dma_start(m.load[:, u], tok_img[:, bass.ds(g * GRP, GRP), :]).then_inc(arrived[u], 16)
            body(0)
            with sp.Fori(1, NG // UN) as it:
                body(it)

        @block.tensor
        def _(pe):
            def body(it):
                for u in range(UN):
                    g = it * UN + u
                    pe.wait_ge(arrived[u], (it + 1) * 16)
                    reached(pe, s.copied, g - 1)
                    for j in range(GRP):
                        mm = pe.matmul(m.ps[u % 2][:, j * FQ:j * FQ + FQ], m.load[:, u, j, :], m.dft,
                                       start=True, stop=True)
                    mm.then_inc(s.first, 1)
            body(0)
            with pe.Fori(1, NG // UN) as it:
                body(it)
            pe.wait_ge(s.copied, NG)
            for r in range(rounds):
                reached(pe, s.scaled, r - 3)
                for j in range(per):
                    mm = pe.matmul(m.ps[4 + r % 4][:, j * FQ:j * FQ + FQ], m.half33[:, :, r * per + j], m.dft,
                                   start=True, stop=True)
                mm.then_inc(s.second, 1)

        @block.scalar
        def _(act):
            with act.Fori(0, NG // UN) as it:
                for u in range(UN):
                    g = it * UN + u
                    act.wait_ge(s.first, g + 1)
                    act.copy(m.half33[:, bass.ds(g * GRP, GRP), :],
                             m.ps[u % 2][:, 0:GRP * FQ].rearrange("p (t x) -> p t x", t=GRP)).then_inc(s.copied, 1)

        @block.vector
        def _(vec):
            c = Chain(vec, s.v)
            for r in range(rounds):
                vec.wait_ge(s.second, r + 1)
                vec.tensor_scalar(m.ft[:, r * per:r * per + per, :].rearrange("p x y -> p (x y)"),
                                  m.ps[4 + r % 4][:, 0:per * FQ], m.col[:, 0:1], None, ALU.mult)\
                    .then_inc(s.scaled, 1)
            vec.wait_ge(s.scaled, rounds)
            c.step(vec.tensor_scalar(m.ft[:, 0, 0:1], m.ft[:, 0, 0:1], m.col[:, 1:2], None, ALU.add))


def form_modes(vec, c, feat, modes, k):
    f = feat.rearrange("p (a x) (b y) -> p a x b y", a=2, b=2)
    cc, cs, sc, ss = (f[:, a, 0:K17, b, 0:K17] for a in (0, 1) for b in (0, 1))
    re, im = (modes[:, i].rearrange("p (r k) -> p r k", r=ROWS) for i in (0, 1))
    vec.tensor_tensor(re[:, 0:K17], cc, ss, ALU.subtract)
    vec.tensor_tensor(re[:, K17:ROWS], cc, ss, ALU.add)
    vec.tensor_tensor(im[:, K17:ROWS], sc, cs, ALU.subtract)
    c.step(vec.scalar_tensor_tensor(out=im[:, 0:K17], in0=sc, scalar=-1.0, in1=cs, op0=ALU.mult, op1=ALU.subtract))


def stage_modes(nc, held, m):
    s = semaphores(nc, held, "modes", "v modes weights high turned copied gram")
    R2 = 2.0 ** 0.5
    wt = m.weff.rearrange("p c (r k) -> p c r k", r=ROWS)
    jobs = []
    for k, (m0, n) in enumerate(MT):
        jobs += [(m.weff[:, cpt, m0:m0 + n], n, m.wT[0:n, k, cpt, :], 64, 'weights') for cpt in (0, 1)]
    for k, (m0, n) in enumerate(MT):
        jobs += [(m.modes[:, cpt, m0:m0 + n], n, m.modesT[0:n, k, cpt, :], P, 'modes') for cpt in (0, 1)]
    banks = [jobs[i:i + 2] for i in range(0, len(jobs), 2)]
    hbanks = [list(range(i, min(HC, i + 4))) for i in range(0, HC, 4)]
    NBK = 6

    with nc.Block() as block:
        @block.vector
        def _(vec):
            c = Chain(vec, s.v)
            wre, wim = wt[:, 0], wt[:, 1]
            vec.tensor_copy(wre, m.wraw[:, :, :, 0])
            c.step(vec.tensor_copy(wim, m.wraw[:, :, :, 1]))
            pr, nr = wre[0:48, 1:9, 0], wre[0:48, K17 + 1:K17 + 9, 0]
            pi, ni = wim[0:48, 1:9, 0], wim[0:48, K17 + 1:K17 + 9, 0]
            even, odd = m.spare[0:48, 0:8], m.spare[0:48, 8:16]
            vec.tensor_tensor(even, pr, nr, ALU.add)
            c.step(vec.tensor_tensor(odd, pi, ni, ALU.subtract))
            vec.tensor_scalar(pr, even, 0.5, None, ALU.mult)
            vec.tensor_scalar(nr, even, 0.5, None, ALU.mult)
            vec.tensor_scalar(pi, odd, 0.5, None, ALU.mult)
            vec.tensor_scalar(ni, odd, -0.5, None, ALU.mult)
            c.step(vec.memset(wim[0:48, 0:1, 0], 0.0))
            vec.drain().then_inc(s.weights, 1)
            form_modes(vec, c, m.ft, m.modes, K33)
            vec.drain().then_inc(s.modes, 1)
            h, f = m.hg.rearrange("p (x y) -> p x y", x=FQ), m.ft
            c.step(vec.tensor_scalar(m.hg, m.ft.rearrange("p x y -> p (x y)"), 2.0, None, ALU.mult))
            c.step(vec.tensor_scalar(h[:, :, 0:K33:32], f[:, :, 0:K33:32], R2, None, ALU.mult))
            c.step(vec.tensor_scalar(h[:, 0, :], f[:, 0, :], R2, None, ALU.mult))
            c.step(vec.tensor_copy(h[:, 0, 0:K33:32], f[:, 0, 0:K33:32]))
            c.step(vec.memset(h[:, 32:66:33, :], 0.0))
            a1, a2, a3, a4 = (m.spare[:, 16 + 32 * i:48 + 32 * i] for i in range(4))
            vec.tensor_tensor(a1, f[:, 32, 1:33], f[:, 65, 34:66], ALU.add)
            c.step(vec.tensor_tensor(a2, f[:, 65, 1:33], f[:, 32, 34:66], ALU.subtract))
            vec.tensor_scalar(h[:, 32, 1:32], a1[:, 0:31], R2, None, ALU.mult)
            vec.tensor_scalar(h[:, 65, 1:32], a2[:, 0:31], R2, None, ALU.mult)
            vec.tensor_copy(h[:, 32, 0:1], f[:, 32, 0:1])
            vec.tensor_copy(h[:, 32, 32:33], a1[:, 31:32])
            hv = m.hg.rearrange("p (x b y) -> p x b y", x=FQ, b=2)
            vec.memset(hv[:, 0:9, :, 0:9], 0.0)
            vec.memset(hv[:, K33:K33 + 9, :, 0:9], 0.0)
            vec.tensor_tensor(a3[:, 0:8], f[:, 8, 1:9], f[:, 41, 34:42], ALU.subtract)
            c.step(vec.tensor_tensor(a4[:, 0:8], f[:, 41, 1:9], f[:, 8, 34:42], ALU.add))
            vec.tensor_scalar(h[:, 8, 1:9], a3[:, 0:8], R2, None, ALU.mult)
            vec.tensor_scalar(h[:, 41, 1:9], a4[:, 0:8], R2, None, ALU.mult)
            c.step(vec.memset(h[:, :, 65:66], 0.0))
            vec.drain().then_inc(s.high, 1)
            vec.wait_ge(s.gram, 1)
            for b in range(NB):
                q = slice(NT * b, NT * b + NT)
                vec.tensor_copy(m.gram[q, :], m.ps[7][q, NT * b:NT * b + NT])

        @block.tensor
        def _(pe):
            for i, bank in enumerate(banks):
                if i == 0:
                    pe.wait_ge(s.weights, 1)
                if bank[0][4] == 'modes':
                    pe.wait_ge(s.modes, 1)
                reached(pe, s.copied, i - NBK + 1)
                for j, (src, n, _, wide, _) in enumerate(bank):
                    mm = pe.transpose(m.ps[i % NBK][0:n, j * P:j * P + wide], src, m.ident[0:wide, 0:wide])
                mm.then_inc(s.turned, 1)
            pe.wait_ge(s.high, 1)
            for r, cs in enumerate(hbanks):
                i = len(banks) + r
                reached(pe, s.copied, i - NBK + 1)
                for j, k in enumerate(cs):
                    mm = pe.transpose(m.ps[i % NBK][:, j * P:j * P + P], m.hg[:, k * P:k * P + P], m.ident)
                mm.then_inc(s.turned, 1)
            for k in range(HC):
                pe.wait_ge(s.copied, len(banks) + k // 4 + 1)
                mm = pe.matmul(m.ps[7][:, 0:P], m.gramT[:, k, :], m.gramT[:, k, :], start=(k == 0), stop=(k == HC - 1))
            mm.then_inc(s.gram, 1)

        @block.scalar
        def _(act):
            for i, bank in enumerate(banks):
                act.wait_ge(s.turned, i + 1)
                for j, (_, n, dst, wide, _) in enumerate(bank):
                    ins = act.copy(dst, m.ps[i % NBK][0:n, j * P:j * P + wide])
                ins.then_inc(s.copied, 1)
            for r, cs in enumerate(hbanks):
                i = len(banks) + r
                act.wait_ge(s.turned, i + 1)
                act.copy(m.gramT[:, cs[0]:cs[-1] + 1, :].rearrange("p c t -> p (c t)"),
                         m.ps[i % NBK][:, 0:P * len(cs)]).then_inc(s.copied, 1)


def stage_weights(nc, held, m):
    s = semaphores(nc, held, "weights", "v")
    w = weight_views(m)

    with nc.Block() as block:
        @block.vector
        def _(vec):
            c = Chain(vec, s.v)
            sk = m.skips
            n5 = len(MT)
            c.step(vec.tensor_tensor(w.sum, m.wT[:, :, 0, 0:48], over(sk[:, 0:48], 1, n5), ALU.add))
            qr, kr, vr = w.sum[:, :, 0:16], w.sum[:, :, 16:32], w.sum[:, :, 32:48]
            qi, ki, vi, pi = (m.wT[:, :, 1, 16 * i:16 * i + 16] for i in range(4))
            v0, pr = m.wT[:, :, 0, 32:48], m.wT[:, :, 0, 48:64]
            low = over(m.low, 2, HEADS)
            vec.tensor_tensor(w.t1, qr, kr, ALU.mult)
            vec.tensor_tensor(w.t2, qi, ki, ALU.mult)
            vec.tensor_tensor(w.t3, qi, kr, ALU.mult)
            c.step(vec.tensor_tensor(w.t4, qr, ki, ALU.mult))
            vec.tensor_tensor(w.t1, w.t1, w.t2, ALU.add)
            c.step(vec.tensor_tensor(w.t3, w.t3, w.t4, ALU.subtract))
            vec.tensor_tensor(w.ar, w.t1, low, ALU.mult)
            c.step(vec.tensor_tensor(w.ai, w.t3, low, ALU.mult))
            c.step(vec.tensor_scalar(w.an, w.ai, -1.0, None, ALU.mult))
            pw = over(sk[:, 48:64], 1, n5)
            vec.tensor_tensor(w.t1, v0, pw, ALU.mult)
            vec.tensor_tensor(w.t2, pr, vr, ALU.mult)
            vec.tensor_tensor(w.t3, pi, vi, ALU.mult)
            c.step(vec.tensor_tensor(w.t4, pr, pw, ALU.add))
            vec.tensor_tensor(w.t1, w.t1, w.t2, ALU.add)
            c.step(vec.tensor_tensor(w.t4, w.t4, vi, ALU.mult))
            vec.tensor_tensor(w.ur, w.t1, w.t3, ALU.subtract)
            c.step(vec.tensor_tensor(w.t2, pi, vr, ALU.mult))
            c.step(vec.tensor_tensor(w.ui, w.t4, w.t2, ALU.add))
            c.step(vec.tensor_tensor(w.t1[:, 0, :], pr[:, 0, :], sk[:, 48:64], ALU.add))
            c.step(vec.tensor_tensor(w.t1[:, 0, :], w.t1[:, 0, :], m.biases[:, 32:48], ALU.mult))
            c.step(vec.tensor_reduce(m.col[:, 8:9], w.t1[:, 0, :], AX.X, ALU.add))
            c.step(vec.tensor_tensor(m.col[:, 8:9], m.col[:, 8:9], m.sc[:, 16:17], ALU.add))
            c.step(vec.tensor_tensor(w.cg, sk[:, 0:16], sk[:, 16:32], ALU.mult))
            vec.tensor_scalar(w.cg, w.cg, 64.0, None, ALU.mult)
            c.step(vec.tensor_tensor(w.cm, sk[:, 32:48], sk[:, 48:64], ALU.mult))
            aq, ak = w.sum[0:1, 0, 0:16], w.sum[0:1, 0, 16:32]
            bq, bk = m.biases[0:1, 0:16], m.biases[0:1, 16:32]
            c.step(vec.scalar_tensor_tensor(out=w.r1[0:1], in0=aq, scalar=64.0, in1=bk, op0=ALU.mult, op1=ALU.mult))
            c.step(vec.scalar_tensor_tensor(out=w.r2[0:1], in0=ak, scalar=64.0, in1=bq, op0=ALU.mult, op1=ALU.mult))
            c.step(vec.scalar_tensor_tensor(out=w.r3[0:1], in0=bq, scalar=64.0, in1=bk, op0=ALU.mult, op1=ALU.mult))
            vec.tensor_copy(m.dcq, over(w.r1[0:1], 2, NT))
            c.step(vec.tensor_tensor(m.dck, over(m.modesT[0:1, 0, 0, :], 1, HEADS), over(w.r2[0:1], 2, P), ALU.mult))
            c.step(vec.tensor_tensor(m.dck, m.dck, over(w.r3[0:1], 2, P), ALU.add))
            c.step(vec.memset(w.one[0:1], 1.0))


def weight_views(m):
    w = Views()
    w.sum = m.wk[:, 0:240].rearrange("p (k h) -> p k h", k=5)
    big = [m.wk[:, 240 + 80 * i:320 + 80 * i].rearrange("p (k h) -> p k h", k=5) for i in range(9)]
    w.ar, w.ai, w.an, w.ur, w.ui, w.t1, w.t2, w.t3, w.t4 = big
    w.cg, w.cm = m.wk[:, 960:976], m.wk[:, 976:992]
    w.r1, w.mix = m.wk[:, 640:656], m.wk[:, 656:688]
    w.r2, w.r3, w.one = m.wk[:, 720:736], m.wk[:, 800:816], m.wk[:, 880:912]
    return w


def stage_scores(nc, held, m):
    s = semaphores(nc, held, "scores", "v a p0 p1 p2 p3 used done sub exp cleared probs turned copied mixed mixc")
    w = weight_views(m)
    ready = [s.p0, s.p1, s.p2, s.p3]
    left = [(w.ar, 0), (w.ai, 1), (w.ar, 1), (w.an, 0)]

    with nc.Block() as block:
        def operands(k, j):
            a, part = left[j]
            return over(m.modesT[:, k, part, :], 1, HEADS), over(a[:, k, :], 2, P)

        @block.vector
        def _(vec):
            c = Chain(vec, s.v)
            for k in range(LOWT):
                for j in (0, 1):
                    if k:
                        vec.wait_ge(s.used, 4 * (k - 1) + j + 1)
                    x, a = operands(k, j)
                    vec.tensor_tensor(m.prod[:, j], x, a, ALU.mult).then_inc(ready[j], 1)
            sh = [HEADS, NT]
            gram = over(m.gram, 1, HEADS)
            c.step(vec.tensor_tensor(m.score, gram, over(w.cg, 2, NT), ALU.mult))
            vec.wait_ge(s.done, 1)
            c.step(vec.tensor_tensor(m.score, m.ps[0][:, :].rearrange("p (h s) -> p h s", h=HEADS), m.score, ALU.add))
            c.step(vec.tensor_reduce(w.r1, m.score, AX.X, ALU.max))
            vec.tensor_tensor(m.score, m.score, over(w.r1, 2, NT), ALU.subtract).then_inc(s.sub, 1)
            vec.wait_ge(s.exp, 1)
            c.step(vec.tensor_reduce(w.r1, m.expo, AX.X, ALU.add))
            c.step(vec.reciprocal(w.r1, w.r1))
            c.step(vec.tensor_tensor(m.prob, m.expo, over(w.r1, 2, NT), ALU.mult))
            vec.wait_ge(s.cleared, 2)
            for b in range(NB):
                q = slice(NT * b, NT * b + NT)
                ins = vec.tensor_copy(m.probD[q, :, NT * b:NT * b + NT], m.prob[q])
            ins.then_inc(s.probs, 1)
            c.step(vec.tensor_tensor(m.score, m.prob, over(w.cm, 2, NT), ALU.mult))
            c.step(vec.tensor_reduce(w.mix, m.score.rearrange("p h s -> p s h"), AX.X, ALU.add))
            for b in range(NB):
                q = slice(NT * b, NT * b + NT)
                ins = vec.tensor_copy(m.mixD[q, NT * b:NT * b + NT], w.mix[q])
            ins.then_inc(s.probs, 1)
            vec.wait_ge(s.mixed, 1)
            c.step(vec.tensor_copy(m.mixT, m.ps[5][:, 0:P]))
            vec.scalar_tensor_tensor(out=m.mixA, in0=m.ps[5][:, 0:P], scalar=m.col[:, 0:1], in1=m.ident,
                                     op0=ALU.mult, op1=ALU.add).then_inc(s.mixc, 1)
            vec.wait_ge(s.mixed, 2)
            c.step(vec.tensor_copy(m.col[:, 9:10], m.ps[6][:, 0:1]))

        @block.gpsimd
        def _(pool):
            for k in range(LOWT):
                if k:
                    pool.wait_ge(s.used, 4 * (k - 1) + 3)
                x, a = operands(k, 2)
                pool.tensor_tensor(m.prod[:, 2], x, a, ALU.mult).then_inc(ready[2], 1)
            pool.wait_ge(s.done, 1)
            pool.memset(m.probD, 0.0).then_inc(s.cleared, 1)
            pool.memset(m.mixD, 0.0).then_inc(s.cleared, 1)

        @block.scalar
        def _(act):
            for k in range(LOWT):
                if k:
                    act.wait_ge(s.used, 4 * (k - 1) + 4)
                a, part = left[3]
                for h in range(HEADS):
                    ins = act.activation(m.prod[:, 3, h, :], m.modesT[:, k, part, :], ACT.Copy, scale=a[:, k, h:h + 1])
                ins.then_inc(ready[3], 1)
            act.wait_ge(s.sub, 1)
            act.activation(m.expo, m.score, ACT.Exp).then_inc(s.exp, 1)
            for i in range(4):
                act.wait_ge(s.turned, i + 1)
                act.copy(m.probT[:, 4 * i:4 * i + 4, :].rearrange("p h t -> p (h t)"), m.ps[1 + i][:, :])\
                    .then_inc(s.copied, 1)

        @block.tensor
        def _(pe):
            for k in range(LOWT):
                for j in range(4):
                    pe.wait_ge(ready[j], k + 1)
                    for b in range(NB):
                        q = slice(NT * b, NT * b + NT)
                        mm = pe.matmul(m.ps[0][q, :], m.modesT[:, k, j // 2, q], m.prod[:, j, :, q],
                                       start=(k == 0 and j == 0), stop=False)
                    mm.then_inc(s.used, 1)
            for b in range(NB):
                q = slice(NT * b, NT * b + NT)
                pe.matmul(m.ps[0][q, :], m.modesT[0:1, 0, 0, q], m.dcq, start=False, stop=False)
                mm = pe.matmul(m.ps[0][q, :], w.one[0:1], m.dck[:, :, q], start=False, stop=True)
            mm.then_inc(s.done, 1)
            pe.wait_ge(s.probs, 1)
            for h in range(HEADS):
                mm = pe.transpose(m.ps[1 + h // 4][:, (h % 4) * P:(h % 4) * P + P], m.probD[:, h, :], m.ident)
                if h % 4 == 3:
                    mm.then_inc(s.turned, 1)
            pe.wait_ge(s.probs, 2)
            pe.transpose(m.ps[5][:, 0:P], m.mixD, m.ident).then_inc(s.mixed, 1)
            pe.wait_ge(s.mixc, 1)
            pe.matmul(m.ps[6][:, 0:1], m.mixT, m.col[:, 1:2], start=True, stop=True).then_inc(s.mixed, 1)


def stage_mix(nc, held, m, mix):
    s = semaphores(nc, held, "mix", "v mixed added stored xm used summed free reduced dc turned copied coef")
    w = weight_views(m)
    NCH = PIX // 512
    steps = [(k, q) for k in range(len(MT)) for q in range(4)]
    a = m.a[:, :, :].rearrange("p a b -> p (a b)")

    with nc.Block() as block:
        @block.tensor
        def _(pe):
            def body(it):
                for u in range(4):
                    i = it * 4 + u
                    reached(pe, s.added, i - 3)
                    pe.matmul(m.ps[u][:, :], m.mixA, a[:, bass.ds(i * 512, 512)], start=True, stop=True)\
                        .then_inc(s.mixed, 1)
            body(0)
            with pe.Fori(1, NCH // 4) as it:
                body(it)
            for i, (k, q) in enumerate(steps):
                m0, n = MT[k]
                if i < 2:
                    pe.wait_ge(s.added, NCH)
                reached(pe, s.used, i - 2)
                for part in (0, 1):
                    mm = pe.matmul(m.ps[2 * (i % 3) + part][0:n, :], m.modes[:, part, m0:m0 + n],
                                   m.probT[:, 4 * q:4 * q + 4, :], start=True, stop=True)
                mm.then_inc(s.xm, 1)
            for k, (m0, n) in enumerate(MT):
                pe.wait_ge(s.reduced, k + 1)
                if k == 0:
                    pe.wait_ge(s.dc, 1)
                    pe.wait_ge(s.used, len(steps))
                reached(pe, s.copied, k - 2)
                for part in (0, 1):
                    mm = pe.transpose(m.ps[k % 3][:, part * P:part * P + n], m.modesT[0:n, k, part, :], m.ident[0:n, 0:n])
                mm.then_inc(s.turned, 1)
            turn_coefficients(pe, m, s, len(MT))

        @block.scalar
        def _(act):
            for k, (m0, n) in enumerate(MT):
                act.wait_ge(s.turned, k + 1)
                src = m.ps[k % 3][:, 0:2 * P].rearrange("p (c n) -> p c n", c=2)[:, :, 0:n]
                act.copy(m.modes[:, :, m0:m0 + n], src).then_inc(s.copied, 1)
            copy_coefficients(act, m, s, len(MT))

        @block.sync
        def _(sp):
            sp.wait_ge(s.added, NCH)
            for q in range(4):
                sp.dma_start(mix[:, 32 * q:32 * q + 32, :], m.a[:, 32 * q:32 * q + 32, :]).then_inc(s.stored, 16)
            sp.wait_ge(s.stored, 64)

        @block.vector
        def _(vec):
            c = Chain(vec, s.v)
            with vec.Fori(0, NCH // 4) as it:
                for u in range(4):
                    i = it * 4 + u
                    vec.wait_ge(s.mixed, i + 1)
                    vec.tensor_scalar(a[:, bass.ds(i * 512, 512)], m.ps[u][:, :], m.col[:, 9:10], None, ALU.add)\
                        .then_inc(s.added, 1)
            for i, (k, q) in enumerate(steps):
                n = MT[k][1]
                vec.wait_ge(s.xm, i + 1)
                reached(vec, s.summed, i - 1)
                for j, (part, u) in enumerate([(0, w.ur), (1, w.ui), (0, w.ui), (1, w.ur)]):
                    src = m.ps[2 * (i % 3) + part][0:n, :].rearrange("p (h t) -> p h t", h=4)
                    ins = vec.tensor_tensor(m.zprod[0:n, i % 2, j], src, over(u[0:n, k, 4 * q:4 * q + 4], 2, P), ALU.mult)
                ins.then_inc(s.used, 1)
                if q == 3:
                    vec.wait_ge(s.summed, i + 1)
                    for part in (0, 1):
                        ins = vec.tensor_reduce(m.modesT[0:n, k, part, :], m.zsum[0:n, part].rearrange("p h t -> p t h"),
                                                AX.X, ALU.add)
                    ins.then_inc(s.reduced, 1)
            vec.wait_ge(s.reduced, len(MT))
            vec.tensor_scalar(m.modesT[0:1, 0, 0, :], m.modesT[0:1, 0, 0, :], m.col[0:1, 8:9], None, ALU.add)\
                .then_inc(s.dc, 1)
            vec.wait_ge(s.copied, len(MT))
            form_coefficients(vec, m, m.modes[:, 0], m.modes[:, 1])
            vec.drain().then_inc(s.coef, 1)

        @block.gpsimd
        def _(pool):
            for i, (k, q) in enumerate(steps):
                n = MT[k][1]
                pool.wait_ge(s.used, i + 1)
                if q == 0:
                    reached(pool, s.reduced, k)
                pool.tensor_tensor(m.zsum[0:n, 0, 4 * q:4 * q + 4], m.zprod[0:n, i % 2, 0], m.zprod[0:n, i % 2, 1], ALU.subtract)
                pool.tensor_tensor(m.zsum[0:n, 1, 4 * q:4 * q + 4], m.zprod[0:n, i % 2, 2], m.zprod[0:n, i % 2, 3], ALU.add)\
                    .then_inc(s.summed, 1)


def form_coefficients(vec, m, re, im):
    g = m.coef.rearrange("p (a x) (b y) -> p a x b y", a=2, b=2)
    re, im = (v.rearrange("p (r k) -> p r k", r=ROWS) for v in (re, im))
    rp, rn, ip, im_ = re[:, 0:K17], re[:, K17:ROWS], im[:, 0:K17], im[:, K17:ROWS]
    vec.tensor_tensor(g[:, 0, :, 0], rp, rn, ALU.add)
    vec.tensor_tensor(g[:, 1, :, 1], rn, rp, ALU.subtract)
    vec.tensor_tensor(g[:, 1, :, 0], im_, ip, ALU.subtract)
    return vec.scalar_tensor_tensor(out=g[:, 0, :, 1], in0=ip, scalar=-1.0, in1=im_, op0=ALU.mult, op1=ALU.subtract)


COEF_BANKS = [list(range(i, min(FM, i + 4))) for i in range(0, FM, 4)]


def turn_coefficients(pe, m, s, base):
    pe.wait_ge(s.coef, 1)
    for r, xs in enumerate(COEF_BANKS):
        if r > 2:
            pe.wait_ge(s.copied, base + r - 2)
        for j, xf in enumerate(xs):
            mm = pe.transpose(m.ps[3 + r % 3][0:FM, j * P:j * P + P], m.coef[:, xf, :], m.ident)
        mm.then_inc(s.turned, 1)


def copy_coefficients(act, m, s, base):
    for r, xs in enumerate(COEF_BANKS):
        act.wait_ge(s.turned, base + r + 1)
        act.copy(m.coefT[:, xs[0]:xs[-1] + 1, :].rearrange("p x t -> p (x t)"),
                 m.ps[3 + r % 3][0:FM, 0:P * len(xs)]).then_inc(s.copied, 1)


def sweep(eng, step, lag):
    for u in range(UN):
        step(u, u)
    with eng.Fori(1, NG // UN) as it:
        for u in range(UN):
            step(it * UN + u, u)
    for u in range(lag):
        step(NG + u, u)


def live(g):
    return not isinstance(g, int) or 0 <= g < NG


def group(images, g):
    return images[:, bass.ds(g * GRP, GRP), :]


def banked(m, bank):
    return m.ps[bank][:, :].rearrange("p (t w) -> p t w", t=GRP)


def stage_inverse(nc, held, m, kind, mix=None, ins=None):
    s = semaphores(nc, held, "inverse_" + kind, "in0 in1 in2 in3 staged cols colsc rows used stats "
                   "lin pre ready saved first copied weights")
    arrived = [s.in0, s.in1, s.in2, s.in3]
    dest = m.a if kind == 'mix2' else m.b

    with nc.Block() as block:
        @block.sync
        def _(sp):
            if kind == 'proj':
                mix_img = mix.rearrange("t h w -> h t w")

                def load(t, u):
                    reached(sp, s.used, t - UN + 1)
                    sp.dma_start(group(m.b, t), mix_img[:, bass.ds(t * GRP, GRP), :]).then_inc(arrived[u], 16)
                sweep(sp, load, 0)
            if kind == 'mix1':
                load_mixer(sp, m, ins, 2, s.weights)
                sp.wait_ge(s.weights, 32)

        @block.gpsimd
        def _(pool):
            pool.memset(m.stage[:, :, GRP * FM:], 0.0)

            def step(t, u):
                if live(t):
                    reached(pool, s.cols, t - 1)
                    pool.tensor_copy(m.stage[0:FM, u % 2, 0:GRP * FM].rearrange("p (t x) -> p t x", t=GRP),
                                     m.coefT[:, :, bass.ds(t * GRP, GRP)].rearrange("p x t -> p t x"))\
                        .then_inc(s.staged, 1)
                g = t - 2
                if kind == 'mix1' and live(g):
                    pool.wait_ge(s.ready, g + 1)
                    pool.tensor_copy(group(m.a, g), m.ust[:, u % 2]).then_inc(s.saved, 1)
            sweep(pool, step, 2 if kind == 'mix1' else 0)

        @block.tensor
        def _(pe):
            def step(t, u):
                if live(t):
                    pe.wait_ge(s.staged, t + 1)
                    reached(pe, s.colsc, t - 1)
                    for j in range(GRP):
                        mm = pe.matmul(m.ps[u % 2][:, j * NW:j * NW + NW],
                                       m.stage[0:FM, u % 2, j * FM:j * FM + P], m.cols, start=True, stop=True)
                    mm.then_inc(s.cols, 1)
                g = t - 1
                if live(g):
                    pe.wait_ge(s.colsc, g + 1)
                    reached(pe, s.pre if kind == 'mix1' else s.used, g - 1)
                    pe.matmul(m.ps[2 + (u - 1) % 2][:, :], m.rows, m.half[0:FM, (u - 1) % 2, :], start=True, stop=True)\
                        .then_inc(s.rows, 1)
                g = t - 3
                if kind == 'mix1' and live(g):
                    pe.wait_ge(s.ready, g + 1)
                    reached(pe, s.copied, g - 1)
                    for j in range(GRP):
                        mm = pe.matmul(m.ps[4 + (u - 3) % 2][:, j * FM:j * FM + FM], m.ust[:, (u - 3) % 2, j, :],
                                       m.dft17, start=True, stop=True)
                    mm.then_inc(s.first, 1)
            sweep(pe, step, 3 if kind == 'mix1' else 1)

        @block.scalar
        def _(act):
            def step(t, u):
                if live(t):
                    act.wait_ge(s.cols, t + 1)
                    reached(act, s.rows, t - 1)
                    act.copy(m.half[0:FM, u % 2, :], m.ps[u % 2][0:FM, :]).then_inc(s.colsc, 1)
                g = t - 2
                if kind == 'mix1' and live(g):
                    act.wait_ge(s.pre, g + 1)
                    reached(act, s.first, g - 1)
                    reached(act, s.saved, g - 1)
                    act.activation(m.ust[:, u % 2], m.tmp[:, u % 2], ACT.Gelu).then_inc(s.ready, 1)
                g = t - 3
                if kind == 'mix1' and live(g):
                    act.wait_ge(s.first, g + 1)
                    act.copy(m.half17[:, bass.ds(g * GRP, GRP), :],
                             m.ps[4 + (u - 3) % 2][:, 0:GRP * FM].rearrange("p (t x) -> p t x", t=GRP))\
                        .then_inc(s.copied, 1)
            sweep(act, step, 3 if kind == 'mix1' else 0)

        @block.vector
        def _(vec):
            def step(t, u, it):
                if kind == 'mix1' and live(t):
                    reached(vec, s.ready, t - 1)
                    for j in range(GRP):
                        img = t * GRP + j
                        e = vec.tensor_scalar(m.tmp[:, u % 2, j, :], m.b[:, bass.ds(img, 1), :],
                                              m.aff[:, 4, bass.ds(img, 1)], m.aff[:, 5, bass.ds(img, 1)],
                                              ALU.mult, ALU.add)
                    e.then_inc(s.lin, 1)
                g = t - 1
                if live(g):
                    if kind != 'mix1':
                        reached(vec, s.used, g)
                    vec.wait_ge(s.rows, g + 1)
                    y = banked(m, 2 + (u - 1) % 2)
                    if kind == 'proj':
                        vec.wait_ge(arrived[(u - 1) % UN], (it + (1 if u else 0)) * 16)
                        vec.tensor_tensor(group(m.b, g), group(m.b, g), y, ALU.add).then_inc(s.used, 1)
                    elif kind == 'mix1':
                        vec.wait_ge(s.lin, g + 1)
                        vec.tensor_tensor(m.tmp[:, (u - 1) % 2], m.tmp[:, (u - 1) % 2], y, ALU.add).then_inc(s.pre, 1)
                    else:
                        vec.scalar_tensor_tensor(out=group(m.a, g), in0=group(m.a, g), scalar=m.sc[:, 10:11], in1=y,
                                                 op0=ALU.mult, op1=ALU.add).then_inc(s.used, 1)
                g = t - 2
                if kind != 'mix1' and live(g):
                    if isinstance(g, int) and g == NG - 1:
                        vec.wait_ge(s.used, NG)
                    for j in range(GRP):
                        img = g * GRP + j
                        vec.bn_stats(m.stat[:, bass.ds(img, 1), :], dest[:, bass.ds(img, 1), :])

            for u in range(UN):
                step(u, u, 0)
            with vec.Fori(1, NG // UN) as it:
                for u in range(UN):
                    step(it * UN + u, u, it)
            for u in range(2):
                step(NG + u, u, NG // UN)


def stage_factors(nc, held, m, kind):
    s = semaphores(nc, held, "factors_" + kind, "v ones sums summed added rooted")
    half = m.spare[:, 128:2176]
    ones, total, mean, var = m.spare[:, 0:P], half[:, 0:128], half[:, 128:256], half[:, 256:384]
    root, root2, t = half[:, 384:512], half[:, 512:640], half[:, 640:768]
    dev = half[:, 768:1024].rearrange("p (t k) -> p t k", k=2)
    sc1, bi1, sc2, bi2, sa, sb = (m.aff[:, i, :] for i in range(6))

    def scalar(i):
        return m.sc[:, i:i + 1]

    with nc.Block() as block:
        @block.tensor
        def _(pe):
            pe.wait_ge(s.ones, 1)
            for i, src in enumerate([total, t]):
                pe.wait_ge(s.sums, i + 1)
                pe.matmul(m.ps[i][:, 0:P], ones, src, start=True, stop=True).then_inc(s.summed, 1)

        @block.scalar
        def _(act):
            for i, (dst, src) in enumerate([(root, var), (root2, t)][:2 if kind == 'proj' else 1]):
                act.wait_ge(s.added, i + 1)
                act.activation(dst, src if i else root, ACT.Sqrt).then_inc(s.rooted, 1)

        @block.vector
        def _(vec):
            c = Chain(vec, s.v)
            vec.memset(ones, 1.0).then_inc(s.ones, 1)
            vec.tensor_tensor(total, m.stat[:, :, 1], m.stat[:, :, 4], ALU.add).then_inc(s.sums, 1)
            vec.wait_ge(s.summed, 1)
            c.step(vec.tensor_scalar(mean, m.ps[0][:, 0:P], 1.0 / (2 * P), None, ALU.mult))
            c.step(vec.tensor_tensor(dev, m.stat[:, :, 1::3], over(mean, 2, 2), ALU.subtract))
            c.step(vec.tensor_tensor(dev, dev, dev, ALU.mult))
            c.step(vec.tensor_tensor(t, dev[:, :, 0], dev[:, :, 1], ALU.add))
            c.step(vec.tensor_tensor(var, m.stat[:, :, 2], m.stat[:, :, 5], ALU.add))
            vec.scalar_tensor_tensor(out=t, in0=t, scalar=float(NW // 2), in1=var, op0=ALU.mult, op1=ALU.add)\
                .then_inc(s.sums, 1)
            vec.wait_ge(s.summed, 2)
            c.step(vec.tensor_scalar(var, m.ps[1][:, 0:P], 1.0 / PIX, None, ALU.mult))
            vec.tensor_scalar(root, var, EPS, None, ALU.add).then_inc(s.added, 1)
            vec.wait_ge(s.rooted, 1)
            g, b = (2, 3) if kind == 'proj' else (14, 15)
            c.step(vec.reciprocal(root, root))
            c.step(vec.tensor_scalar(sc1, root, scalar(g), None, ALU.mult))
            c.step(vec.tensor_tensor(t, mean, sc1, ALU.mult))
            c.step(vec.tensor_scalar(bi1, t, -1.0, scalar(b), ALU.mult, ALU.add))
            if kind == 'proj':
                c.step(vec.tensor_tensor(t, sc1, sc1, ALU.mult))
                c.step(vec.tensor_tensor(t, t, var, ALU.mult))
                vec.tensor_scalar(t, t, EPS, None, ALU.add).then_inc(s.added, 1)
                vec.wait_ge(s.rooted, 2)
                c.step(vec.reciprocal(root2, root2))
                c.step(vec.tensor_scalar(sc2, root2, scalar(4), None, ALU.mult))
                c.step(vec.tensor_scalar(t, sc2, scalar(3), None, ALU.mult))
                c.step(vec.tensor_scalar(bi2, t, -1.0, scalar(5), ALU.mult, ALU.add))
                vec.tensor_scalar(sa, sc2, scalar(6), None, ALU.mult)
                vec.tensor_scalar(sb, bi2, scalar(6), None, ALU.mult)


def stage_attended(nc, held, m):
    s = semaphores(nc, held, "attended", "normed staged first copied")

    with nc.Block() as block:
        @block.vector
        def _(vec):
            def step(t, u):
                if live(t):
                    for j in range(GRP):
                        img = bass.ds(t * GRP + j, 1)
                        e = vec.tensor_scalar(m.b[:, img, :], m.b[:, img, :], m.aff[:, 0, img], m.aff[:, 1, img],
                                              ALU.mult, ALU.add)
                    e.then_inc(s.normed, 1)
                g = t - 2
                if live(g):
                    vec.wait_ge(s.first, g + 1)
                    vec.tensor_copy(m.half17[:, bass.ds(g * GRP, GRP), :],
                                    m.ps[u % 2][:, 0:GRP * FM].rearrange("p (t x) -> p t x", t=GRP))\
                        .then_inc(s.copied, 1)
            sweep(vec, step, 2)

        @block.scalar
        def _(act):
            def step(t, u):
                act.wait_ge(s.normed, t + 1)
                reached(act, s.first, t - 1)
                for j in range(GRP):
                    img = bass.ds(t * GRP + j, 1)
                    e = act.activation(m.ust[:, u % 2, j, :], m.b[:, img, :].rearrange("p a w -> p (a w)"), ACT.Identity,
                                       scale=m.aff[:, 2, img], bias=m.aff[:, 3, img])
                e.then_inc(s.staged, 1)
            sweep(act, step, 0)

        @block.tensor
        def _(pe):
            def step(t, u):
                pe.wait_ge(s.staged, t + 1)
                reached(pe, s.copied, t - 1)
                for j in range(GRP):
                    mm = pe.matmul(m.ps[u % 2][:, j * FM:j * FM + FM], m.ust[:, u % 2, j, :], m.dft17,
                                   start=True, stop=True)
                mm.then_inc(s.first, 1)
            sweep(pe, step, 0)


def stage_mixer(nc, held, m, i):
    s = semaphores(nc, held, f"mixer{i}", "v second added rooted coef turned copied")
    rounds = [(0, 12), (12, 24), (24, 34)]
    zr, zi, t1, t2 = (m.spare[:, NM * k:NM * k + NM] for k in range(4))
    wide = m.spare[:, 4 * NM:4 * NM + FM * FM]
    prod = m.spare[:, 0:FM * FM]
    k0 = 6 if i == 1 else 10
    var, root, fac, con = (m.col[:, 16 + j:17 + j] for j in range(4))

    with nc.Block() as block:
        @block.tensor
        def _(pe):
            for r, (lo, hi) in enumerate(rounds):
                for xf in range(lo, hi):
                    mm = pe.matmul(m.ps[r][:, (xf - lo) * FM:(xf - lo) * FM + FM], m.half17[:, :, xf], m.dft17,
                                   start=True, stop=True)
                mm.then_inc(s.second, 1)
            turn_coefficients(pe, m, s, 0)

        @block.scalar
        def _(act):
            act.wait_ge(s.added, 1)
            act.activation(root, var, ACT.Sqrt).then_inc(s.rooted, 1)
            copy_coefficients(act, m, s, 0)

        @block.vector
        def _(vec):
            c = Chain(vec, s.v)
            for r, (lo, hi) in enumerate(rounds):
                vec.wait_ge(s.second, r + 1)
                e = vec.tensor_copy(m.feat[:, lo:hi, :].rearrange("p x y -> p (x y)"), m.ps[r][:, 0:(hi - lo) * FM])
                if r == 2:
                    c.step(e)
            form_modes(vec, c, m.feat, m.modes, K17)
            wr, wi = (m.mixw[:, :, :, k].rearrange("p r k -> p (r k)") for k in (0, 1))
            xr, xi = m.modes[:, 0], m.modes[:, 1]
            vec.tensor_tensor(zr, xr, wr, ALU.mult)
            vec.tensor_tensor(t1, xi, wi, ALU.mult)
            vec.tensor_tensor(zi, xr, wi, ALU.mult)
            c.step(vec.tensor_tensor(t2, xi, wr, ALU.mult))
            vec.tensor_tensor(zr, zr, t1, ALU.subtract)
            c.step(vec.tensor_tensor(zi, zi, t2, ALU.add))
            c.step(form_coefficients(vec, m, zr, zi))
            g = m.coef.rearrange("p x y -> p (x y)")
            c.step(vec.tensor_tensor(wide, g, m.var, ALU.mult))
            c.step(vec.tensor_tensor_reduce(prod, wide, g, 1.0, 0.0, ALU.mult, ALU.add, var))
            vec.tensor_scalar(var, var, EPS, None, ALU.add).then_inc(s.added, 1)
            vec.wait_ge(s.rooted, 1)
            c.step(vec.reciprocal(root, root))
            c.step(vec.tensor_tensor(fac, root, m.sc[:, k0 + 2:k0 + 3], ALU.mult))
            c.step(vec.tensor_tensor(con, m.sc[:, k0 + 1:k0 + 2], m.sc[:, k0 + 3:k0 + 4], ALU.add))
            c.step(vec.tensor_scalar(g, g, fac, None, ALU.mult))
            vec.tensor_copy(g[:, 0:1], con).then_inc(s.coef, 1)


def stage_residual(nc, held, m, ins):
    s = semaphores(nc, held, "residual", "in0 in1 in2 in3 normed partly whole")
    arrived = [s.in0, s.in1, s.in2, s.in3]
    x_img = ins['x'].rearrange("b t h w -> h (b t) w")
    load = m.spare[:, 0:4 * 512].rearrange("p (s t w) -> p s t w", s=4, t=GRP)

    with nc.Block() as block:
        @block.sync
        def _(sp):
            def body(it):
                for u in range(UN):
                    g = it * UN + u
                    reached(sp, s.whole, g - UN + 1)
                    sp.dma_start(load[:, u], x_img[:, bass.ds(g * GRP, GRP), :]).then_inc(arrived[u], 16)
            body(0)
            with sp.Fori(1, NG // UN) as it:
                body(it)

        @block.scalar
        def _(act):
            def step(t, u):
                for j in range(GRP):
                    img = bass.ds(t * GRP + j, 1)
                    a = m.a[:, img, :].rearrange("p a w -> p (a w)")
                    e = act.activation(a, a, ACT.Identity, scale=m.aff[:, 0, img], bias=m.aff[:, 1, img])
                e.then_inc(s.normed, 1)
            sweep(act, step, 0)

        @block.gpsimd
        def _(pool):
            def body(it):
                for u in range(UN):
                    g = it * UN + u
                    pool.wait_ge(arrived[u], (it + 1) * 16)
                    pool.tensor_tensor(group(m.b, g), group(m.b, g), load[:, u], ALU.add).then_inc(s.partly, 1)
            with pool.Fori(0, NG // UN) as it:
                body(it)

        @block.vector
        def _(vec):
            def step(t, u):
                if live(t):
                    reached(vec, s.whole, t)
                    vec.wait_ge(s.normed, t + 1)
                    vec.wait_ge(s.partly, t + 1)
                    vec.tensor_tensor(group(m.b, t), group(m.b, t), group(m.a, t), ALU.add).then_inc(s.whole, 1)
                g = t - 1
                if live(g):
                    if isinstance(g, int) and g == NG - 1:
                        vec.wait_ge(s.whole, NG)
                    for j in range(GRP):
                        img = bass.ds(g * GRP + j, 1)
                        vec.bn_stats(m.stat[:, img, :], m.b[:, img, :])
            sweep(vec, step, 1)



def row_factors(vec, c, st, fac, factor, rooted):
    mean, dev, t, q = (fac[:, i, :] for i in range(4))
    vec.tensor_tensor(t, st[:, :, 1], st[:, :, 4], ALU.add)
    c.step(vec.tensor_tensor(dev, st[:, :, 1], st[:, :, 4], ALU.subtract))
    vec.tensor_scalar(mean, t, 0.5, None, ALU.mult)
    c.step(vec.tensor_scalar(dev, dev, 0.5, None, ALU.mult))
    c.step(vec.tensor_tensor(dev, dev, dev, ALU.mult))
    c.step(vec.tensor_tensor(q, st[:, :, 2], st[:, :, 5], ALU.add))
    c.step(vec.scalar_tensor_tensor(out=dev, in0=q, scalar=1.0 / D, in1=dev, op0=ALU.mult, op1=ALU.add))
    vec.tensor_scalar(dev, dev, EPS, None, ALU.add).then_inc(factor, 1)
    vec.wait_ge(rooted, 1)
    c.step(vec.reciprocal(dev, dev))


def stage_normed(nc, held, m, ins):
    s = semaphores(nc, held, "normed", "v loaded turned mapsc maps done rooted factor staged turnedr copied scaled units")
    names = ['L1_attn_rotation_params', 'L1_attn_entangle_params', 'L1_attn_Wq', 'L1_attn_Wk', 'L1_attn_Wv']
    raw = m.scratch[:, 0:640].rearrange("p (k d) -> p k d", k=5)
    rawT = m.scratch[:, 640:1280].rearrange("p (k d) -> p k d", k=5)
    fac = m.scratch[:, 1280:1280 + 4 * NI].rearrange("p (k t) -> p k t", k=4)
    ln = m.scratch[:, 1792:2816].rearrange("p (s t w) -> p s t w", s=2, t=GRP)
    diag, unit = m.scratch[:, 2816:2944], m.scratch[:, 2944:2948]

    with nc.Block() as block:
        @block.sync
        def _(sp):
            for i, n in enumerate(names):
                src = ins[n]
                if len(src.shape) == 1:
                    src = src.rearrange("(d e) -> d e", d=D)
                sp.dma_start(raw[:, i, :], src).then_inc(s.loaded, 16)

        @block.tensor
        def _(pe):
            pe.wait_ge(s.loaded, 80)
            pe.wait_ge(s.scaled, 1)
            pe.matmul(m.ps[7][:, 0:D], m.halves[:, :], diag, start=True, stop=True).then_inc(s.units, 1)
            for i in range(5):
                mm = pe.transpose(m.ps[4 + i // 4][:, (i % 4) * D:(i % 4) * D + D], raw[:, i, :], m.ident)
            mm.then_inc(s.turned, 1)
            pe.wait_ge(s.mapsc, 1)
            for i in (0, 1):
                mm = pe.matmul(m.ps[6][:, i * D:i * D + D], rawT[:, i, :], rawT[:, 2 + i, :], start=True, stop=True)
            mm.then_inc(s.maps, 1)

            def step(t, u):
                pe.wait_ge(s.staged, t + 1)
                reached(pe, s.copied, t - 1)
                for j in range(GRP):
                    mm = pe.transpose(m.ps[u % 2][:, j * P:j * P + P], ln[:, u % 2, j, :], m.ident)
                mm.then_inc(s.turnedr, 1)
            sweep(pe, step, 0)

        @block.scalar
        def _(act):
            act.wait_ge(s.factor, 1)
            act.activation(fac[:, 1], fac[:, 1], ACT.Sqrt).then_inc(s.rooted, 1)

            def step(t, u):
                act.wait_ge(s.turnedr, t + 1)
                act.copy(group(m.a, t), banked(m, u % 2)).then_inc(s.copied, 1)
            sweep(act, step, 0)

        @block.vector
        def _(vec):
            c = Chain(vec, s.v)
            row_factors(vec, c, m.stat, fac, s.factor, s.rooted)
            vec.memset(m.halves[:, :], 0.5)
            vec.memset(m.v[:, :, D:D + 1], 1.0)
            vec.wait_ge(s.loaded, 80)
            vec.tensor_reduce(unit[:, 0:1], raw[:, 4, :], AX.X, ALU.max)
            c.step(vec.tensor_reduce(unit[:, 1:2], raw[:, 4, :], AX.X, ALU.min))
            c.step(vec.scalar_tensor_tensor(out=unit[:, 2:3], in0=unit[:, 1:2], scalar=-1.0, in1=unit[:, 0:1],
                                            op0=ALU.mult, op1=ALU.max))
            c.step(vec.tensor_scalar(unit[:, 2:3], unit[:, 2:3], 1e-30, None, ALU.max))
            c.step(vec.reciprocal(unit[:, 3:4], unit[:, 2:3]))
            vec.tensor_scalar(diag, m.ident, unit[:, 2:3], None, ALU.mult)
            vec.tensor_scalar(raw[:, 4, :], raw[:, 4, :], unit[:, 3:4], None, ALU.mult).then_inc(s.scaled, 1)
            vec.wait_ge(s.units, 1)
            vec.tensor_scalar(m.unit[:, :], m.ps[7][:, 0:D], 2.0, None, ALU.mult)
            vec.wait_ge(s.turned, 1)
            vec.tensor_copy(rawT[:, 0:4, :].rearrange("p k d -> p (k d)"), m.ps[4][:, :])
            vec.tensor_copy(rawT[:, 4, :], m.ps[5][:, 0:D]).then_inc(s.mapsc, 1)
            vec.wait_ge(s.maps, 1)
            vec.wait_ge(s.mapsc, 1)
            vec.tensor_copy(m.maps[:, 0:2, :].rearrange("p k d -> p (k d)"), m.ps[6][:, 0:2 * D])
            vec.tensor_copy(m.maps[:, 2, :], rawT[:, 4, :])

            def step(t, u):
                reached(vec, s.turnedr, t - 1)
                for j in range(GRP):
                    img = t * GRP + j
                    e = vec.tensor_scalar(ln[:, u % 2, j, :], m.b[:, bass.ds(img, 1), :], fac[:, 0, bass.ds(img, 1)],
                                          fac[:, 1, bass.ds(img, 1)], ALU.subtract, ALU.mult)
                e.then_inc(s.staged, 1)
            sweep(vec, step, 0)


LEAD = 3


def stage_attention(nc, held, m):
    s = semaphores(nc, held, "attn", "proj_k proj_v k_high k_low k_squared k_norm k_norm_copied v_copied turned v_high "
                   "v_low proj_q q_high q_low q_squared q_norm q_norm_copied scores dist inner outer high low "
                   "summed_high summed_low left_a left_b sums merged scaled added")
    a = m.a[:, :, :].rearrange("p a b -> p (a b)")
    NC = SEQ // 512
    START = 2
    TILES = NQC * KT

    def results(c, slot):
        return a[:, bass.ds((c - slot) * QC, 2 * QC)].rearrange("p (j s d) -> p j s d", j=4, s=2)

    def both(j):
        return m.ps[4 + j][:, 0:2 * D + 2].rearrange("p (s d) -> p s d", s=2)[:, :, 0:D]

    with nc.Block() as block:
        @block.tensor
        def _(pe):
            for sem in (s.summed_high, s.summed_low):
                pe.sem_inc(sem, START)

            def project_queries(c):
                pe.wait_ge(s.q_norm_copied, START + c)
                pe.matmul(m.ps[3][:, :], m.maps[:, 0, :], a[:, bass.ds(c * QC, QC)], start=True, stop=True)\
                    .then_inc(s.proj_q, 1)

            def query_norms(c, slot):
                pe.wait_ge(s.q_squared, c + 1)
                pe.wait_ge(s.q_low, c + 1)
                pe.matmul(m.ps[3][:, :], m.halves[:, :], m.q2[:, slot, :], start=True, stop=True).then_inc(s.q_norm, 1)

            def norm_and_turn(b, ch):
                n = b * NC + ch
                pe.wait_ge(s.k_squared, n + 1)
                for j in range(4):
                    mm = pe.matmul(m.ps[6][:, ch * 4 + j:ch * 4 + j + 1], m.wt[:, ch % 2, j * P:j * P + P],
                                   m.halves[:, 0:1], start=True, stop=True)
                mm.then_inc(s.k_norm, 1)
                if ch >= 2:
                    pe.wait_ge(s.v_low, n - 1)
                pe.wait_ge(s.v_copied, n + 1)
                for j in range(4):
                    mm = pe.transpose(m.ps[7 if ch % 2 else 2][:, j * P:j * P + P], m.dist[:, ch % 2, j * P:j * P + P],
                                      m.ident)
                mm.then_inc(s.turned, 1)

            with pe.Fori(0, NB) as b:
                pe.wait_ge(s.dist, START + b * TILES)
                pe.wait_ge(s.left_a, START + b * (NQC * 2))
                pe.wait_ge(s.left_b, START + b * (NQC * 2))
                project_queries(b * NQC)
                for ch in range(NC):
                    n = b * NC + ch
                    src = a[:, bass.ds(n * 512, 512)]
                    if ch >= 2:
                        pe.wait_ge(s.k_low, n - 1)
                        pe.wait_ge(s.k_squared, n - 1)
                    pe.matmul(m.ps[ch % 2][:, :], m.maps[:, 1, :], src, start=True, stop=True).then_inc(s.proj_k, 1)
                    if ch >= 2:
                        pe.wait_ge(s.v_copied, n - 1)
                    pe.matmul(m.ps[4 + ch % 2][:, :], m.maps[:, 2, :], src, start=True, stop=True).then_inc(s.proj_v, 1)
                    if ch == 0:
                        query_norms(b * NQC, 0)
                    else:
                        norm_and_turn(b, ch - 1)
                norm_and_turn(b, NC - 1)
                for sem in (s.k_low, s.k_squared, s.v_low, s.v_copied):
                    pe.wait_ge(sem, (b + 1) * NC)
                pe.wait_ge(s.k_norm_copied, b + 1)

                def run(qc, slot, first, last):
                    c = b * NQC + qc
                    n0 = c * KT

                    def scores(k):
                        tile, q = k % KT, (slot + k // KT) % 2
                        if k == KT:
                            pe.wait_ge(s.q_low, c + 2)
                        if not first or k >= LEAD:
                            pe.wait_ge(s.dist, START + n0 + k + 1 - (2 if tile < 2 else 3))
                        for i, (key, query) in enumerate(((m.kH, m.qH), (m.kL, m.qH), (m.kH, m.qL))):
                            mm = pe.matmul(m.ps[tile % 3][:, :], key[:, tile * P:tile * P + P], query[:, q, :],
                                           start=(i == 0), stop=(i == 2))
                        mm.then_inc(s.scores, 1)

                    def sum_low(k):
                        pe.wait_ge(s.low, START + n0 + k + 1)
                        for j in range(4):
                            mm = pe.matmul(m.ps[4 + j][:, 0:D + 1], m.wL[:, k % 2, j * P:j * P + P],
                                           m.v[:, k, 0:D + 1], start=False, stop=(k == KT - 1))
                        mm.then_inc(s.summed_low, 1)
                    if first:
                        for k in range(LEAD):
                            scores(k)
                    for k in range(KT):
                        if k + LEAD < (KT if last else KT + LEAD):
                            scores(k + LEAD)
                        if k == 8 and not last:
                            project_queries(c + 1)
                        if k == 17 and not last:
                            query_norms(c + 1, 1 - slot)
                        pe.wait_ge(s.high, START + n0 + k + 1)
                        for j in range(4):
                            if k == 0 and not first:
                                pe.wait_ge(s.left_a if j < 2 else s.left_b, START + (c - 1) * 2 + j % 2 + 1)
                            mm = pe.matmul(m.ps[4 + j][:, 0:2 * D + 1], m.wH[:, k % 2, j * P:j * P + P],
                                           m.v[:, k, 0:2 * D + 1], start=(k == 0), stop=False)
                        mm.then_inc(s.summed_high, 1)
                        if k > 0:
                            sum_low(k - 1)
                    sum_low(KT - 1)
                run(0, 0, True, False)
                with pe.Fori(0, NQC // 2 - 1) as pair:
                    for i in (1, 2):
                        run(pair * 2 + i, i % 2, False, False)
                run(NQC - 1, 1, False, True)

        @block.vector
        def _(vec):
            for sem in (s.q_norm_copied, s.dist, s.high, s.left_a, s.added):
                vec.sem_inc(sem, START)

            def split_queries(c, slot):
                vec.wait_ge(s.proj_q, c + 1)
                vec.tensor_copy(m.qH[:, slot, :], m.ps[3][:, :]).then_inc(s.q_high, 1)
                vec.wait_ge(s.q_high, c + 1)
                vec.tensor_tensor(m.qL[:, slot, :], m.ps[3][:, :], m.qH[:, slot, :], ALU.subtract).then_inc(s.q_low, 1)

            with vec.Fori(0, NB) as b:
                split_queries(b * NQC, 0)
                for ch in range(NC + 1):
                    n = b * NC + ch
                    part = slice(ch * 512, ch * 512 + 512)
                    if ch < NC:
                        vec.wait_ge(s.proj_k, n + 1)
                        vec.tensor_copy(m.kH[:, part], m.ps[ch % 2][:, :]).then_inc(s.k_high, 1)
                    if ch < NC:
                        vec.wait_ge(s.k_high, n + 1)
                        vec.tensor_tensor(m.kL[:, part], m.ps[ch % 2][:, :], m.kH[:, part], ALU.subtract)\
                            .then_inc(s.k_low, 1)
                    if ch > 0:
                        tiles = slice(4 * ch - 4, 4 * ch)
                        vec.wait_ge(s.v_high, n)
                        vec.tensor_tensor(m.v[:, tiles, D + 1:2 * D + 1],
                                          m.ps[2 if ch % 2 else 7][:, :].rearrange("p (j d) -> p j d", j=4),
                                          m.v[:, tiles, 0:D], ALU.subtract).then_inc(s.v_low, 1)
                vec.wait_ge(s.k_norm, (b + 1) * NC)
                vec.tensor_copy(m.k2[:, :], m.ps[6][:, 0:KT]).then_inc(s.k_norm_copied, 1)
                vec.wait_ge(s.k_norm_copied, b + 1)

                def distances(qc, slot, k):
                    c = b * NQC + qc + k // KT
                    t, slot = (b * NQC + qc) * KT + k, (slot + k // KT) % 2
                    if k % KT == 0:
                        vec.wait_ge(s.q_norm_copied, START + c + 1)
                    vec.wait_ge(s.scores, t + 1)
                    vec.wait_ge(s.outer, START + t - 1)
                    vec.scalar_tensor_tensor(out=m.dist[:, k % 2, :], in0=m.ps[k % KT % 3][:, :],
                                             scalar=m.k2[:, k % KT:k % KT + 1], in1=m.q2[:, slot, :],
                                             op0=ALU.subtract, op1=ALU.subtract).then_inc(s.dist, 1)

                def high_part(qc, k):
                    t = (b * NQC + qc) * KT + k
                    vec.wait_ge(s.outer, START + t + 1)
                    vec.wait_ge(s.summed_high, START + t - 1)
                    vec.wait_ge(s.low, START + t - 1)
                    vec.tensor_copy(m.wH[:, k % 2, :], m.wt[:, k % 2, :]).then_inc(s.high, 1)

                def leave_banks(qc, slot):
                    c = b * NQC + qc
                    vec.wait_ge(s.summed_high, START + (c + 1) * KT)
                    vec.wait_ge(s.summed_low, START + (c + 1) * KT)
                    vec.wait_ge(s.added, START + c)
                    for j in (0, 1):
                        vec.tensor_copy(m.sums[:, j:j + 1], m.ps[4 + j][:, D:D + 1])
                        vec.tensor_copy(results(c, slot)[:, j], both(j)).then_inc(s.left_a, 1)

                def merge(qc, slot):
                    c = b * NQC + qc
                    vec.wait_ge(s.left_a, START + (c + 1) * 2)
                    vec.wait_ge(s.left_b, START + (c + 1) * 2)
                    vec.reciprocal(m.rden[:, 0:4], m.sums[:, :])
                    r = results(c, slot)
                    vec.tensor_tensor(r[:, :, 0], r[:, :, 0], r[:, :, 1], ALU.add).then_inc(s.merged, 1)

                def finish(qc, slot):
                    c = b * NQC + qc
                    r = results(c, slot)
                    vec.wait_ge(s.merged, c + 1)
                    for j in range(4):
                        e = vec.scalar_tensor_tensor(out=r[:, j, 0], in0=r[:, j, 0], scalar=m.rden[:, j:j + 1],
                                                     in1=m.unit[:, :], op0=ALU.mult, op1=ALU.mult)
                    e.then_inc(s.scaled, 1)
                    vec.wait_ge(s.scaled, c + 1)
                    x = m.b[:, bass.ds(c * 4, 4), :]
                    vec.tensor_tensor(x, r[:, :, 0], x, ALU.add).then_inc(s.added, 1)

                def statistics(qc, slot):
                    c = b * NQC + qc
                    vec.wait_ge(s.added, START + c + 1)
                    vec.tensor_copy(m.rden[:, 4:8], m.rden[:, 0:4])
                    for j in range(4):
                        row = bass.ds(c * 4 + j, 1)
                        vec.bn_stats(m.st[:, row, :], m.b[:, row, :])

                def run(qc, slot, first, last):
                    for k in range(KT):
                        if k + 1 < KT or not last:
                            distances(qc, slot, k + 1)
                        high_part(qc, k)
                        if not first:
                            if k == 0:
                                leave_banks(qc - 1, 1 - slot)
                            if k == 2:
                                merge(qc - 1, 1 - slot)
                            if k == 4:
                                finish(qc - 1, 1 - slot)
                            if k == 7:
                                statistics(qc - 1, 1 - slot)
                        if k == 12 and not last:
                            split_queries(b * NQC + qc + 1, 1 - slot)
                distances(0, 0, 0)
                run(0, 0, True, False)
                with vec.Fori(0, NQC // 2 - 1) as pair:
                    for i in (1, 2):
                        run(pair * 2 + i, i % 2, False, False)
                run(NQC - 1, 1, False, True)
                for part in (leave_banks, merge, finish, statistics):
                    part(NQC - 1, 1)

        @block.scalar
        def _(act):
            for sem in (s.outer, s.left_b):
                act.sem_inc(sem, START)

            def square_queries(c, slot):
                act.wait_ge(s.proj_q, c + 1)
                act.wait_ge(s.q_low, c + 1)
                act.activation(m.q2[:, slot, :], m.ps[3][:, :], ACT.Square).then_inc(s.q_squared, 1)

            def copy_norms(c, slot):
                act.wait_ge(s.q_norm, c + 1)
                act.copy(m.q2[:, slot, :], m.ps[3][:, :]).then_inc(s.q_norm_copied, 1)

            with act.Fori(0, NB) as b:
                act.wait_ge(s.low, START + b * TILES)
                act.wait_ge(s.summed_high, START + b * TILES)
                act.wait_ge(s.summed_low, START + b * TILES)
                square_queries(b * NQC, 0)
                for ch in range(NC + 1):
                    n = b * NC + ch
                    if ch < NC:
                        act.wait_ge(s.proj_v, n + 1)
                        if ch >= 2:
                            act.wait_ge(s.turned, n - 1)
                        act.copy(m.dist[:, ch % 2, :], m.ps[4 + ch % 2][:, :]).then_inc(s.v_copied, 1)
                    if ch == 0:
                        copy_norms(b * NQC, 0)
                    if ch < NC:
                        act.wait_ge(s.k_low, n + 1)
                        if ch >= 2:
                            act.wait_ge(s.k_norm, n - 1)
                        act.activation(m.wt[:, ch % 2, :], m.ps[ch % 2][:, :], ACT.Square).then_inc(s.k_squared, 1)
                    if ch > 0:
                        act.wait_ge(s.turned, n)
                        act.copy(m.v[:, 4 * ch - 4:4 * ch, 0:D],
                                 m.ps[2 if ch % 2 else 7][:, :].rearrange("p (j d) -> p j d", j=4)).then_inc(s.v_high, 1)
                act.wait_ge(s.k_norm, (b + 1) * NC)

                def leave_banks(qc, slot):
                    c = b * NQC + qc
                    act.wait_ge(s.summed_high, START + (c + 1) * KT)
                    act.wait_ge(s.summed_low, START + (c + 1) * KT)
                    act.wait_ge(s.added, START + c)
                    for j in (2, 3):
                        act.copy(m.sums[:, j:j + 1], m.ps[4 + j][:, D:D + 1])
                        act.copy(results(c, slot)[:, j], both(j)).then_inc(s.left_b, 1)

                def run(qc, slot, first, last):
                    n0 = (b * NQC + qc) * KT
                    for k in range(KT):
                        act.wait_ge(s.dist, START + n0 + k + 1)
                        act.activation(m.dist[:, k % 2, :], m.dist[:, k % 2, :], ACT.Exp, scale=2.0).then_inc(s.inner, 1)
                        act.wait_ge(s.low, START + n0 + k - 1)
                        act.wait_ge(s.inner, n0 + k + 1)
                        act.activation(m.wt[:, k % 2, :], m.dist[:, k % 2, :], ACT.Exp).then_inc(s.outer, 1)
                        if k == 0 and not first:
                            leave_banks(qc - 1, 1 - slot)
                        if k == 12 and not last:
                            square_queries(b * NQC + qc + 1, 1 - slot)
                        if k == 20 and not last:
                            copy_norms(b * NQC + qc + 1, 1 - slot)
                run(0, 0, True, False)
                with act.Fori(0, NQC // 2 - 1) as pair:
                    for i in (1, 2):
                        run(pair * 2 + i, i % 2, False, False)
                run(NQC - 1, 1, False, True)
                leave_banks(NQC - 1, 1)

        @block.gpsimd
        def _(pool):
            pool.sem_inc(s.low, START)
            with pool.Fori(0, NB * NQC) as c:
                for k in range(KT):
                    pool.wait_ge(s.high, START + c * KT + k + 1)
                    pool.wait_ge(s.summed_low, START + c * KT + k - 1)
                    pool.tensor_tensor(m.wL[:, k % 2, :], m.wt[:, k % 2, :], m.wH[:, k % 2, :], ALU.subtract)\
                        .then_inc(s.low, 1)


def stage_experts(nc, held, m, ins, out):
    s = semaphores(nc, held, "experts", "loaded v factor rooted normed turned copied logits shifted exp gates gates_turned "
                   "gates_copied biased tiles scaled_a scaled_b scaled_sum reduced partly result stored0 stored1")
    out_img = out.rearrange("b t h w -> h (b t) w")
    ONE = 1
    stored = [s.stored0, s.stored1]

    with nc.Block() as block:
        @block.sync
        def _(sp):
            with nc.allow_non_contiguous_dma(reason="weights of the experts, once"):
                sp.dma_start(m.w8[:, :].rearrange("p (e c) -> p e c", e=EXPERTS),
                             ins['L1_ffn_expert_w'].rearrange("e d c -> d e c")).then_inc(s.loaded, 16)
                sp.dma_start(m.rw[:, :], ins['L1_ffn_router_w']).then_inc(s.loaded, 16)
                sp.dma_start(m.rb[:, :], ins['L1_ffn_router_b'].partition_broadcast(P)).then_inc(s.loaded, 16)
                sp.dma_start(m.eb[:, :], ins['L1_ffn_expert_b']).then_inc(s.loaded, 16)
            with sp.Fori(0, NG // 2) as it:
                for u in (0, 1):
                    g = it * 2 + u
                    sp.wait_ge(s.result, g + 1)
                    sp.dma_start(out_img[:, bass.ds(g * GRP, GRP), :], m.y[:, u]).then_inc(stored[u], 16)
            for u in (0, 1):
                sp.wait_ge(stored[u], NG // 2 * 16)

        @block.tensor
        def _(pe):
            pe.wait_ge(s.loaded, 64)

            def experts(g, u, tiles):
                for j in tiles:
                    n = g * GRP + j
                    reached(pe, s.scaled_a, n - 1)
                    reached(pe, s.scaled_b, n - 1)
                    for h in (0, 1):
                        mm = pe.matmul(m.ps[4 + 2 * (j % 2) + h][:, :], m.lnT[:, u, j, :], m.w8[:, 512 * h:512 * h + 512],
                                       start=True, stop=True)
                    mm.then_inc(s.tiles, 1)

            def step(t, u):
                if live(t):
                    pe.wait_ge(s.normed, t + 1)
                    reached(pe, s.copied, t)
                    for j in range(GRP):
                        mm = pe.transpose(m.ps[0][:, j * P:j * P + P], m.ln[:, u % 2, j, :], m.ident)
                    mm.then_inc(s.turned, 1)
                g, v = t - 1, (u - 1) % 2
                if live(g):
                    pe.wait_ge(s.gates_copied, g + 1)
                    reached(pe, s.result, g)
                    for j in range(GRP):
                        mm = pe.matmul(m.ps[3][:, j * D:j * D + D], m.gT[:, v, j, :], m.eb[:, :], start=True, stop=True)
                    mm.then_inc(s.biased, 1)
                    experts(g, v, (0, 1))
                if live(t):
                    pe.wait_ge(s.copied, t + 1)
                    reached(pe, s.shifted, t)
                    for j in range(GRP):
                        mm = pe.matmul(m.ps[1][:, j * EXPERTS:j * EXPERTS + EXPERTS], m.lnT[:, u % 2, j, :], m.rw[:, :],
                                       start=True, stop=True)
                    mm.then_inc(s.logits, 1)
                if live(g):
                    experts(g, v, (2, 3))
                if live(t):
                    pe.wait_ge(s.gates, t + 1)
                    reached(pe, s.gates_copied, t)
                    for j in range(GRP):
                        mm = pe.transpose(m.ps[2][0:EXPERTS, j * P:j * P + P], m.gt[:, u % 2, 5, j, :], m.ident)
                    mm.then_inc(s.gates_turned, 1)
            sweep(pe, step, 1)

        @block.scalar
        def _(act):
            act.wait_ge(s.factor, 1)
            act.activation(m.fac[:, 1], m.fac[:, 1], ACT.Sqrt).then_inc(s.rooted, 1)

            def scale(g, u, tiles):
                for j in tiles:
                    n = g * GRP + j
                    act.wait_ge(s.tiles, n + 1)
                    reached(act, s.scaled_sum, n - 1)
                    for e in range(4):
                        o = act.activation(m.pb[:, j % 2, e, :], m.ps[5 + 2 * (j % 2)][:, e * D:e * D + D], ACT.Copy,
                                           scale=m.gt[:, u, 5, j, 4 + e:5 + e])
                    o.then_inc(s.scaled_b, 1)

            def step(t, u):
                if live(t):
                    act.wait_ge(s.turned, t + 1)
                    reached(act, s.tiles, (t - 1) * GRP)
                    act.copy(m.lnT[:, u % 2], banked(m, 0)).then_inc(s.copied, 1)
                g, v = t - 1, (u - 1) % 2
                if live(g):
                    scale(g, v, (0, 1))
                if live(t):
                    act.wait_ge(s.shifted, t + 1)
                    act.activation(m.gt[:, u % 2, 1], m.gt[:, u % 2, 1], ACT.Exp).then_inc(s.exp, 1)
                if live(g):
                    scale(g, v, (2, 3))
                if live(t):
                    act.wait_ge(s.gates_turned, t + 1)
                    act.copy(m.gT[:, u % 2], m.ps[2][0:EXPERTS, :].rearrange("p (t w) -> p t w", t=GRP))\
                        .then_inc(s.gates_copied, 1)
            sweep(act, step, 1)

        @block.gpsimd
        def _(pool):
            with pool.Fori(0, NI // 2) as it:
                for u in (0, 1):
                    n = it * 2 + u
                    pool.wait_ge(s.scaled_a, n + 1)
                    pool.wait_ge(s.scaled_b, n + 1)
                    pool.wait_ge(s.reduced, ONE + it * 2)
                    pool.tensor_tensor(m.pc[:, u], m.pa[:, u], m.pb[:, u], ALU.add).then_inc(s.scaled_sum, 1)

        @block.vector
        def _(vec):
            c = Chain(vec, s.v)
            vec.sem_inc(s.reduced, ONE)
            vec.wait_ge(s.loaded, 64)
            row_factors(vec, c, m.st, m.fac, s.factor, s.rooted)

            def normed(t, u):
                reached(vec, s.turned, t - 1)
                for j in range(GRP):
                    img = bass.ds(t * GRP + j, 1)
                    e = vec.tensor_scalar(m.ln[:, u % 2, j, :], m.b[:, img, :], m.fac[:, 0, img], m.fac[:, 1, img],
                                          ALU.subtract, ALU.mult)
                e.then_inc(s.normed, 1)

            def weigh(g, u, tiles, before):
                for j in tiles:
                    n = g * GRP + j
                    vec.wait_ge(s.tiles, n + 1)
                    reached(vec, s.scaled_sum, n - 1)
                    src = m.ps[4 + 2 * (j % 2)][:, :].rearrange("p (e c) -> p e c", e=4)
                    vec.tensor_tensor(m.pa[:, j % 2], src, over(m.gt[:, u, 5, j, 0:4], 2, D), ALU.mult)\
                        .then_inc(s.scaled_a, 1)
                for j in tiles:
                    n = g * GRP + j
                    if j == 0:
                        reached(vec, stored[u], before * 16)
                    vec.wait_ge(s.scaled_sum, n + 1)
                    vec.tensor_reduce(m.y[:, u, j, :], m.pc[:, j % 2].rearrange("p e c -> p c e"), AX.X, ALU.add)\
                        .then_inc(s.reduced, 1)

            def gates(t, u):
                logit, ex, sel, cnt, best, gate = (m.gt[:, u, i] for i in range(6))
                top, total = m.g1[:, 0], m.g1[:, 1]
                vec.wait_ge(s.logits, t + 1)
                c.step(vec.tensor_tensor(logit, m.ps[1][:, 0:GRP * EXPERTS].rearrange("p (t e) -> p t e", t=GRP),
                                         over(m.rb[:, :], 1, GRP), ALU.add))
                c.step(vec.tensor_reduce(top, logit, AX.X, ALU.max))
                vec.tensor_tensor(ex, logit, over(top, 2, EXPERTS), ALU.subtract).then_inc(s.shifted, 1)
                other, own = over(logit, 2, EXPERTS), over(logit, 3, EXPERTS)
                vec.tensor_tensor(m.rk[:, 0], other, own, ALU.is_gt)
                c.step(vec.tensor_tensor(m.rk[:, 1], other, own, ALU.is_equal))
                c.step(vec.tensor_tensor(m.rk[:, 1], m.rk[:, 1], over(m.tie, 1, GRP), ALU.mult))
                c.step(vec.tensor_tensor(m.rk[:, 0], m.rk[:, 0], m.rk[:, 1], ALU.add))
                c.step(vec.tensor_reduce(cnt, m.rk[:, 0], AX.X, ALU.add))
                c.step(vec.tensor_scalar(sel, cnt, 1.5, None, ALU.is_lt))
                vec.wait_ge(s.exp, t + 1)
                c.step(vec.tensor_tensor(best, ex, sel, ALU.mult))
                c.step(vec.tensor_reduce(total, best, AX.X, ALU.add))
                c.step(vec.reciprocal(total, total))
                vec.tensor_tensor(gate, best, over(total, 2, EXPERTS), ALU.mult).then_inc(s.gates, 1)
            PER = 10

            def step(t, u, it):
                if isinstance(t, int) and t == 0:
                    normed(0, 0)
                g, v = t - 1, (u - 1) % 2
                before = it * (UN // 2) + (u - 1) // 2
                if live(g):
                    weigh(g, v, (0, 1), before)
                if live(t):
                    gates(t, u % 2)
                if live(t + 1):
                    normed(t + 1, u + 1)
                if live(g):
                    weigh(g, v, (2, 3), before)
                    vec.wait_ge(s.biased, g + 1)
                    vec.wait_ge(s.reduced, ONE + (g + 1) * GRP)
                    vec.tensor_tensor(m.y[:, v], m.y[:, v], banked(m, 3), ALU.add).then_inc(s.partly, 1)
                    vec.wait_ge(s.partly, g + 1)
                    vec.tensor_tensor(m.y[:, v], m.y[:, v], group(m.b, g), ALU.add).then_inc(s.result, 1)
            for u in range(UN):
                step(u, u, 0)
            with vec.Fori(1, NG // UN - 1) as it:
                c.enter(it - 1, PER * UN)
                for u in range(UN):
                    step(it * UN + u, u, it)
            c.leave(NG // UN - 2)
            for u in range(UN + 1):
                step(NG - UN + u, u, NG // UN - 1)


def build(nc, ins, const, where, out, upto=99):
    with ExitStack() as ctx:
        tok = nc.dram_tensor("tokens_scratch", (NI, NH, NW), F32, kind="Internal").ap()
        mix = nc.dram_tensor("mixed_scratch", (NI, NH, NW), F32, kind="Internal").ap()
        m = memory(nc, ctx, where)
        held = []
        stages = [
            lambda: stage_tokens(nc, held, m, ins, tok, const),
            lambda: stage_forward(nc, held, m, tok),
            lambda: stage_modes(nc, held, m),
            lambda: stage_weights(nc, held, m),
            lambda: stage_scores(nc, held, m),
            lambda: stage_mix(nc, held, m, mix),
            lambda: stage_inverse(nc, held, m, 'proj', mix=mix),
            lambda: stage_factors(nc, held, m, 'proj'),
            lambda: stage_attended(nc, held, m),
            lambda: stage_mixer(nc, held, m, 1),
            lambda: stage_inverse(nc, held, m, 'mix1', ins=ins),
            lambda: stage_mixer(nc, held, m, 2),
            lambda: stage_inverse(nc, held, m, 'mix2'),
            lambda: stage_factors(nc, held, m, 'mix2'),
            lambda: stage_residual(nc, held, m, ins),
            lambda: stage_normed(nc, held, m, ins),
            lambda: stage_attention(nc, held, m),
            lambda: stage_experts(nc, held, m, ins, out),
        ]
        for i, stage in enumerate(stages[:upto]):
            if i == 8:
                nc.clear_and_free_semaphores(held)
                held.clear()
                nc.all_engine_barrier()
            stage()


NAMES = ['x'] + SCALARS + [
    'L0_conv_key_w', 'L0_conv_key_skip_w', 'L0_conv_key_skip_b', 'L0_conv_query_w', 'L0_conv_query_skip_w',
    'L0_conv_query_skip_b', 'L0_conv_value_w', 'L0_conv_value_skip_w', 'L0_conv_value_skip_b', 'L0_conv_proj_w',
    'L0_conv_proj_skip_w', 'L0_conv_mixer_w1', 'L0_conv_mixer_w2', 'L1_attn_rotation_params',
    'L1_attn_entangle_params', 'L1_attn_Wq', 'L1_attn_Wk', 'L1_attn_Wv', 'L1_ffn_router_w', 'L1_ffn_router_b',
    'L1_ffn_expert_w', 'L1_ffn_expert_b']


def kernel(**inputs):
    import concourse.bacc as bacc
    from concourse.bass_utils import run_bass_kernel_spmd

    nc = bacc.Bacc("TRN2", target_bir_lowering=False, num_devices=1)
    arrays, ins = {}, {}
    for name in NAMES:
        a = np.ascontiguousarray(inputs[name])
        arrays[f"in_{name}"] = a
        ins[name] = nc.dram_tensor(f"in_{name}", a.shape, mybir.dt.from_np(a.dtype), kind="ExternalInput").ap()
    table, where = tables()
    arrays["tables"] = table
    const = nc.dram_tensor("tables", table.shape, F32, kind="ExternalInput").ap()
    out = nc.dram_tensor("result", inputs['x'].shape, F32, kind="ExternalOutput").ap()
    build(nc, ins, const, where, out)
    got = run_bass_kernel_spmd(nc, [arrays], core_ids=[0])
    return got.results[0]["result"]
```

```python
from contextlib import ExitStack

import numpy as np
import concourse.bass as bass
from concourse import mybir

F32 = mybir.dt.float32
F32R = mybir.dt.float32r
F16 = mybir.dt.float16
ALU = mybir.AluOpType
ACT = mybir.ActivationFunctionType
AX = mybir.AxisListType

P = 128
NB, NT, NH, NW = 4, 32, 128, 128
NI = NB * NT
HEADS = 16
K33 = 33
FQ = 2 * K33
K17 = 17
FM = 2 * K17
ROWS = 2 * K17
NM = ROWS * K17
MT = [(m, min(P, NM - m)) for m in range(0, NM, P)]
LOWT = 4
HC = 34
GRP = 4
NG = NI // GRP
UN = 4
PIX = NH * NW
EPS = 1e-5
D = 128
SEQ = NT * NH
KT = SEQ // P
QC = 512
NQC = SEQ // QC
EXPERTS = 8
SCALARS = ['L0_conv_norm1_g', 'L0_conv_norm1_b', 'L0_conv_attn_norm_g', 'L0_conv_attn_norm_b',
           'L0_conv_norm2_g', 'L0_conv_norm2_b', 'L0_conv_mixer_skip_w1', 'L0_conv_mixer_skip_b1',
           'L0_conv_mixer_norm_g1', 'L0_conv_mixer_norm_b1', 'L0_conv_mixer_skip_w2',
           'L0_conv_mixer_skip_b2', 'L0_conv_mixer_norm_g2', 'L0_conv_mixer_norm_b2',
           'L0_conv_mixer_out_g', 'L0_conv_mixer_out_b', 'L0_conv_proj_skip_b']


def tables():
    n = np.arange(P)[:, None]
    k = np.arange(K33)[None, :]
    dft = np.concatenate([np.cos(2 * np.pi * n * k / P), np.sin(2 * np.pi * n * k / P)], 1) / P
    dft[:, K33] = 0.0
    k = np.arange(K17)[:, None]
    idft = np.zeros((P, P))
    idft[:K17] = np.cos(2 * np.pi * k * n.T / P)
    idft[K17:FM] = np.sin(2 * np.pi * k * n.T / P)
    twice = np.where(np.arange(P) % K17 > 0, 2.0, 1.0)[:, None]
    batch = np.kron(np.eye(NB), np.ones((NT, NT))) / NT
    low = np.zeros((ROWS, K17))
    low[0:8, 1:9] = 2
    low[K17 + 1:K17 + 9, 1:9] = 2
    low[1:9, 0] = 2
    low[0, 0] = 1
    lowm = np.zeros(P * len(MT))
    lowm[:NM] = 64 * low.ravel()
    var = np.zeros((2, K17, 2, K17))
    var[:, 1:, :, 1:] = 1
    var[0, 0, :, 1:] = 2
    var[:, 1:, 0, 0] = 0.5
    tie = np.arange(EXPERTS)[None, :] < np.arange(EXPERTS)[:, None]

    def on_all(a):
        return np.broadcast_to(a.reshape(1, -1), (P, a.size))
    parts = [('ident', np.eye(P)), ('tie', on_all(tie)), ('dft', dft), ('rows', idft), ('cols', idft * twice),
             ('batch', batch), ('low', lowm.reshape(len(MT), P).T), ('var', on_all(var))]
    at, where = 0, {}
    for name, a in parts:
        where[name] = (at, at + a.shape[1])
        at += a.shape[1]
    return np.concatenate([a for _, a in parts], 1).astype(np.float32), where


class Names(dict):

    def __getattr__(self, name):
        return self[name]


class Views:
    pass


class Chain:

    def __init__(self, eng, sem):
        self.eng, self.sem, self.n, self.off = eng, sem, 0, 0

    def step(self, ins):
        ins.then_inc(self.sem, 1)
        self.n += 1
        self.eng.wait_ge(self.sem, self.off + self.n)

    def enter(self, it, per):
        self.before, self.per = self.n, per
        self.off = it * per

    def leave(self, count):
        assert self.n - self.before == self.per, (self.n - self.before, self.per)
        self.n = self.before + self.per * count
        self.off = 0


def reached(eng, sem, value):
    if not (isinstance(value, int) and value <= 0):
        eng.wait_ge(sem, value)


def over(ap, axis, n):
    shape = list(ap.shape)
    return ap.unsqueeze(axis).to_broadcast(shape[:axis] + [n] + shape[axis:])


def semaphores(nc, held, stage, names):
    made = {n: nc.alloc_semaphore(f"{stage}_{n}") for n in names.split()}
    held.extend(made.values())
    return Names(made)


def memory(nc, ctx, where):
    m = Views()

    def sb(scope, name, shape, dtype=F32):
        return scope.enter_context(nc.sbuf_tensor(name, shape, dtype))

    m.a = sb(ctx, "images_a", [P, NI, NW])
    m.b = sb(ctx, "images_b", [P, NI, NW])
    keep = sb(ctx, "keep", [P, where['tie'][1]])
    m.keep = keep
    m.ident = keep[:, 0:P]
    m.tie = keep[:, P:].rearrange("p (i j) -> p i j", i=EXPERTS)
    small = sb(ctx, "small", [P, 208])
    m.sc = small[:, 0:len(SCALARS)]
    m.skips = small[:, 32:96]
    m.biases = small[:, 96:144]
    m.col = small[:, 144:176]
    m.gram = small[:, 176:208]
    m.ps = [ctx.enter_context(nc.psum_tensor(f"bank{i}", [P, 512], F32)) for i in range(6)]
    pair = ctx.enter_context(nc.psum_tensor("banks_6_7", [P, 1024], F32))
    m.ps += [pair[:, 0:512], pair[:, 512:1024]]
    m.logits = pair[:, :]

    with ExitStack() as l0:
        c0 = where['dft'][0]
        m.tab = sb(l0, "table", [P, where['var'][1] - c0])

        def tab(name, rows=P):
            lo, hi = where[name]
            return m.tab[0:rows, lo - c0:hi - c0]
        m.dft = tab('dft')
        m.dft17 = m.dft.rearrange("p (s k) -> p s k", s=2)[:, :, 0:K17]
        m.rows, m.cols, m.batch, m.low, m.var = tab('rows', FM), tab('cols', FM), tab('batch'), tab('low'), tab('var')
        pair = sb(l0, "pair", [P, 2, 2 * NM])
        m.wraw = pair[0:64, 0, :].rearrange("p (r k c) -> p r k c", r=ROWS, c=2)
        m.weff = pair[0:64, 1, :].rearrange("p (c m) -> p c m", c=2)
        m.feat = pair[:, 0, :].rearrange("p (x y) -> p x y", x=FM)
        m.coef = pair[:, 1, :].rearrange("p (x y) -> p x y", x=FM)
        mixw = sb(l0, "mixer_weights", [P, 2 * NM])
        m.mixw = mixw[:, :].rearrange("p (r k c) -> p r k c", r=ROWS, c=2)
        f = sb(l0, "features", [P, FQ * FQ])
        m.ft = f[:, :].rearrange("p (x y) -> p x y", x=FQ)
        m.half17 = f[:, 0:P * FM].rearrange("p (t x) -> p t x", t=P)
        g = sb(l0, "spare", [P, HC * P])
        m.spare = g[:, :]
        m.gramT = g[:, :].rearrange("p (c t) -> p c t", c=HC)
        m.coefT = g[0:FM, :].rearrange("p (x t) -> p x t", x=FM)
        m.modes = sb(l0, "modes", [P, 2, NM])
        r = sb(l0, "transposed", [P, 1920])
        m.turned = r[:, :]
        m.modesT = r[:, 0:1280].rearrange("p (k c t) -> p k c t", k=5, c=2)
        m.wT = r[:, 1280:1920].rearrange("p (k c h) -> p k c h", k=5, c=2)
        m.stat = r[:, 0:768].rearrange("p (t s) -> p t s", t=P)
        m.aff = r[:, 768:768 + 8 * P].rearrange("p (k t) -> p k t", k=8)
        m.stage = sb(l0, "coef_stage", [P, 2, (GRP - 1) * FM + P])
        m.half = sb(l0, "half_inverse", [P, 2, GRP * NW])
        m.ust = sb(l0, "image_stage", [P, 2, GRP, NW])
        m.tmp = m.modes[:, :, 0:GRP * NW].rearrange("p s (t w) -> p s t w", t=GRP)

    b = m.b[:, :, :].rearrange("p a b -> p (a b)")
    m.half33 = b[:, 0:P * FQ].rearrange("p (t x) -> p t x", t=P)
    m.load = b[:, 12804:12804 + 2048].rearrange("p (s t w) -> p s t w", s=4, t=GRP)
    m.prod = b[:, 0:8192].rearrange("p (k h t) -> p k h t", k=4, h=HEADS)
    m.hg = b[:, 8448:8448 + FQ * FQ]
    m.probT = b[:, 8448:10496].rearrange("p (h t) -> p h t", h=HEADS)
    m.probD = b[:, 0:2048].rearrange("p (h t) -> p h t", h=HEADS)
    m.mixD = b[:, 2048:2176]
    m.mixT = b[:, 2176:2304]
    m.mixA = b[:, 2304:2432]
    m.score, m.expo, m.prob = (b[:, 10496 + 512 * i:11008 + 512 * i].rearrange("p (h s) -> p h s", h=HEADS)
                               for i in range(3))
    m.dcq = b[0:1, 12804:13316].rearrange("p (h s) -> p h s", h=HEADS)
    m.dck = b[0:1, 13316:15364].rearrange("p (h t) -> p h t", h=HEADS)
    m.wk = b[:, 15364:16384]
    m.zprod = b[:, 0:4096].rearrange("p (s k h t) -> p s k h t", s=2, k=4, h=4)
    m.zsum = b[:, 4096:8192].rearrange("p (c h t) -> p c h t", c=2, h=HEADS)

    m.st = sb(ctx, "row_stats", [P, NI, 6])
    with ExitStack() as l1:
        m.scratch = sb(l1, "normed_scratch", [P, 3072])
    with ExitStack() as l1:
        m.kH = sb(l1, "keys_high", [P, SEQ], F32R)
        m.kL = sb(l1, "keys_low", [P, SEQ], F32R)
        m.v = sb(l1, "values", [P, KT, 2 * D + 2], F16)
        m.qH = sb(l1, "queries_high", [P, 2, QC], F32R)
        m.qL = sb(l1, "queries_low", [P, 2, QC], F32R)
        m.q2 = sb(l1, "query_norms", [P, 2, QC])
        m.dist = sb(l1, "distances", [P, 2, QC])
        m.wt = sb(l1, "weights", [P, 2, QC])
        m.wH = sb(l1, "weights_high", [P, 2, QC], F16)
        m.wL = sb(l1, "weights_low", [P, 2, QC], F16)
        m.maps = sb(l1, "maps", [P, 3, D])
        m.unit = sb(l1, "value_units", [P, D])
        m.halves = sb(l1, "halves", [P, P])
        m.k2 = sb(l1, "key_norms", [P, KT])
        m.rden = sb(l1, "reciprocals", [P, 8])
        m.sums = sb(l1, "softmax_sums", [P, 4])
    with ExitStack() as l2:
        m.w8H = sb(l2, "expert_weights_high", [P, EXPERTS * D], F32R)
        m.w8L = sb(l2, "expert_weights_low", [P, EXPERTS * D], F32R)
        m.lnT = sb(l2, "normed_T", [P, 2, GRP, P])
        m.lnH = sb(l2, "normed_high", [P, 2, GRP, P], F32R)
        m.lnL = sb(l2, "normed_low", [P, 2, GRP, P], F32R)
        m.gate = sb(l2, "gates", [P, NI, EXPERTS])
        m.y = sb(l2, "group_result", [P, 2, GRP, D])
        m.pa = sb(l2, "scaled_a", [P, 2, 4, D])
        m.pb = sb(l2, "scaled_b", [P, 2, 4, D])
        m.pc = sb(l2, "scaled_sum", [P, 2, 4, D])
        m.ln = sb(l2, "normed", [P, 2, GRP, D])
        m.rw = sb(l2, "router_weights", [P, EXPERTS])
        m.rb = sb(l2, "router_biases", [P, EXPERTS])
        m.w8 = sb(l2, "expert_weights", [P, EXPERTS * D])
        m.eb = sb(l2, "expert_biases", [P, P // EXPERTS * D])
        m.gT = sb(l2, "gates_T", [P, NI * EXPERTS // P, P])
        m.fac = sb(l2, "row_factors", [P, 4, NI])
        m.g1 = sb(l2, "gate_sums", [P, 2, NI])
        m.logit, m.ex, m.cnt, m.win = (t[:, :, :, :].rearrange("p a b c -> p (a b c)").rearrange("p (t e) -> p t e", e=EXPERTS)
                                       for t in (m.pa, m.pb, m.pc, m.y))
    return m



def stage_tokens(nc, held, m, ins, tok, const):
    s = semaphores(nc, held, "tokens", "tables x weights cleared scalars v sums averaged added rooted stored ready")
    x = ins['x'].rearrange("b t h w -> (b t) h w")
    Q = NH // 4
    nt = m.keep.shape[1]

    with nc.Block() as block:
        @block.sync
        def _(sp):
            for q in range(4):
                sp.dma_start(m.a[:, q * Q:q * Q + Q, :], x[:, q * Q:q * Q + Q, :]).then_inc(s.x, 16)
            sp.wait_ge(s.ready, 1)
            for q in range(4):
                sp.dma_start(tok[:, q * Q:q * Q + Q, :], m.a[:, q * Q:q * Q + Q, :]).then_inc(s.stored, 16)
            sp.wait_ge(s.stored, 64)

        @block.gpsimd
        def _(pool):
            pool.memset(m.wraw, 0.0).then_inc(s.cleared, 1)
            pool.memset(m.mixw, 0.0).then_inc(s.cleared, 1)
            pool.memset(m.turned, 0.0)

        @block.scalar
        def _(act):
            act.dma_start(m.keep[:, :], const[:, 0:nt]).then_inc(s.tables, 16)
            act.dma_start(m.tab[:, :], const[:, nt:]).then_inc(s.tables, 16)
            act.wait_ge(s.cleared, 2)
            with nc.allow_non_contiguous_dma(reason="skip weights and biases, a few numbers"):
                for i, n in enumerate(SCALARS):
                    src = ins[n]
                    if len(src.shape) == 2:
                        src = src.rearrange("a b -> (a b)")
                    act.dma_start(m.sc[:, i:i + 1], src.partition_broadcast(P)).then_inc(s.scalars, 16)
                for i, n in enumerate(['query', 'key', 'value', 'proj']):
                    w = ins[f'L0_conv_{n}_skip_w'].rearrange("a b -> (a b)")
                    act.dma_start(m.skips[:, 16 * i:16 * i + 16], w.partition_broadcast(P)).then_inc(s.scalars, 16)
                    if n == 'proj':
                        w = ins['L0_conv_proj_w'][:, 0]
                        act.dma_start(m.wraw[48:64, 0:16], w[:, 0:16]).then_inc(s.weights, 16)
                        act.dma_start(m.wraw[48:64, K17 + 1:ROWS], w[:, 31:15:-1]).then_inc(s.weights, 16)
                        continue
                    act.dma_start(m.biases[:, 16 * i:16 * i + 16],
                                  ins[f'L0_conv_{n}_skip_b'].partition_broadcast(P)).then_inc(s.scalars, 16)
                    w = ins[f'L0_conv_{n}_w'][0]
                    act.dma_start(m.wraw[16 * i:16 * i + 16, 0:8, 0:9], w[:, 0:8]).then_inc(s.weights, 16)
                    act.dma_start(m.wraw[16 * i:16 * i + 16, K17 + 1:K17 + 9, 0:9], w[:, 15:7:-1])\
                        .then_inc(s.weights, 16)
                load_mixer(act, m, ins, 1, s.weights)
            act.wait_ge(s.added, 1)
            act.activation(m.spare[:, 320:352], m.spare[:, 320:352], ACT.Sqrt).then_inc(s.rooted, 1)
            act.wait_ge(s.added, 2)
            act.activation(m.col[:, 4:5], m.col[:, 3:4], ACT.Sqrt).then_inc(s.rooted, 1)
            act.wait_ge(s.tables, 32)
            act.wait_ge(s.weights, 16 * 10)
            act.wait_ge(s.scalars, 16 * (len(SCALARS) + 7))

        @block.tensor
        def _(pe):
            pe.wait_ge(s.tables, 32)
            pe.wait_ge(s.sums, 1)
            pe.matmul(m.ps[0][:, 0:32], m.batch, m.spare[:, 192:224], start=True, stop=True).then_inc(s.averaged, 1)
            pe.wait_ge(s.sums, 2)
            pe.matmul(m.ps[1][:, 0:32], m.batch, m.spare[:, 352:384], start=True, stop=True).then_inc(s.averaged, 1)

        @block.vector
        def _(vec):
            c = Chain(vec, s.v)
            gs = m.spare[:, 0:192].rearrange("p (g k) -> p g k", g=32)
            two, mean, var, rstd, work = (m.spare[:, 192 + 32 * i:224 + 32 * i] for i in (0, 1, 5, 4, 6))
            dev = m.spare[:, 384:448].rearrange("p (g k) -> p g k", g=32)
            sq = m.spare[:, 448:512].rearrange("p (g k) -> p g k", g=32)
            vec.wait_ge(s.x, 64)
            with vec.Fori(0, 4) as it:
                c.enter(it, 1)
                for u in range(8):
                    g = it * 8 + u
                    e = vec.bn_stats(gs[:, g, :], m.a[:, :, bass.ds(g * 4, 4)])
                c.step(e)
            c.leave(4)
            vec.tensor_tensor(two, gs[:, :, 1], gs[:, :, 4], ALU.add).then_inc(s.sums, 1)
            vec.wait_ge(s.averaged, 1)
            c.step(vec.tensor_scalar(mean, m.ps[0][:, 0:32], 0.5, None, ALU.mult))
            c.step(vec.tensor_tensor(dev, gs[:, :, 1::3], over(mean, 2, 2), ALU.subtract))
            c.step(vec.tensor_tensor(sq, dev, dev, ALU.mult))
            c.step(vec.tensor_reduce(work, sq, AX.X, ALU.add))
            c.step(vec.tensor_scalar(work, work, 0.5, None, ALU.mult))
            c.step(vec.tensor_tensor(var, gs[:, :, 2], gs[:, :, 5], ALU.add))
            vec.scalar_tensor_tensor(out=var, in0=var, scalar=1.0 / 512, in1=work, op0=ALU.mult, op1=ALU.add)\
                .then_inc(s.sums, 1)
            vec.wait_ge(s.averaged, 2)
            vec.tensor_scalar(rstd, m.ps[1][:, 0:32], EPS, None, ALU.add).then_inc(s.added, 1)
            vec.wait_ge(s.rooted, 1)
            c.step(vec.reciprocal(rstd, rstd))
            with vec.Fori(0, 4) as it:
                c.enter(it, 1)
                for u in range(8):
                    g = it * 8 + u
                    e = vec.tensor_scalar(m.a[:, :, bass.ds(g * 4, 4)], m.a[:, :, bass.ds(g * 4, 4)],
                                          mean[:, bass.ds(g, 1)], rstd[:, bass.ds(g, 1)], ALU.subtract, ALU.mult)
                c.step(e)
            c.leave(4)
            vec.drain().then_inc(s.ready, 1)
            with vec.Fori(0, 4) as it:
                c.enter(it, 1)
                for u in range(8):
                    g = it * 8 + u
                    e = vec.bn_stats(gs[:, g, :], m.a[:, bass.ds(g * 4, 4), :].rearrange("p a b -> p (a b)"))
                c.step(e)
            c.leave(4)
            c.step(vec.bn_aggr(m.col[:, 2:4], m.spare[:, 0:192]))
            vec.tensor_scalar(m.col[:, 3:4], m.col[:, 3:4], EPS, None, ALU.add).then_inc(s.added, 1)
            vec.wait_ge(s.rooted, 2)
            vec.wait_ge(s.scalars, 16 * (len(SCALARS) + 7))
            c.step(vec.reciprocal(m.col[:, 4:5], m.col[:, 4:5]))
            c.step(vec.tensor_tensor(m.col[:, 0:1], m.col[:, 4:5], m.sc[:, 0:1], ALU.mult))
            c.step(vec.tensor_tensor(m.col[:, 5:6], m.col[:, 0:1], m.col[:, 2:3], ALU.mult))
            c.step(vec.tensor_tensor(m.col[:, 1:2], m.sc[:, 1:2], m.col[:, 5:6], ALU.subtract))


def load_mixer(eng, m, ins, i, sem):
    w = ins[f'L0_conv_mixer_w{i}'][0, 0]
    eng.dma_start(m.mixw[:, 0:16], w[0:16].partition_broadcast(P)).then_inc(sem, 16)
    eng.dma_start(m.mixw[:, K17 + 1:ROWS], w[31:15:-1].partition_broadcast(P)).then_inc(sem, 16)


def stage_forward(nc, held, m, tok):
    s = semaphores(nc, held, "forward", "in0 in1 in2 in3 first copied second scaled v")
    arrived = [s.in0, s.in1, s.in2, s.in3]
    tok_img = tok.rearrange("t h w -> h t w")
    per = 6
    rounds = FQ // per

    with nc.Block() as block:
        @block.sync
        def _(sp):
            def body(it):
                for u in range(UN):
                    g = it * UN + u
                    reached(sp, s.first, g - UN + 1)
                    sp.dma_start(m.load[:, u], tok_img[:, bass.ds(g * GRP, GRP), :]).then_inc(arrived[u], 16)
            body(0)
            with sp.Fori(1, NG // UN) as it:
                body(it)

        @block.tensor
        def _(pe):
            def body(it):
                for u in range(UN):
                    g = it * UN + u
                    pe.wait_ge(arrived[u], (it + 1) * 16)
                    reached(pe, s.copied, g - 1)
                    for j in range(GRP):
                        mm = pe.matmul(m.ps[u % 2][:, j * FQ:j * FQ + FQ], m.load[:, u, j, :], m.dft,
                                       start=True, stop=True)
                    mm.then_inc(s.first, 1)
            body(0)
            with pe.Fori(1, NG // UN) as it:
                body(it)
            pe.wait_ge(s.copied, NG)
            for r in range(rounds):
                reached(pe, s.scaled, r - 3)
                for j in range(per):
                    mm = pe.matmul(m.ps[4 + r % 4][:, j * FQ:j * FQ + FQ], m.half33[:, :, r * per + j], m.dft,
                                   start=True, stop=True)
                mm.then_inc(s.second, 1)

        @block.scalar
        def _(act):
            with act.Fori(0, NG // UN) as it:
                for u in range(UN):
                    g = it * UN + u
                    act.wait_ge(s.first, g + 1)
                    act.copy(m.half33[:, bass.ds(g * GRP, GRP), :],
                             m.ps[u % 2][:, 0:GRP * FQ].rearrange("p (t x) -> p t x", t=GRP)).then_inc(s.copied, 1)

        @block.vector
        def _(vec):
            c = Chain(vec, s.v)
            for r in range(rounds):
                vec.wait_ge(s.second, r + 1)
                vec.tensor_scalar(m.ft[:, r * per:r * per + per, :].rearrange("p x y -> p (x y)"),
                                  m.ps[4 + r % 4][:, 0:per * FQ], m.col[:, 0:1], None, ALU.mult)\
                    .then_inc(s.scaled, 1)
            vec.wait_ge(s.scaled, rounds)
            c.step(vec.tensor_scalar(m.ft[:, 0, 0:1], m.ft[:, 0, 0:1], m.col[:, 1:2], None, ALU.add))


def form_modes(vec, c, feat, modes, k):
    f = feat.rearrange("p (a x) (b y) -> p a x b y", a=2, b=2)
    cc, cs, sc, ss = (f[:, a, 0:K17, b, 0:K17] for a in (0, 1) for b in (0, 1))
    re, im = (modes[:, i].rearrange("p (r k) -> p r k", r=ROWS) for i in (0, 1))
    vec.tensor_tensor(re[:, 0:K17], cc, ss, ALU.subtract)
    vec.tensor_tensor(re[:, K17:ROWS], cc, ss, ALU.add)
    vec.tensor_tensor(im[:, K17:ROWS], sc, cs, ALU.subtract)
    c.step(vec.scalar_tensor_tensor(out=im[:, 0:K17], in0=sc, scalar=-1.0, in1=cs, op0=ALU.mult, op1=ALU.subtract))


def stage_modes(nc, held, m):
    s = semaphores(nc, held, "modes", "v modes weights high turned copied gram")
    R2 = 2.0 ** 0.5
    wt = m.weff.rearrange("p c (r k) -> p c r k", r=ROWS)
    jobs = []
    for k, (m0, n) in enumerate(MT):
        jobs += [(m.weff[:, cpt, m0:m0 + n], n, m.wT[0:n, k, cpt, :], 64, 'weights') for cpt in (0, 1)]
    for k, (m0, n) in enumerate(MT):
        jobs += [(m.modes[:, cpt, m0:m0 + n], n, m.modesT[0:n, k, cpt, :], P, 'modes') for cpt in (0, 1)]
    banks = [jobs[i:i + 2] for i in range(0, len(jobs), 2)]
    hbanks = [list(range(i, min(HC, i + 4))) for i in range(0, HC, 4)]
    NBK = 6

    with nc.Block() as block:
        @block.vector
        def _(vec):
            c = Chain(vec, s.v)
            wre, wim = wt[:, 0], wt[:, 1]
            vec.tensor_copy(wre, m.wraw[:, :, :, 0])
            c.step(vec.tensor_copy(wim, m.wraw[:, :, :, 1]))
            pr, nr = wre[0:48, 1:9, 0], wre[0:48, K17 + 1:K17 + 9, 0]
            pi, ni = wim[0:48, 1:9, 0], wim[0:48, K17 + 1:K17 + 9, 0]
            even, odd = m.spare[0:48, 0:8], m.spare[0:48, 8:16]
            vec.tensor_tensor(even, pr, nr, ALU.add)
            c.step(vec.tensor_tensor(odd, pi, ni, ALU.subtract))
            vec.tensor_scalar(pr, even, 0.5, None, ALU.mult)
            vec.tensor_scalar(nr, even, 0.5, None, ALU.mult)
            vec.tensor_scalar(pi, odd, 0.5, None, ALU.mult)
            vec.tensor_scalar(ni, odd, -0.5, None, ALU.mult)
            c.step(vec.memset(wim[0:48, 0:1, 0], 0.0))
            vec.drain().then_inc(s.weights, 1)
            form_modes(vec, c, m.ft, m.modes, K33)
            vec.drain().then_inc(s.modes, 1)
            h, f = m.hg.rearrange("p (x y) -> p x y", x=FQ), m.ft
            c.step(vec.tensor_scalar(m.hg, m.ft.rearrange("p x y -> p (x y)"), 2.0, None, ALU.mult))
            c.step(vec.tensor_scalar(h[:, :, 0:K33:32], f[:, :, 0:K33:32], R2, None, ALU.mult))
            c.step(vec.tensor_scalar(h[:, 0, :], f[:, 0, :], R2, None, ALU.mult))
            c.step(vec.tensor_copy(h[:, 0, 0:K33:32], f[:, 0, 0:K33:32]))
            c.step(vec.memset(h[:, 32:66:33, :], 0.0))
            a1, a2, a3, a4 = (m.spare[:, 16 + 32 * i:48 + 32 * i] for i in range(4))
            vec.tensor_tensor(a1, f[:, 32, 1:33], f[:, 65, 34:66], ALU.add)
            c.step(vec.tensor_tensor(a2, f[:, 65, 1:33], f[:, 32, 34:66], ALU.subtract))
            vec.tensor_scalar(h[:, 32, 1:32], a1[:, 0:31], R2, None, ALU.mult)
            vec.tensor_scalar(h[:, 65, 1:32], a2[:, 0:31], R2, None, ALU.mult)
            vec.tensor_copy(h[:, 32, 0:1], f[:, 32, 0:1])
            vec.tensor_copy(h[:, 32, 32:33], a1[:, 31:32])
            hv = m.hg.rearrange("p (x b y) -> p x b y", x=FQ, b=2)
            vec.memset(hv[:, 0:9, :, 0:9], 0.0)
            vec.memset(hv[:, K33:K33 + 9, :, 0:9], 0.0)
            vec.tensor_tensor(a3[:, 0:8], f[:, 8, 1:9], f[:, 41, 34:42], ALU.subtract)
            c.step(vec.tensor_tensor(a4[:, 0:8], f[:, 41, 1:9], f[:, 8, 34:42], ALU.add))
            vec.tensor_scalar(h[:, 8, 1:9], a3[:, 0:8], R2, None, ALU.mult)
            vec.tensor_scalar(h[:, 41, 1:9], a4[:, 0:8], R2, None, ALU.mult)
            c.step(vec.memset(h[:, :, 65:66], 0.0))
            vec.drain().then_inc(s.high, 1)
            vec.wait_ge(s.gram, 1)
            for b in range(NB):
                q = slice(NT * b, NT * b + NT)
                vec.tensor_copy(m.gram[q, :], m.ps[7][q, NT * b:NT * b + NT])

        @block.tensor
        def _(pe):
            for i, bank in enumerate(banks):
                if i == 0:
                    pe.wait_ge(s.weights, 1)
                if bank[0][4] == 'modes':
                    pe.wait_ge(s.modes, 1)
                reached(pe, s.copied, i - NBK + 1)
                for j, (src, n, _, wide, _) in enumerate(bank):
                    mm = pe.transpose(m.ps[i % NBK][0:n, j * P:j * P + wide], src, m.ident[0:wide, 0:wide])
                mm.then_inc(s.turned, 1)
            pe.wait_ge(s.high, 1)
            for r, cs in enumerate(hbanks):
                i = len(banks) + r
                reached(pe, s.copied, i - NBK + 1)
                for j, k in enumerate(cs):
                    mm = pe.transpose(m.ps[i % NBK][:, j * P:j * P + P], m.hg[:, k * P:k * P + P], m.ident)
                mm.then_inc(s.turned, 1)
            for k in range(HC):
                pe.wait_ge(s.copied, len(banks) + k // 4 + 1)
                mm = pe.matmul(m.ps[7][:, 0:P], m.gramT[:, k, :], m.gramT[:, k, :], start=(k == 0), stop=(k == HC - 1))
            mm.then_inc(s.gram, 1)

        @block.scalar
        def _(act):
            for i, bank in enumerate(banks):
                act.wait_ge(s.turned, i + 1)
                for j, (_, n, dst, wide, _) in enumerate(bank):
                    ins = act.copy(dst, m.ps[i % NBK][0:n, j * P:j * P + wide])
                ins.then_inc(s.copied, 1)
            for r, cs in enumerate(hbanks):
                i = len(banks) + r
                act.wait_ge(s.turned, i + 1)
                act.copy(m.gramT[:, cs[0]:cs[-1] + 1, :].rearrange("p c t -> p (c t)"),
                         m.ps[i % NBK][:, 0:P * len(cs)]).then_inc(s.copied, 1)


def stage_weights(nc, held, m):
    s = semaphores(nc, held, "weights", "v")
    w = weight_views(m)

    with nc.Block() as block:
        @block.vector
        def _(vec):
            c = Chain(vec, s.v)
            sk = m.skips
            n5 = len(MT)
            c.step(vec.tensor_tensor(w.sum, m.wT[:, :, 0, 0:48], over(sk[:, 0:48], 1, n5), ALU.add))
            qr, kr, vr = w.sum[:, :, 0:16], w.sum[:, :, 16:32], w.sum[:, :, 32:48]
            qi, ki, vi, pi = (m.wT[:, :, 1, 16 * i:16 * i + 16] for i in range(4))
            v0, pr = m.wT[:, :, 0, 32:48], m.wT[:, :, 0, 48:64]
            low = over(m.low, 2, HEADS)
            vec.tensor_tensor(w.t1, qr, kr, ALU.mult)
            vec.tensor_tensor(w.t2, qi, ki, ALU.mult)
            vec.tensor_tensor(w.t3, qi, kr, ALU.mult)
            c.step(vec.tensor_tensor(w.t4, qr, ki, ALU.mult))
            vec.tensor_tensor(w.t1, w.t1, w.t2, ALU.add)
            c.step(vec.tensor_tensor(w.t3, w.t3, w.t4, ALU.subtract))
            vec.tensor_tensor(w.ar, w.t1, low, ALU.mult)
            c.step(vec.tensor_tensor(w.ai, w.t3, low, ALU.mult))
            c.step(vec.tensor_scalar(w.an, w.ai, -1.0, None, ALU.mult))
            pw = over(sk[:, 48:64], 1, n5)
            vec.tensor_tensor(w.t1, v0, pw, ALU.mult)
            vec.tensor_tensor(w.t2, pr, vr, ALU.mult)
            vec.tensor_tensor(w.t3, pi, vi, ALU.mult)
            c.step(vec.tensor_tensor(w.t4, pr, pw, ALU.add))
            vec.tensor_tensor(w.t1, w.t1, w.t2, ALU.add)
            c.step(vec.tensor_tensor(w.t4, w.t4, vi, ALU.mult))
            vec.tensor_tensor(w.ur, w.t1, w.t3, ALU.subtract)
            c.step(vec.tensor_tensor(w.t2, pi, vr, ALU.mult))
            c.step(vec.tensor_tensor(w.ui, w.t4, w.t2, ALU.add))
            c.step(vec.tensor_tensor(w.t1[:, 0, :], pr[:, 0, :], sk[:, 48:64], ALU.add))
            c.step(vec.tensor_tensor(w.t1[:, 0, :], w.t1[:, 0, :], m.biases[:, 32:48], ALU.mult))
            c.step(vec.tensor_reduce(m.col[:, 8:9], w.t1[:, 0, :], AX.X, ALU.add))
            c.step(vec.tensor_tensor(m.col[:, 8:9], m.col[:, 8:9], m.sc[:, 16:17], ALU.add))
            c.step(vec.tensor_tensor(w.cg, sk[:, 0:16], sk[:, 16:32], ALU.mult))
            vec.tensor_scalar(w.cg, w.cg, 64.0, None, ALU.mult)
            c.step(vec.tensor_tensor(w.cm, sk[:, 32:48], sk[:, 48:64], ALU.mult))
            aq, ak = w.sum[0:1, 0, 0:16], w.sum[0:1, 0, 16:32]
            bq, bk = m.biases[0:1, 0:16], m.biases[0:1, 16:32]
            c.step(vec.scalar_tensor_tensor(out=w.r1[0:1], in0=aq, scalar=64.0, in1=bk, op0=ALU.mult, op1=ALU.mult))
            c.step(vec.scalar_tensor_tensor(out=w.r2[0:1], in0=ak, scalar=64.0, in1=bq, op0=ALU.mult, op1=ALU.mult))
            c.step(vec.scalar_tensor_tensor(out=w.r3[0:1], in0=bq, scalar=64.0, in1=bk, op0=ALU.mult, op1=ALU.mult))
            vec.tensor_copy(m.dcq, over(w.r1[0:1], 2, NT))
            c.step(vec.tensor_tensor(m.dck, over(m.modesT[0:1, 0, 0, :], 1, HEADS), over(w.r2[0:1], 2, P), ALU.mult))
            c.step(vec.tensor_tensor(m.dck, m.dck, over(w.r3[0:1], 2, P), ALU.add))
            c.step(vec.memset(w.one[0:1], 1.0))


def weight_views(m):
    w = Views()
    w.sum = m.wk[:, 0:240].rearrange("p (k h) -> p k h", k=5)
    big = [m.wk[:, 240 + 80 * i:320 + 80 * i].rearrange("p (k h) -> p k h", k=5) for i in range(9)]
    w.ar, w.ai, w.an, w.ur, w.ui, w.t1, w.t2, w.t3, w.t4 = big
    w.cg, w.cm = m.wk[:, 960:976], m.wk[:, 976:992]
    w.r1, w.mix = m.wk[:, 640:656], m.wk[:, 656:688]
    w.r2, w.r3, w.one = m.wk[:, 720:736], m.wk[:, 800:816], m.wk[:, 880:912]
    return w


def stage_scores(nc, held, m):
    s = semaphores(nc, held, "scores", "v a p0 p1 p2 p3 used done sub exp cleared probs turned copied mixed mixc")
    w = weight_views(m)
    ready = [s.p0, s.p1, s.p2, s.p3]
    left = [(w.ar, 0), (w.ai, 1), (w.ar, 1), (w.an, 0)]

    with nc.Block() as block:
        def operands(k, j):
            a, part = left[j]
            return over(m.modesT[:, k, part, :], 1, HEADS), over(a[:, k, :], 2, P)

        @block.vector
        def _(vec):
            c = Chain(vec, s.v)
            for k in range(LOWT):
                for j in (0, 1):
                    if k:
                        vec.wait_ge(s.used, 4 * (k - 1) + j + 1)
                    x, a = operands(k, j)
                    vec.tensor_tensor(m.prod[:, j], x, a, ALU.mult).then_inc(ready[j], 1)
            sh = [HEADS, NT]
            gram = over(m.gram, 1, HEADS)
            c.step(vec.tensor_tensor(m.score, gram, over(w.cg, 2, NT), ALU.mult))
            vec.wait_ge(s.done, 1)
            c.step(vec.tensor_tensor(m.score, m.ps[0][:, :].rearrange("p (h s) -> p h s", h=HEADS), m.score, ALU.add))
            c.step(vec.tensor_reduce(w.r1, m.score, AX.X, ALU.max))
            vec.tensor_tensor(m.score, m.score, over(w.r1, 2, NT), ALU.subtract).then_inc(s.sub, 1)
            vec.wait_ge(s.exp, 1)
            c.step(vec.tensor_reduce(w.r1, m.expo, AX.X, ALU.add))
            c.step(vec.reciprocal(w.r1, w.r1))
            c.step(vec.tensor_tensor(m.prob, m.expo, over(w.r1, 2, NT), ALU.mult))
            vec.wait_ge(s.cleared, 2)
            for b in range(NB):
                q = slice(NT * b, NT * b + NT)
                ins = vec.tensor_copy(m.probD[q, :, NT * b:NT * b + NT], m.prob[q])
            ins.then_inc(s.probs, 1)
            c.step(vec.tensor_tensor(m.score, m.prob, over(w.cm, 2, NT), ALU.mult))
            c.step(vec.tensor_reduce(w.mix, m.score.rearrange("p h s -> p s h"), AX.X, ALU.add))
            for b in range(NB):
                q = slice(NT * b, NT * b + NT)
                ins = vec.tensor_copy(m.mixD[q, NT * b:NT * b + NT], w.mix[q])
            ins.then_inc(s.probs, 1)
            vec.wait_ge(s.mixed, 1)
            c.step(vec.tensor_copy(m.mixT, m.ps[5][:, 0:P]))
            vec.scalar_tensor_tensor(out=m.mixA, in0=m.ps[5][:, 0:P], scalar=m.col[:, 0:1], in1=m.ident,
                                     op0=ALU.mult, op1=ALU.add).then_inc(s.mixc, 1)
            vec.wait_ge(s.mixed, 2)
            c.step(vec.tensor_copy(m.col[:, 9:10], m.ps[6][:, 0:1]))

        @block.gpsimd
        def _(pool):
            for k in range(LOWT):
                if k:
                    pool.wait_ge(s.used, 4 * (k - 1) + 3)
                x, a = operands(k, 2)
                pool.tensor_tensor(m.prod[:, 2], x, a, ALU.mult).then_inc(ready[2], 1)
            pool.wait_ge(s.done, 1)
            pool.memset(m.probD, 0.0).then_inc(s.cleared, 1)
            pool.memset(m.mixD, 0.0).then_inc(s.cleared, 1)

        @block.scalar
        def _(act):
            for k in range(LOWT):
                if k:
                    act.wait_ge(s.used, 4 * (k - 1) + 4)
                a, part = left[3]
                for h in range(HEADS):
                    ins = act.activation(m.prod[:, 3, h, :], m.modesT[:, k, part, :], ACT.Copy, scale=a[:, k, h:h + 1])
                ins.then_inc(ready[3], 1)
            act.wait_ge(s.sub, 1)
            act.activation(m.expo, m.score, ACT.Exp).then_inc(s.exp, 1)
            for i in range(4):
                act.wait_ge(s.turned, i + 1)
                act.copy(m.probT[:, 4 * i:4 * i + 4, :].rearrange("p h t -> p (h t)"), m.ps[1 + i][:, :])\
                    .then_inc(s.copied, 1)

        @block.tensor
        def _(pe):
            for k in range(LOWT):
                for j in range(4):
                    pe.wait_ge(ready[j], k + 1)
                    for b in range(NB):
                        q = slice(NT * b, NT * b + NT)
                        mm = pe.matmul(m.ps[0][q, :], m.modesT[:, k, j // 2, q], m.prod[:, j, :, q],
                                       start=(k == 0 and j == 0), stop=False)
                    mm.then_inc(s.used, 1)
            for b in range(NB):
                q = slice(NT * b, NT * b + NT)
                pe.matmul(m.ps[0][q, :], m.modesT[0:1, 0, 0, q], m.dcq, start=False, stop=False)
                mm = pe.matmul(m.ps[0][q, :], w.one[0:1], m.dck[:, :, q], start=False, stop=True)
            mm.then_inc(s.done, 1)
            pe.wait_ge(s.probs, 1)
            for h in range(HEADS):
                mm = pe.transpose(m.ps[1 + h // 4][:, (h % 4) * P:(h % 4) * P + P], m.probD[:, h, :], m.ident)
                if h % 4 == 3:
                    mm.then_inc(s.turned, 1)
            pe.wait_ge(s.probs, 2)
            pe.transpose(m.ps[5][:, 0:P], m.mixD, m.ident).then_inc(s.mixed, 1)
            pe.wait_ge(s.mixc, 1)
            pe.matmul(m.ps[6][:, 0:1], m.mixT, m.col[:, 1:2], start=True, stop=True).then_inc(s.mixed, 1)


def stage_mix(nc, held, m, mix):
    s = semaphores(nc, held, "mix", "v mixed added stored xm used summed free reduced dc turned copied coef")
    w = weight_views(m)
    NCH = PIX // 512
    steps = [(k, q) for k in range(len(MT)) for q in range(4)]
    a = m.a[:, :, :].rearrange("p a b -> p (a b)")

    with nc.Block() as block:
        @block.tensor
        def _(pe):
            def body(it):
                for u in range(4):
                    i = it * 4 + u
                    reached(pe, s.added, i - 3)
                    pe.matmul(m.ps[u][:, :], m.mixA, a[:, bass.ds(i * 512, 512)], start=True, stop=True)\
                        .then_inc(s.mixed, 1)
            body(0)
            with pe.Fori(1, NCH // 4) as it:
                body(it)
            for i, (k, q) in enumerate(steps):
                m0, n = MT[k]
                if i < 2:
                    pe.wait_ge(s.added, NCH)
                reached(pe, s.used, i - 2)
                for part in (0, 1):
                    mm = pe.matmul(m.ps[2 * (i % 3) + part][0:n, :], m.modes[:, part, m0:m0 + n],
                                   m.probT[:, 4 * q:4 * q + 4, :], start=True, stop=True)
                mm.then_inc(s.xm, 1)
            for k, (m0, n) in enumerate(MT):
                pe.wait_ge(s.reduced, k + 1)
                if k == 0:
                    pe.wait_ge(s.dc, 1)
                    pe.wait_ge(s.used, len(steps))
                reached(pe, s.copied, k - 2)
                for part in (0, 1):
                    mm = pe.transpose(m.ps[k % 3][:, part * P:part * P + n], m.modesT[0:n, k, part, :], m.ident[0:n, 0:n])
                mm.then_inc(s.turned, 1)
            turn_coefficients(pe, m, s, len(MT))

        @block.scalar
        def _(act):
            for k, (m0, n) in enumerate(MT):
                act.wait_ge(s.turned, k + 1)
                src = m.ps[k % 3][:, 0:2 * P].rearrange("p (c n) -> p c n", c=2)[:, :, 0:n]
                act.copy(m.modes[:, :, m0:m0 + n], src).then_inc(s.copied, 1)
            copy_coefficients(act, m, s, len(MT))

        @block.sync
        def _(sp):
            sp.wait_ge(s.added, NCH)
            for q in range(4):
                sp.dma_start(mix[:, 32 * q:32 * q + 32, :], m.a[:, 32 * q:32 * q + 32, :]).then_inc(s.stored, 16)
            sp.wait_ge(s.stored, 64)

        @block.vector
        def _(vec):
            c = Chain(vec, s.v)
            with vec.Fori(0, NCH // 4) as it:
                for u in range(4):
                    i = it * 4 + u
                    vec.wait_ge(s.mixed, i + 1)
                    vec.tensor_scalar(a[:, bass.ds(i * 512, 512)], m.ps[u][:, :], m.col[:, 9:10], None, ALU.add)\
                        .then_inc(s.added, 1)
            for i, (k, q) in enumerate(steps):
                n = MT[k][1]
                vec.wait_ge(s.xm, i + 1)
                reached(vec, s.summed, i - 1)
                for j, (part, u) in enumerate([(0, w.ur), (1, w.ui), (0, w.ui), (1, w.ur)]):
                    src = m.ps[2 * (i % 3) + part][0:n, :].rearrange("p (h t) -> p h t", h=4)
                    ins = vec.tensor_tensor(m.zprod[0:n, i % 2, j], src, over(u[0:n, k, 4 * q:4 * q + 4], 2, P), ALU.mult)
                ins.then_inc(s.used, 1)
                if q == 3:
                    vec.wait_ge(s.summed, i + 1)
                    for part in (0, 1):
                        ins = vec.tensor_reduce(m.modesT[0:n, k, part, :], m.zsum[0:n, part].rearrange("p h t -> p t h"),
                                                AX.X, ALU.add)
                    ins.then_inc(s.reduced, 1)
            vec.wait_ge(s.reduced, len(MT))
            vec.tensor_scalar(m.modesT[0:1, 0, 0, :], m.modesT[0:1, 0, 0, :], m.col[0:1, 8:9], None, ALU.add)\
                .then_inc(s.dc, 1)
            vec.wait_ge(s.copied, len(MT))
            form_coefficients(vec, m, m.modes[:, 0], m.modes[:, 1])
            vec.drain().then_inc(s.coef, 1)

        @block.gpsimd
        def _(pool):
            for i, (k, q) in enumerate(steps):
                n = MT[k][1]
                pool.wait_ge(s.used, i + 1)
                if q == 0:
                    reached(pool, s.reduced, k)
                pool.tensor_tensor(m.zsum[0:n, 0, 4 * q:4 * q + 4], m.zprod[0:n, i % 2, 0], m.zprod[0:n, i % 2, 1], ALU.subtract)
                pool.tensor_tensor(m.zsum[0:n, 1, 4 * q:4 * q + 4], m.zprod[0:n, i % 2, 2], m.zprod[0:n, i % 2, 3], ALU.add)\
                    .then_inc(s.summed, 1)


def form_coefficients(vec, m, re, im):
    g = m.coef.rearrange("p (a x) (b y) -> p a x b y", a=2, b=2)
    re, im = (v.rearrange("p (r k) -> p r k", r=ROWS) for v in (re, im))
    rp, rn, ip, im_ = re[:, 0:K17], re[:, K17:ROWS], im[:, 0:K17], im[:, K17:ROWS]
    vec.tensor_tensor(g[:, 0, :, 0], rp, rn, ALU.add)
    vec.tensor_tensor(g[:, 1, :, 1], rn, rp, ALU.subtract)
    vec.tensor_tensor(g[:, 1, :, 0], im_, ip, ALU.subtract)
    return vec.scalar_tensor_tensor(out=g[:, 0, :, 1], in0=ip, scalar=-1.0, in1=im_, op0=ALU.mult, op1=ALU.subtract)


COEF_BANKS = [list(range(i, min(FM, i + 4))) for i in range(0, FM, 4)]


def turn_coefficients(pe, m, s, base):
    pe.wait_ge(s.coef, 1)
    for r, xs in enumerate(COEF_BANKS):
        if r > 2:
            pe.wait_ge(s.copied, base + r - 2)
        for j, xf in enumerate(xs):
            mm = pe.transpose(m.ps[3 + r % 3][0:FM, j * P:j * P + P], m.coef[:, xf, :], m.ident)
        mm.then_inc(s.turned, 1)


def copy_coefficients(act, m, s, base):
    for r, xs in enumerate(COEF_BANKS):
        act.wait_ge(s.turned, base + r + 1)
        act.copy(m.coefT[:, xs[0]:xs[-1] + 1, :].rearrange("p x t -> p (x t)"),
                 m.ps[3 + r % 3][0:FM, 0:P * len(xs)]).then_inc(s.copied, 1)


def sweep(eng, step, lag):
    for u in range(UN):
        step(u, u)
    with eng.Fori(1, NG // UN) as it:
        for u in range(UN):
            step(it * UN + u, u)
    for u in range(lag):
        step(NG + u, u)


def live(g):
    return not isinstance(g, int) or 0 <= g < NG


def group(images, g):
    return images[:, bass.ds(g * GRP, GRP), :]


def banked(m, bank):
    return m.ps[bank][:, :].rearrange("p (t w) -> p t w", t=GRP)


def stage_inverse(nc, held, m, kind, mix=None, ins=None):
    s = semaphores(nc, held, "inverse_" + kind, "in0 in1 in2 in3 staged cols colsc rows used stats "
                   "lin pre ready saved first copied weights")
    arrived = [s.in0, s.in1, s.in2, s.in3]
    dest = m.a if kind == 'mix2' else m.b

    with nc.Block() as block:
        @block.sync
        def _(sp):
            if kind == 'proj':
                mix_img = mix.rearrange("t h w -> h t w")

                def load(t, u):
                    reached(sp, s.used, t - UN + 1)
                    sp.dma_start(group(m.b, t), mix_img[:, bass.ds(t * GRP, GRP), :]).then_inc(arrived[u], 16)
                sweep(sp, load, 0)
            if kind == 'mix1':
                load_mixer(sp, m, ins, 2, s.weights)
                sp.wait_ge(s.weights, 32)

        @block.gpsimd
        def _(pool):
            pool.memset(m.stage[:, :, GRP * FM:], 0.0)

            def step(t, u):
                if live(t):
                    reached(pool, s.cols, t - 1)
                    pool.tensor_copy(m.stage[0:FM, u % 2, 0:GRP * FM].rearrange("p (t x) -> p t x", t=GRP),
                                     m.coefT[:, :, bass.ds(t * GRP, GRP)].rearrange("p x t -> p t x"))\
                        .then_inc(s.staged, 1)
                g = t - 2
                if kind == 'mix1' and live(g):
                    pool.wait_ge(s.ready, g + 1)
                    pool.tensor_copy(group(m.a, g), m.ust[:, u % 2]).then_inc(s.saved, 1)
            sweep(pool, step, 2 if kind == 'mix1' else 0)

        @block.tensor
        def _(pe):
            def step(t, u):
                if live(t):
                    pe.wait_ge(s.staged, t + 1)
                    reached(pe, s.colsc, t - 1)
                    for j in range(GRP):
                        mm = pe.matmul(m.ps[u % 2][:, j * NW:j * NW + NW],
                                       m.stage[0:FM, u % 2, j * FM:j * FM + P], m.cols, start=True, stop=True)
                    mm.then_inc(s.cols, 1)
                g = t - 1
                if live(g):
                    pe.wait_ge(s.colsc, g + 1)
                    reached(pe, s.pre if kind == 'mix1' else s.used, g - 1)
                    pe.matmul(m.ps[2 + (u - 1) % 2][:, :], m.rows, m.half[0:FM, (u - 1) % 2, :], start=True, stop=True)\
                        .then_inc(s.rows, 1)
                g = t - 3
                if kind == 'mix1' and live(g):
                    pe.wait_ge(s.ready, g + 1)
                    reached(pe, s.copied, g - 1)
                    for j in range(GRP):
                        mm = pe.matmul(m.ps[4 + (u - 3) % 2][:, j * FM:j * FM + FM], m.ust[:, (u - 3) % 2, j, :],
                                       m.dft17, start=True, stop=True)
                    mm.then_inc(s.first, 1)
            sweep(pe, step, 3 if kind == 'mix1' else 1)

        @block.scalar
        def _(act):
            def step(t, u):
                if live(t):
                    act.wait_ge(s.cols, t + 1)
                    reached(act, s.rows, t - 1)
                    act.copy(m.half[0:FM, u % 2, :], m.ps[u % 2][0:FM, :]).then_inc(s.colsc, 1)
                g = t - 2
                if kind == 'mix1' and live(g):
                    act.wait_ge(s.pre, g + 1)
                    reached(act, s.first, g - 1)
                    reached(act, s.saved, g - 1)
                    act.activation(m.ust[:, u % 2], m.tmp[:, u % 2], ACT.Gelu).then_inc(s.ready, 1)
                g = t - 3
                if kind == 'mix1' and live(g):
                    act.wait_ge(s.first, g + 1)
                    act.copy(m.half17[:, bass.ds(g * GRP, GRP), :],
                             m.ps[4 + (u - 3) % 2][:, 0:GRP * FM].rearrange("p (t x) -> p t x", t=GRP))\
                        .then_inc(s.copied, 1)
            sweep(act, step, 3 if kind == 'mix1' else 0)

        @block.vector
        def _(vec):
            def step(t, u, it):
                if kind == 'mix1' and live(t):
                    reached(vec, s.ready, t - 1)
                    for j in range(GRP):
                        img = t * GRP + j
                        e = vec.tensor_scalar(m.tmp[:, u % 2, j, :], m.b[:, bass.ds(img, 1), :],
                                              m.aff[:, 4, bass.ds(img, 1)], m.aff[:, 5, bass.ds(img, 1)],
                                              ALU.mult, ALU.add)
                    e.then_inc(s.lin, 1)
                g = t - 1
                if live(g):
                    if kind != 'mix1':
                        reached(vec, s.used, g)
                    vec.wait_ge(s.rows, g + 1)
                    y = banked(m, 2 + (u - 1) % 2)
                    if kind == 'proj':
                        vec.wait_ge(arrived[(u - 1) % UN], (it + (1 if u else 0)) * 16)
                        vec.tensor_tensor(group(m.b, g), group(m.b, g), y, ALU.add).then_inc(s.used, 1)
                    elif kind == 'mix1':
                        vec.wait_ge(s.lin, g + 1)
                        vec.tensor_tensor(m.tmp[:, (u - 1) % 2], m.tmp[:, (u - 1) % 2], y, ALU.add).then_inc(s.pre, 1)
                    else:
                        vec.scalar_tensor_tensor(out=group(m.a, g), in0=group(m.a, g), scalar=m.sc[:, 10:11], in1=y,
                                                 op0=ALU.mult, op1=ALU.add).then_inc(s.used, 1)
                g = t - 2
                if kind != 'mix1' and live(g):
                    if isinstance(g, int) and g == NG - 1:
                        vec.wait_ge(s.used, NG)
                    for j in range(GRP):
                        img = g * GRP + j
                        vec.bn_stats(m.stat[:, bass.ds(img, 1), :], dest[:, bass.ds(img, 1), :])

            for u in range(UN):
                step(u, u, 0)
            with vec.Fori(1, NG // UN) as it:
                for u in range(UN):
                    step(it * UN + u, u, it)
            for u in range(2):
                step(NG + u, u, NG // UN)


def stage_factors(nc, held, m, kind):
    s = semaphores(nc, held, "factors_" + kind, "v ones sums summed added rooted")
    half = m.spare[:, 128:2176]
    ones, total, mean, var = m.spare[:, 0:P], half[:, 0:128], half[:, 128:256], half[:, 256:384]
    root, root2, t = half[:, 384:512], half[:, 512:640], half[:, 640:768]
    dev = half[:, 768:1024].rearrange("p (t k) -> p t k", k=2)
    sc1, bi1, sc2, bi2, sa, sb = (m.aff[:, i, :] for i in range(6))

    def scalar(i):
        return m.sc[:, i:i + 1]

    with nc.Block() as block:
        @block.tensor
        def _(pe):
            pe.wait_ge(s.ones, 1)
            for i, src in enumerate([total, t]):
                pe.wait_ge(s.sums, i + 1)
                pe.matmul(m.ps[i][:, 0:P], ones, src, start=True, stop=True).then_inc(s.summed, 1)

        @block.scalar
        def _(act):
            for i, (dst, src) in enumerate([(root, var), (root2, t)][:2 if kind == 'proj' else 1]):
                act.wait_ge(s.added, i + 1)
                act.activation(dst, src if i else root, ACT.Sqrt).then_inc(s.rooted, 1)

        @block.vector
        def _(vec):
            c = Chain(vec, s.v)
            vec.memset(ones, 1.0).then_inc(s.ones, 1)
            vec.tensor_tensor(total, m.stat[:, :, 1], m.stat[:, :, 4], ALU.add).then_inc(s.sums, 1)
            vec.wait_ge(s.summed, 1)
            c.step(vec.tensor_scalar(mean, m.ps[0][:, 0:P], 1.0 / (2 * P), None, ALU.mult))
            c.step(vec.tensor_tensor(dev, m.stat[:, :, 1::3], over(mean, 2, 2), ALU.subtract))
            c.step(vec.tensor_tensor(dev, dev, dev, ALU.mult))
            c.step(vec.tensor_tensor(t, dev[:, :, 0], dev[:, :, 1], ALU.add))
            c.step(vec.tensor_tensor(var, m.stat[:, :, 2], m.stat[:, :, 5], ALU.add))
            vec.scalar_tensor_tensor(out=t, in0=t, scalar=float(NW // 2), in1=var, op0=ALU.mult, op1=ALU.add)\
                .then_inc(s.sums, 1)
            vec.wait_ge(s.summed, 2)
            c.step(vec.tensor_scalar(var, m.ps[1][:, 0:P], 1.0 / PIX, None, ALU.mult))
            vec.tensor_scalar(root, var, EPS, None, ALU.add).then_inc(s.added, 1)
            vec.wait_ge(s.rooted, 1)
            g, b = (2, 3) if kind == 'proj' else (14, 15)
            c.step(vec.reciprocal(root, root))
            c.step(vec.tensor_scalar(sc1, root, scalar(g), None, ALU.mult))
            c.step(vec.tensor_tensor(t, mean, sc1, ALU.mult))
            c.step(vec.tensor_scalar(bi1, t, -1.0, scalar(b), ALU.mult, ALU.add))
            if kind == 'proj':
                c.step(vec.tensor_tensor(t, sc1, sc1, ALU.mult))
                c.step(vec.tensor_tensor(t, t, var, ALU.mult))
                vec.tensor_scalar(t, t, EPS, None, ALU.add).then_inc(s.added, 1)
                vec.wait_ge(s.rooted, 2)
                c.step(vec.reciprocal(root2, root2))
                c.step(vec.tensor_scalar(sc2, root2, scalar(4), None, ALU.mult))
                c.step(vec.tensor_scalar(t, sc2, scalar(3), None, ALU.mult))
                c.step(vec.tensor_scalar(bi2, t, -1.0, scalar(5), ALU.mult, ALU.add))
                vec.tensor_scalar(sa, sc2, scalar(6), None, ALU.mult)
                vec.tensor_scalar(sb, bi2, scalar(6), None, ALU.mult)


def stage_attended(nc, held, m):
    s = semaphores(nc, held, "attended", "normed staged first copied")

    with nc.Block() as block:
        @block.vector
        def _(vec):
            def step(t, u):
                if live(t):
                    for j in range(GRP):
                        img = bass.ds(t * GRP + j, 1)
                        e = vec.tensor_scalar(m.b[:, img, :], m.b[:, img, :], m.aff[:, 0, img], m.aff[:, 1, img],
                                              ALU.mult, ALU.add)
                    e.then_inc(s.normed, 1)
                g = t - 2
                if live(g):
                    vec.wait_ge(s.first, g + 1)
                    vec.tensor_copy(m.half17[:, bass.ds(g * GRP, GRP), :],
                                    m.ps[u % 2][:, 0:GRP * FM].rearrange("p (t x) -> p t x", t=GRP))\
                        .then_inc(s.copied, 1)
            sweep(vec, step, 2)

        @block.scalar
        def _(act):
            def step(t, u):
                act.wait_ge(s.normed, t + 1)
                reached(act, s.first, t - 1)
                for j in range(GRP):
                    img = bass.ds(t * GRP + j, 1)
                    e = act.activation(m.ust[:, u % 2, j, :], m.b[:, img, :].rearrange("p a w -> p (a w)"), ACT.Identity,
                                       scale=m.aff[:, 2, img], bias=m.aff[:, 3, img])
                e.then_inc(s.staged, 1)
            sweep(act, step, 0)

        @block.tensor
        def _(pe):
            def step(t, u):
                pe.wait_ge(s.staged, t + 1)
                reached(pe, s.copied, t - 1)
                for j in range(GRP):
                    mm = pe.matmul(m.ps[u % 2][:, j * FM:j * FM + FM], m.ust[:, u % 2, j, :], m.dft17,
                                   start=True, stop=True)
                mm.then_inc(s.first, 1)
            sweep(pe, step, 0)


def stage_mixer(nc, held, m, i):
    s = semaphores(nc, held, f"mixer{i}", "v second added rooted coef turned copied")
    rounds = [(0, 12), (12, 24), (24, 34)]
    zr, zi, t1, t2 = (m.spare[:, NM * k:NM * k + NM] for k in range(4))
    wide = m.spare[:, 4 * NM:4 * NM + FM * FM]
    prod = m.spare[:, 0:FM * FM]
    k0 = 6 if i == 1 else 10
    var, root, fac, con = (m.col[:, 16 + j:17 + j] for j in range(4))

    with nc.Block() as block:
        @block.tensor
        def _(pe):
            for r, (lo, hi) in enumerate(rounds):
                for xf in range(lo, hi):
                    mm = pe.matmul(m.ps[r][:, (xf - lo) * FM:(xf - lo) * FM + FM], m.half17[:, :, xf], m.dft17,
                                   start=True, stop=True)
                mm.then_inc(s.second, 1)
            turn_coefficients(pe, m, s, 0)

        @block.scalar
        def _(act):
            act.wait_ge(s.added, 1)
            act.activation(root, var, ACT.Sqrt).then_inc(s.rooted, 1)
            copy_coefficients(act, m, s, 0)

        @block.vector
        def _(vec):
            c = Chain(vec, s.v)
            for r, (lo, hi) in enumerate(rounds):
                vec.wait_ge(s.second, r + 1)
                e = vec.tensor_copy(m.feat[:, lo:hi, :].rearrange("p x y -> p (x y)"), m.ps[r][:, 0:(hi - lo) * FM])
                if r == 2:
                    c.step(e)
            form_modes(vec, c, m.feat, m.modes, K17)
            wr, wi = (m.mixw[:, :, :, k].rearrange("p r k -> p (r k)") for k in (0, 1))
            xr, xi = m.modes[:, 0], m.modes[:, 1]
            vec.tensor_tensor(zr, xr, wr, ALU.mult)
            vec.tensor_tensor(t1, xi, wi, ALU.mult)
            vec.tensor_tensor(zi, xr, wi, ALU.mult)
            c.step(vec.tensor_tensor(t2, xi, wr, ALU.mult))
            vec.tensor_tensor(zr, zr, t1, ALU.subtract)
            c.step(vec.tensor_tensor(zi, zi, t2, ALU.add))
            c.step(form_coefficients(vec, m, zr, zi))
            g = m.coef.rearrange("p x y -> p (x y)")
            c.step(vec.tensor_tensor(wide, g, m.var, ALU.mult))
            c.step(vec.tensor_tensor_reduce(prod, wide, g, 1.0, 0.0, ALU.mult, ALU.add, var))
            vec.tensor_scalar(var, var, EPS, None, ALU.add).then_inc(s.added, 1)
            vec.wait_ge(s.rooted, 1)
            c.step(vec.reciprocal(root, root))
            c.step(vec.tensor_tensor(fac, root, m.sc[:, k0 + 2:k0 + 3], ALU.mult))
            c.step(vec.tensor_tensor(con, m.sc[:, k0 + 1:k0 + 2], m.sc[:, k0 + 3:k0 + 4], ALU.add))
            c.step(vec.tensor_scalar(g, g, fac, None, ALU.mult))
            vec.tensor_copy(g[:, 0:1], con).then_inc(s.coef, 1)


def stage_residual(nc, held, m, ins):
    s = semaphores(nc, held, "residual", "in0 in1 in2 in3 normed partly whole")
    arrived = [s.in0, s.in1, s.in2, s.in3]
    x_img = ins['x'].rearrange("b t h w -> h (b t) w")
    load = m.spare[:, 0:4 * 512].rearrange("p (s t w) -> p s t w", s=4, t=GRP)

    with nc.Block() as block:
        @block.sync
        def _(sp):
            def body(it):
                for u in range(UN):
                    g = it * UN + u
                    reached(sp, s.whole, g - UN + 1)
                    sp.dma_start(load[:, u], x_img[:, bass.ds(g * GRP, GRP), :]).then_inc(arrived[u], 16)
            body(0)
            with sp.Fori(1, NG // UN) as it:
                body(it)

        @block.scalar
        def _(act):
            def step(t, u):
                for j in range(GRP):
                    img = bass.ds(t * GRP + j, 1)
                    a = m.a[:, img, :].rearrange("p a w -> p (a w)")
                    e = act.activation(a, a, ACT.Identity, scale=m.aff[:, 0, img], bias=m.aff[:, 1, img])
                e.then_inc(s.normed, 1)
            sweep(act, step, 0)

        @block.gpsimd
        def _(pool):
            def body(it):
                for u in range(UN):
                    g = it * UN + u
                    pool.wait_ge(arrived[u], (it + 1) * 16)
                    pool.tensor_tensor(group(m.b, g), group(m.b, g), load[:, u], ALU.add).then_inc(s.partly, 1)
            with pool.Fori(0, NG // UN) as it:
                body(it)

        @block.vector
        def _(vec):
            def step(t, u):
                if live(t):
                    reached(vec, s.whole, t)
                    vec.wait_ge(s.normed, t + 1)
                    vec.wait_ge(s.partly, t + 1)
                    vec.tensor_tensor(group(m.b, t), group(m.b, t), group(m.a, t), ALU.add).then_inc(s.whole, 1)
                g = t - 1
                if live(g):
                    if isinstance(g, int) and g == NG - 1:
                        vec.wait_ge(s.whole, NG)
                    for j in range(GRP):
                        img = bass.ds(g * GRP + j, 1)
                        vec.bn_stats(m.stat[:, img, :], m.b[:, img, :])
            sweep(vec, step, 1)



def row_factors(vec, c, st, fac, factor, rooted):
    mean, dev, t, q = (fac[:, i, :] for i in range(4))
    vec.tensor_tensor(t, st[:, :, 1], st[:, :, 4], ALU.add)
    c.step(vec.tensor_tensor(dev, st[:, :, 1], st[:, :, 4], ALU.subtract))
    vec.tensor_scalar(mean, t, 0.5, None, ALU.mult)
    c.step(vec.tensor_scalar(dev, dev, 0.5, None, ALU.mult))
    c.step(vec.tensor_tensor(dev, dev, dev, ALU.mult))
    c.step(vec.tensor_tensor(q, st[:, :, 2], st[:, :, 5], ALU.add))
    c.step(vec.scalar_tensor_tensor(out=dev, in0=q, scalar=1.0 / D, in1=dev, op0=ALU.mult, op1=ALU.add))
    vec.tensor_scalar(dev, dev, EPS, None, ALU.add).then_inc(factor, 1)
    vec.wait_ge(rooted, 1)
    c.step(vec.reciprocal(dev, dev))


def stage_normed(nc, held, m, ins):
    s = semaphores(nc, held, "normed", "v loaded turned mapsc maps done rooted factor staged turnedr copied scaled units")
    names = ['L1_attn_rotation_params', 'L1_attn_entangle_params', 'L1_attn_Wq', 'L1_attn_Wk', 'L1_attn_Wv']
    raw = m.scratch[:, 0:640].rearrange("p (k d) -> p k d", k=5)
    rawT = m.scratch[:, 640:1280].rearrange("p (k d) -> p k d", k=5)
    fac = m.scratch[:, 1280:1280 + 4 * NI].rearrange("p (k t) -> p k t", k=4)
    ln = m.scratch[:, 1792:2816].rearrange("p (s t w) -> p s t w", s=2, t=GRP)
    diag, unit = m.scratch[:, 2816:2944], m.scratch[:, 2944:2948]

    with nc.Block() as block:
        @block.sync
        def _(sp):
            for i, n in enumerate(names):
                src = ins[n]
                if len(src.shape) == 1:
                    src = src.rearrange("(d e) -> d e", d=D)
                sp.dma_start(raw[:, i, :], src).then_inc(s.loaded, 16)

        @block.tensor
        def _(pe):
            pe.wait_ge(s.loaded, 80)
            pe.wait_ge(s.scaled, 1)
            pe.matmul(m.ps[7][:, 0:D], m.halves[:, :], diag, start=True, stop=True).then_inc(s.units, 1)
            for i in range(5):
                mm = pe.transpose(m.ps[4 + i // 4][:, (i % 4) * D:(i % 4) * D + D], raw[:, i, :], m.ident)
            mm.then_inc(s.turned, 1)
            pe.wait_ge(s.mapsc, 1)
            for i in (0, 1):
                mm = pe.matmul(m.ps[6][:, i * D:i * D + D], rawT[:, i, :], rawT[:, 2 + i, :], start=True, stop=True)
            mm.then_inc(s.maps, 1)

            def step(t, u):
                pe.wait_ge(s.staged, t + 1)
                reached(pe, s.copied, t - 1)
                for j in range(GRP):
                    mm = pe.transpose(m.ps[u % 2][:, j * P:j * P + P], ln[:, u % 2, j, :], m.ident)
                mm.then_inc(s.turnedr, 1)
            sweep(pe, step, 0)

        @block.scalar
        def _(act):
            act.wait_ge(s.factor, 1)
            act.activation(fac[:, 1], fac[:, 1], ACT.Sqrt).then_inc(s.rooted, 1)

            def step(t, u):
                act.wait_ge(s.turnedr, t + 1)
                act.copy(group(m.a, t), banked(m, u % 2)).then_inc(s.copied, 1)
            sweep(act, step, 0)

        @block.vector
        def _(vec):
            c = Chain(vec, s.v)
            row_factors(vec, c, m.stat, fac, s.factor, s.rooted)
            vec.memset(m.halves[:, :], 0.5)
            vec.memset(m.v[:, :, D:D + 1], 1.0)
            vec.wait_ge(s.loaded, 80)
            vec.tensor_reduce(unit[:, 0:1], raw[:, 4, :], AX.X, ALU.max)
            c.step(vec.tensor_reduce(unit[:, 1:2], raw[:, 4, :], AX.X, ALU.min))
            c.step(vec.scalar_tensor_tensor(out=unit[:, 2:3], in0=unit[:, 1:2], scalar=-1.0, in1=unit[:, 0:1],
                                            op0=ALU.mult, op1=ALU.max))
            c.step(vec.tensor_scalar(unit[:, 2:3], unit[:, 2:3], 1e-30, None, ALU.max))
            c.step(vec.reciprocal(unit[:, 3:4], unit[:, 2:3]))
            vec.tensor_scalar(diag, m.ident, unit[:, 2:3], None, ALU.mult)
            vec.tensor_scalar(raw[:, 4, :], raw[:, 4, :], unit[:, 3:4], None, ALU.mult).then_inc(s.scaled, 1)
            vec.wait_ge(s.units, 1)
            vec.tensor_scalar(m.unit[:, :], m.ps[7][:, 0:D], 2.0, None, ALU.mult)
            vec.wait_ge(s.turned, 1)
            vec.tensor_copy(rawT[:, 0:4, :].rearrange("p k d -> p (k d)"), m.ps[4][:, :])
            vec.tensor_copy(rawT[:, 4, :], m.ps[5][:, 0:D]).then_inc(s.mapsc, 1)
            vec.wait_ge(s.maps, 1)
            vec.wait_ge(s.mapsc, 1)
            vec.tensor_copy(m.maps[:, 0:2, :].rearrange("p k d -> p (k d)"), m.ps[6][:, 0:2 * D])
            vec.tensor_copy(m.maps[:, 2, :], rawT[:, 4, :])

            def step(t, u):
                reached(vec, s.turnedr, t - 1)
                for j in range(GRP):
                    img = t * GRP + j
                    e = vec.tensor_scalar(ln[:, u % 2, j, :], m.b[:, bass.ds(img, 1), :], fac[:, 0, bass.ds(img, 1)],
                                          fac[:, 1, bass.ds(img, 1)], ALU.subtract, ALU.mult)
                e.then_inc(s.staged, 1)
            sweep(vec, step, 0)


LEAD = 3


def stage_attention(nc, held, m):
    s = semaphores(nc, held, "attn", "proj_k proj_v k_high k_low k_squared k_norm k_norm_copied v_copied turned v_high "
                   "v_low proj_q q_high q_low q_squared q_norm q_norm_copied scores dist inner outer high low "
                   "summed_high summed_low left_a left_b sums merged scaled added")
    a = m.a[:, :, :].rearrange("p a b -> p (a b)")
    NC = SEQ // 512
    START = 2
    TILES = NQC * KT

    def results(c, slot):
        return a[:, bass.ds((c - slot) * QC, 2 * QC)].rearrange("p (j s d) -> p j s d", j=4, s=2)

    def both(j):
        return m.ps[4 + j][:, 0:2 * D + 2].rearrange("p (s d) -> p s d", s=2)[:, :, 0:D]

    with nc.Block() as block:
        @block.tensor
        def _(pe):
            for sem in (s.summed_high, s.summed_low):
                pe.sem_inc(sem, START)

            def project_queries(c):
                pe.wait_ge(s.q_norm_copied, START + c)
                pe.matmul(m.ps[3][:, :], m.maps[:, 0, :], a[:, bass.ds(c * QC, QC)], start=True, stop=True)\
                    .then_inc(s.proj_q, 1)

            def query_norms(c, slot):
                pe.wait_ge(s.q_squared, c + 1)
                pe.wait_ge(s.q_low, c + 1)
                pe.matmul(m.ps[3][:, :], m.halves[:, :], m.q2[:, slot, :], start=True, stop=True).then_inc(s.q_norm, 1)

            def norm_and_turn(b, ch):
                n = b * NC + ch
                pe.wait_ge(s.k_squared, n + 1)
                for j in range(4):
                    mm = pe.matmul(m.ps[6][:, ch * 4 + j:ch * 4 + j + 1], m.wt[:, ch % 2, j * P:j * P + P],
                                   m.halves[:, 0:1], start=True, stop=True)
                mm.then_inc(s.k_norm, 1)
                if ch >= 2:
                    pe.wait_ge(s.v_low, n - 1)
                pe.wait_ge(s.v_copied, n + 1)
                for j in range(4):
                    mm = pe.transpose(m.ps[7 if ch % 2 else 2][:, j * P:j * P + P], m.dist[:, ch % 2, j * P:j * P + P],
                                      m.ident)
                mm.then_inc(s.turned, 1)

            with pe.Fori(0, NB) as b:
                pe.wait_ge(s.dist, START + b * TILES)
                pe.wait_ge(s.left_a, START + b * (NQC * 2))
                pe.wait_ge(s.left_b, START + b * (NQC * 2))
                project_queries(b * NQC)
                for ch in range(NC):
                    n = b * NC + ch
                    src = a[:, bass.ds(n * 512, 512)]
                    if ch >= 2:
                        pe.wait_ge(s.k_low, n - 1)
                        pe.wait_ge(s.k_squared, n - 1)
                    pe.matmul(m.ps[ch % 2][:, :], m.maps[:, 1, :], src, start=True, stop=True).then_inc(s.proj_k, 1)
                    if ch >= 2:
                        pe.wait_ge(s.v_copied, n - 1)
                    pe.matmul(m.ps[4 + ch % 2][:, :], m.maps[:, 2, :], src, start=True, stop=True).then_inc(s.proj_v, 1)
                    if ch == 0:
                        query_norms(b * NQC, 0)
                    else:
                        norm_and_turn(b, ch - 1)
                norm_and_turn(b, NC - 1)
                for sem in (s.k_low, s.k_squared, s.v_low, s.v_copied):
                    pe.wait_ge(sem, (b + 1) * NC)
                pe.wait_ge(s.k_norm_copied, b + 1)

                def run(qc, slot, first, last):
                    c = b * NQC + qc
                    n0 = c * KT

                    def scores(k):
                        tile, q = k % KT, (slot + k // KT) % 2
                        if k == KT:
                            pe.wait_ge(s.q_low, c + 2)
                        if not first or k >= LEAD:
                            pe.wait_ge(s.dist, START + n0 + k + 1 - (2 if tile < 2 else 3))
                        for i, (key, query) in enumerate(((m.kH, m.qH), (m.kL, m.qH), (m.kH, m.qL))):
                            mm = pe.matmul(m.ps[tile % 3][:, :], key[:, tile * P:tile * P + P], query[:, q, :],
                                           start=(i == 0), stop=(i == 2))
                        mm.then_inc(s.scores, 1)

                    def sum_low(k):
                        pe.wait_ge(s.low, START + n0 + k + 1)
                        for j in range(4):
                            mm = pe.matmul(m.ps[4 + j][:, 0:D + 1], m.wL[:, k % 2, j * P:j * P + P],
                                           m.v[:, k, 0:D + 1], start=False, stop=(k == KT - 1))
                        mm.then_inc(s.summed_low, 1)
                    if first:
                        for k in range(LEAD):
                            scores(k)
                    for k in range(KT):
                        if k + LEAD < (KT if last else KT + LEAD):
                            scores(k + LEAD)
                        if k == 12 and not last:
                            project_queries(c + 1)
                        if k == 22 and not last:
                            query_norms(c + 1, 1 - slot)
                        pe.wait_ge(s.high, START + n0 + k + 1)
                        for j in range(4):
                            if k == 0 and not first:
                                pe.wait_ge(s.left_a if j < 2 else s.left_b, START + (c - 1) * 2 + j % 2 + 1)
                            mm = pe.matmul(m.ps[4 + j][:, 0:2 * D + 1], m.wH[:, k % 2, j * P:j * P + P],
                                           m.v[:, k, 0:2 * D + 1], start=(k == 0), stop=False)
                        mm.then_inc(s.summed_high, 1)
                        if k > 0:
                            sum_low(k - 1)
                    sum_low(KT - 1)
                run(0, 0, True, False)
                with pe.Fori(0, NQC // 2 - 1) as pair:
                    for i in (1, 2):
                        run(pair * 2 + i, i % 2, False, False)
                run(NQC - 1, 1, False, True)

        @block.vector
        def _(vec):
            for sem in (s.q_norm_copied, s.dist, s.high, s.left_a, s.added):
                vec.sem_inc(sem, START)

            def high_queries(c, slot):
                vec.wait_ge(s.proj_q, c + 1)
                vec.tensor_copy(m.qH[:, slot, :], m.ps[3][:, :]).then_inc(s.q_high, 1)

            def low_queries(c, slot):
                vec.wait_ge(s.q_high, c + 1)
                vec.tensor_tensor(m.qL[:, slot, :], m.ps[3][:, :], m.qH[:, slot, :], ALU.subtract).then_inc(s.q_low, 1)

            with vec.Fori(0, NB) as b:
                high_queries(b * NQC, 0)
                low_queries(b * NQC, 0)
                for ch in range(NC + 1):
                    n = b * NC + ch
                    part = slice(ch * 512, ch * 512 + 512)
                    if ch < NC:
                        vec.wait_ge(s.proj_k, n + 1)
                        vec.tensor_copy(m.kH[:, part], m.ps[ch % 2][:, :]).then_inc(s.k_high, 1)
                    if ch < NC:
                        vec.wait_ge(s.k_high, n + 1)
                        vec.tensor_tensor(m.kL[:, part], m.ps[ch % 2][:, :], m.kH[:, part], ALU.subtract)\
                            .then_inc(s.k_low, 1)
                    if ch > 0:
                        tiles = slice(4 * ch - 4, 4 * ch)
                        vec.wait_ge(s.v_high, n)
                        vec.tensor_tensor(m.v[:, tiles, D + 1:2 * D + 1],
                                          m.ps[2 if ch % 2 else 7][:, :].rearrange("p (j d) -> p j d", j=4),
                                          m.v[:, tiles, 0:D], ALU.subtract).then_inc(s.v_low, 1)
                vec.wait_ge(s.k_norm, (b + 1) * NC)
                vec.tensor_copy(m.k2[:, :], m.ps[6][:, 0:KT]).then_inc(s.k_norm_copied, 1)
                vec.wait_ge(s.k_norm_copied, b + 1)

                def distances(qc, slot, k):
                    c = b * NQC + qc + k // KT
                    t, slot = (b * NQC + qc) * KT + k, (slot + k // KT) % 2
                    if k % KT == 0:
                        vec.wait_ge(s.q_norm_copied, START + c + 1)
                    vec.wait_ge(s.scores, t + 1)
                    vec.wait_ge(s.outer, START + t - 1)
                    vec.scalar_tensor_tensor(out=m.dist[:, k % 2, :], in0=m.ps[k % KT % 3][:, :],
                                             scalar=m.k2[:, k % KT:k % KT + 1], in1=m.q2[:, slot, :],
                                             op0=ALU.subtract, op1=ALU.subtract).then_inc(s.dist, 1)

                def high_part(qc, k):
                    t = (b * NQC + qc) * KT + k
                    vec.wait_ge(s.outer, START + t + 1)
                    vec.wait_ge(s.summed_high, START + t - 1)
                    vec.wait_ge(s.low, START + t - 1)
                    vec.tensor_copy(m.wH[:, k % 2, :], m.wt[:, k % 2, :]).then_inc(s.high, 1)

                def leave_banks(qc, slot):
                    c = b * NQC + qc
                    vec.wait_ge(s.summed_high, START + (c + 1) * KT)
                    vec.wait_ge(s.summed_low, START + (c + 1) * KT)
                    vec.wait_ge(s.added, START + c * 2)
                    for j in (0, 1):
                        vec.tensor_copy(m.sums[:, j:j + 1], m.ps[4 + j][:, D:D + 1])
                        vec.tensor_copy(results(c, slot)[:, j], both(j)).then_inc(s.left_a, 1)

                def merge(qc, slot, half):
                    c = b * NQC + qc
                    vec.wait_ge(s.left_a, START + (c + 1) * 2)
                    vec.wait_ge(s.left_b, START + (c + 1) * 2)
                    part = slice(2 * half, 2 * half + 2)
                    vec.reciprocal(m.rden[:, part], m.sums[:, part])
                    r = results(c, slot)
                    vec.tensor_tensor(r[:, part, 0], r[:, part, 0], r[:, part, 1], ALU.add).then_inc(s.merged, 1)

                def divide(qc, slot, half):
                    c = b * NQC + qc
                    r = results(c, slot)
                    vec.wait_ge(s.merged, c * 2 + half + 1)
                    for j in (2 * half, 2 * half + 1):
                        e = vec.scalar_tensor_tensor(out=r[:, j, 0], in0=r[:, j, 0], scalar=m.rden[:, j:j + 1],
                                                     in1=m.unit[:, :], op0=ALU.mult, op1=ALU.mult)
                    e.then_inc(s.scaled, 1)

                def add(qc, slot, half):
                    c = b * NQC + qc
                    vec.wait_ge(s.scaled, c * 2 + half + 1)
                    x = m.b[:, bass.ds(c * 4 + 2 * half, 2), :]
                    vec.tensor_tensor(x, results(c, slot)[:, 2 * half:2 * half + 2, 0], x, ALU.add).then_inc(s.added, 1)

                def statistics(qc, slot, half):
                    c = b * NQC + qc
                    vec.wait_ge(s.added, START + c * 2 + half + 1)
                    part = 2 * half
                    vec.tensor_copy(m.rden[:, 4 + part:6 + part], m.rden[:, part:part + 2])
                    for j in (2 * half, 2 * half + 1):
                        row = bass.ds(c * 4 + j, 1)
                        vec.bn_stats(m.st[:, row, :], m.b[:, row, :])

                LATER = {2: (merge, 0), 3: (merge, 1), 5: (divide, 0), 6: (divide, 1), 8: (add, 0), 10: (add, 1),
                         12: (statistics, 0), 14: (statistics, 1)}

                def run(qc, slot, first, last):
                    for k in range(KT):
                        if k + 1 < KT or not last:
                            distances(qc, slot, k + 1)
                        high_part(qc, k)
                        if not first:
                            if k == 0:
                                leave_banks(qc - 1, 1 - slot)
                            if k in LATER:
                                part, half = LATER[k]
                                part(qc - 1, 1 - slot, half)
                        if k == 16 and not last:
                            high_queries(b * NQC + qc + 1, 1 - slot)
                        if k == 18 and not last:
                            low_queries(b * NQC + qc + 1, 1 - slot)
                distances(0, 0, 0)
                run(0, 0, True, False)
                with vec.Fori(0, NQC // 2 - 1) as pair:
                    for i in (1, 2):
                        run(pair * 2 + i, i % 2, False, False)
                run(NQC - 1, 1, False, True)
                leave_banks(NQC - 1, 1)
                for part, half in LATER.values():
                    part(NQC - 1, 1, half)

        @block.scalar
        def _(act):
            for sem in (s.outer, s.left_b):
                act.sem_inc(sem, START)

            def square_queries(c, slot):
                act.wait_ge(s.proj_q, c + 1)
                act.wait_ge(s.q_low, c + 1)
                act.activation(m.q2[:, slot, :], m.ps[3][:, :], ACT.Square).then_inc(s.q_squared, 1)

            def copy_norms(c, slot):
                act.wait_ge(s.q_norm, c + 1)
                act.copy(m.q2[:, slot, :], m.ps[3][:, :]).then_inc(s.q_norm_copied, 1)

            with act.Fori(0, NB) as b:
                act.wait_ge(s.low, START + b * TILES)
                act.wait_ge(s.summed_high, START + b * TILES)
                act.wait_ge(s.summed_low, START + b * TILES)
                square_queries(b * NQC, 0)
                for ch in range(NC + 1):
                    n = b * NC + ch
                    if ch < NC:
                        act.wait_ge(s.proj_v, n + 1)
                        if ch >= 2:
                            act.wait_ge(s.turned, n - 1)
                        act.copy(m.dist[:, ch % 2, :], m.ps[4 + ch % 2][:, :]).then_inc(s.v_copied, 1)
                    if ch == 0:
                        copy_norms(b * NQC, 0)
                    if ch < NC:
                        act.wait_ge(s.k_low, n + 1)
                        if ch >= 2:
                            act.wait_ge(s.k_norm, n - 1)
                        act.activation(m.wt[:, ch % 2, :], m.ps[ch % 2][:, :], ACT.Square).then_inc(s.k_squared, 1)
                    if ch > 0:
                        act.wait_ge(s.turned, n)
                        act.copy(m.v[:, 4 * ch - 4:4 * ch, 0:D],
                                 m.ps[2 if ch % 2 else 7][:, :].rearrange("p (j d) -> p j d", j=4)).then_inc(s.v_high, 1)
                act.wait_ge(s.k_norm, (b + 1) * NC)

                def leave_banks(qc, slot):
                    c = b * NQC + qc
                    act.wait_ge(s.summed_high, START + (c + 1) * KT)
                    act.wait_ge(s.summed_low, START + (c + 1) * KT)
                    act.wait_ge(s.added, START + c * 2)
                    for j in (2, 3):
                        act.copy(m.sums[:, j:j + 1], m.ps[4 + j][:, D:D + 1])
                        act.copy(results(c, slot)[:, j], both(j)).then_inc(s.left_b, 1)

                def run(qc, slot, first, last):
                    n0 = (b * NQC + qc) * KT
                    for k in range(KT):
                        act.wait_ge(s.dist, START + n0 + k + 1)
                        act.activation(m.dist[:, k % 2, :], m.dist[:, k % 2, :], ACT.Exp, scale=2.0).then_inc(s.inner, 1)
                        act.wait_ge(s.low, START + n0 + k - 1)
                        act.wait_ge(s.inner, n0 + k + 1)
                        act.activation(m.wt[:, k % 2, :], m.dist[:, k % 2, :], ACT.Exp).then_inc(s.outer, 1)
                        if k == 0 and not first:
                            leave_banks(qc - 1, 1 - slot)
                        if k == 20 and not last:
                            square_queries(b * NQC + qc + 1, 1 - slot)
                        if k == 25 and not last:
                            copy_norms(b * NQC + qc + 1, 1 - slot)
                run(0, 0, True, False)
                with act.Fori(0, NQC // 2 - 1) as pair:
                    for i in (1, 2):
                        run(pair * 2 + i, i % 2, False, False)
                run(NQC - 1, 1, False, True)
                leave_banks(NQC - 1, 1)

        @block.gpsimd
        def _(pool):
            pool.sem_inc(s.low, START)
            with pool.Fori(0, NB * NQC) as c:
                for k in range(KT):
                    pool.wait_ge(s.high, START + c * KT + k + 1)
                    pool.wait_ge(s.summed_low, START + c * KT + k - 1)
                    pool.tensor_tensor(m.wL[:, k % 2, :], m.wt[:, k % 2, :], m.wH[:, k % 2, :], ALU.subtract)\
                        .then_inc(s.low, 1)


def stage_router(nc, held, m, ins):
    s = semaphores(nc, held, "router", "loaded cleared v factor rooted normed turned copied stored logits shifted exp "
                   "high low gates gates_turned gates_copied biased added")
    SIDE = P // EXPERTS

    with nc.Block() as block:
        @block.sync
        def _(sp):
            with nc.allow_non_contiguous_dma(reason="weights of the experts, once"):
                sp.dma_start(m.rw[:, :], ins['L1_ffn_router_w']).then_inc(s.loaded, 16)
                sp.dma_start(m.rb[:, :], ins['L1_ffn_router_b'].partition_broadcast(P)).then_inc(s.loaded, 16)
                sp.dma_start(m.w8[:, :].rearrange("p (e c) -> p e c", e=EXPERTS),
                             ins['L1_ffn_expert_w'].rearrange("e d c -> d e c")).then_inc(s.loaded, 16)
                sp.wait_ge(s.cleared, 1)
                for i in range(SIDE):
                    sp.dma_start(m.eb[i * EXPERTS:(i + 1) * EXPERTS, i * D:(i + 1) * D], ins['L1_ffn_expert_b'])\
                        .then_inc(s.loaded, 16)

        @block.gpsimd
        def _(pool):
            pool.memset(m.eb[:, :], 0.0).then_inc(s.cleared, 1)

        @block.tensor
        def _(pe):
            pe.wait_ge(s.loaded, 16 * (3 + SIDE))

            def step(t, u):
                if live(t):
                    pe.wait_ge(s.normed, t + 1)
                    reached(pe, s.copied, t - 1)
                    for j in range(GRP):
                        mm = pe.transpose(m.ps[u % 2][:, j * P:j * P + P], m.ln[:, u % 2, j, :], m.ident)
                    mm.then_inc(s.turned, 1)
                g, v = t - 1, (u - 1) % 2
                if live(g):
                    pe.wait_ge(s.copied, g + 1)
                    for j in range(GRP):
                        n = g * GRP + j
                        mm = pe.matmul(m.logits[:, bass.ds(n * EXPERTS, EXPERTS)], m.lnT[:, v, j, :], m.rw[:, :],
                                       start=True, stop=True)
                    mm.then_inc(s.logits, 1)
            sweep(pe, step, 1)
            pe.wait_ge(s.gates, 1)
            for i in range(NI // SIDE):
                mm = pe.transpose(m.ps[i // 4][:, i % 4 * P:i % 4 * P + P],
                                  m.gate[:, i * SIDE:(i + 1) * SIDE, :].rearrange("p t e -> p (t e)"), m.ident)
            mm.then_inc(s.gates_turned, 1)
            pe.wait_ge(s.gates_copied, 2)
            for g in range(NG):
                reached(pe, s.added, g - 3)
                q = g % (SIDE // GRP)
                pe.matmul(m.ps[4 + g % 4][:, :], m.gT[:, g * GRP // SIDE, :], m.eb[:, q * 512:q * 512 + 512],
                          start=True, stop=True).then_inc(s.biased, 1)

        @block.scalar
        def _(act):
            act.wait_ge(s.factor, 1)
            act.activation(m.fac[:, 1], m.fac[:, 1], ACT.Sqrt).then_inc(s.rooted, 1)

            def step(t, u):
                act.wait_ge(s.turned, t + 1)
                reached(act, s.logits, t - 1)
                reached(act, s.stored, t - 1)
                act.copy(m.lnT[:, u % 2], banked(m, u % 2)).then_inc(s.copied, 1)
            sweep(act, step, 0)
            act.wait_ge(s.loaded, 16 * (3 + SIDE))
            act.copy(m.w8H[:, :], m.w8[:, :]).then_inc(s.high, 1)
            act.wait_ge(s.shifted, 1)
            act.activation(m.ex[:, :, :], m.ex[:, :, :], ACT.Exp).then_inc(s.exp, 1)
            act.wait_ge(s.gates_turned, 1)
            for i in range(2):
                act.copy(m.gT[:, 4 * i:4 * i + 4, :], banked(m, i)).then_inc(s.gates_copied, 1)

        @block.vector
        def _(vec):
            c = Chain(vec, s.v)
            row_factors(vec, c, m.st, m.fac, s.factor, s.rooted)

            def step(t, u):
                if live(t):
                    reached(vec, s.turned, t - 1)
                    for j in range(GRP):
                        img = bass.ds(t * GRP + j, 1)
                        e = vec.tensor_scalar(m.ln[:, u % 2, j, :], m.b[:, img, :], m.fac[:, 0, img], m.fac[:, 1, img],
                                              ALU.subtract, ALU.mult)
                    e.then_inc(s.normed, 1)
                g, v = t - 2, u % 2
                if live(g):
                    vec.wait_ge(s.copied, g + 1)
                    vec.tensor_copy(group(m.a, g), m.lnT[:, v]).then_inc(s.stored, 1)
            sweep(vec, step, 2)
            vec.wait_ge(s.high, 1)
            vec.tensor_tensor(m.w8L[:, :], m.w8[:, :], m.w8H[:, :], ALU.subtract)

            logit, ex, cnt, win, gate = m.logit, m.ex, m.cnt, m.win, m.gate
            top, total = m.g1[:, 0], m.g1[:, 1]
            vec.wait_ge(s.logits, NG)
            c.step(vec.tensor_tensor(logit[:, :, :], m.logits.rearrange("p (t e) -> p t e", e=EXPERTS),
                                     over(m.rb[:, :], 1, NI), ALU.add))
            c.step(vec.tensor_reduce(top, logit[:, :, :], AX.X, ALU.max))
            vec.tensor_tensor(ex[:, :, :], logit[:, :, :], over(top, 2, EXPERTS), ALU.subtract).then_inc(s.shifted, 1)
            for e in range(EXPERTS):
                vec.memset(cnt[:, :, e:e + 1], float(EXPERTS - 1 - e))
            for d in range(1, EXPERTS):
                first, later = slice(0, EXPERTS - d), slice(d, EXPERTS)
                c.step(vec.tensor_tensor(win[:, :, first], logit[:, :, first], logit[:, :, later], ALU.is_ge))
                c.step(vec.tensor_tensor(cnt[:, :, first], cnt[:, :, first], win[:, :, first], ALU.subtract))
                c.step(vec.tensor_tensor(cnt[:, :, later], cnt[:, :, later], win[:, :, first], ALU.add))
            c.step(vec.tensor_scalar(cnt[:, :, :], cnt[:, :, :], 1.5, None, ALU.is_lt))
            vec.wait_ge(s.exp, 1)
            c.step(vec.tensor_tensor(gate[:, :, :], ex[:, :, :], cnt[:, :, :], ALU.mult))
            c.step(vec.tensor_reduce(total, gate[:, :, :], AX.X, ALU.add))
            c.step(vec.reciprocal(total, total))
            vec.tensor_tensor(gate[:, :, :], gate[:, :, :], over(total, 2, EXPERTS), ALU.mult).then_inc(s.gates, 1)
            for g in range(NG):
                vec.wait_ge(s.biased, g + 1)
                x = m.b[:, g * GRP:g * GRP + GRP, :]
                vec.tensor_tensor(x, banked(m, 4 + g % 4), x, ALU.add).then_inc(s.added, 1)


def stage_experts(nc, held, m, out):
    s = semaphores(nc, held, "experts", "high low tiles scaled_a scaled_b scaled_sum reduced result stored0 stored1")
    out_img = out.rearrange("b t h w -> h (b t) w")
    stored = [s.stored0, s.stored1]

    def gates(n, e, count):
        return m.gate[:, bass.ds(n, 1), e:e + count].rearrange("p a e -> p (a e)")

    with nc.Block() as block:
        @block.sync
        def _(sp):
            with sp.Fori(0, NG // 2) as it:
                for u in (0, 1):
                    g = it * 2 + u
                    sp.wait_ge(s.result, g + 1)
                    sp.dma_start(out_img[:, bass.ds(g * GRP, GRP), :], m.y[:, u]).then_inc(stored[u], 16)
            for u in (0, 1):
                sp.wait_ge(stored[u], NG // 2 * 16)

        @block.tensor
        def _(pe):
            def step(t, u):
                pe.wait_ge(s.low, t + 1)
                for j in range(GRP):
                    n = t * GRP + j
                    reached(pe, s.scaled_a, n - 1)
                    reached(pe, s.scaled_b, n - 1)
                    for h in (0, 1):
                        part = slice(512 * h, 512 * h + 512)
                        bank = m.ps[4 + 2 * (j % 2) + h][:, :]
                        pe.matmul(bank, m.lnH[:, u % 2, j, :], m.w8H[:, part], start=True, stop=False)
                        pe.matmul(bank, m.lnH[:, u % 2, j, :], m.w8L[:, part], start=False, stop=False)
                        mm = pe.matmul(bank, m.lnL[:, u % 2, j, :], m.w8H[:, part], start=False, stop=True)
                    mm.then_inc(s.tiles, 1)
            sweep(pe, step, 0)

        @block.scalar
        def _(act):
            def high(t, u):
                reached(act, s.tiles, (t - 1) * GRP)
                act.copy(m.lnH[:, u % 2], group(m.a, t)).then_inc(s.high, 1)

            def step(t, u):
                g = t - 1
                for j in range(GRP):
                    n = g * GRP + j
                    if j == 1 and live(t):
                        high(t, u)
                    if live(g):
                        act.wait_ge(s.tiles, n + 1)
                        reached(act, s.scaled_sum, n - 1)
                        for e in range(4):
                            o = act.activation(m.pb[:, j % 2, e, :], m.ps[5 + 2 * (j % 2)][:, e * D:e * D + D], ACT.Copy,
                                               scale=gates(n, 4 + e, 1))
                        o.then_inc(s.scaled_b, 1)
            sweep(act, step, 1)

        @block.gpsimd
        def _(pool):
            def residual(g, v):
                pool.wait_ge(s.reduced, (g + 1) * GRP)
                pool.tensor_tensor(m.y[:, v], m.y[:, v], group(m.b, g), ALU.add).then_inc(s.result, 1)

            def step(t, u):
                for j in range(GRP):
                    n = t * GRP + j
                    if live(t):
                        pool.wait_ge(s.scaled_a, n + 1)
                        pool.wait_ge(s.scaled_b, n + 1)
                        reached(pool, s.reduced, n - 1)
                        pool.tensor_tensor(m.pc[:, j % 2], m.pa[:, j % 2], m.pb[:, j % 2], ALU.add)\
                            .then_inc(s.scaled_sum, 1)
                    if j == 1 and live(t - 1):
                        residual(t - 1, (u - 1) % 2)
            sweep(pool, step, 1)

        @block.vector
        def _(vec):
            def low(t, u):
                vec.wait_ge(s.high, t + 1)
                reached(vec, s.tiles, (t - 1) * GRP)
                vec.tensor_tensor(m.lnL[:, u % 2], group(m.a, t), m.lnH[:, u % 2], ALU.subtract).then_inc(s.low, 1)

            def reduce(g, v, j):
                n = g * GRP + j
                vec.wait_ge(s.scaled_sum, n + 1)
                if j == 0:
                    reached(vec, stored[v], (g - v) * 8)
                vec.tensor_reduce(m.y[:, v, j, :], m.pc[:, j % 2].rearrange("p e c -> p c e"), AX.X, ALU.add)\
                    .then_inc(s.reduced, 1)

            def step(t, u):
                g, v = t - 1, (u - 1) % 2
                for j in range(GRP):
                    n = g * GRP + j
                    if live(g):
                        vec.wait_ge(s.tiles, n + 1)
                        reached(vec, s.scaled_sum, n - 1)
                        src = m.ps[4 + 2 * (j % 2)][:, :].rearrange("p (e c) -> p e c", e=4)
                        vec.tensor_tensor(m.pa[:, j % 2], src, over(gates(n, 0, 4), 2, D), ALU.mult)\
                            .then_inc(s.scaled_a, 1)
                    if j > 0 and live(g):
                        reduce(g, v, j - 1)
                    if j == 0 and live(t - 2):
                        reduce(t - 2, u % 2, GRP - 1)
                    if j == 1 and live(t):
                        low(t, u)
            sweep(vec, step, 2)


def build(nc, ins, const, where, out, upto=99):
    with ExitStack() as ctx:
        tok = nc.dram_tensor("tokens_scratch", (NI, NH, NW), F32, kind="Internal").ap()
        mix = nc.dram_tensor("mixed_scratch", (NI, NH, NW), F32, kind="Internal").ap()
        m = memory(nc, ctx, where)
        held = []
        stages = [
            lambda: stage_tokens(nc, held, m, ins, tok, const),
            lambda: stage_forward(nc, held, m, tok),
            lambda: stage_modes(nc, held, m),
            lambda: stage_weights(nc, held, m),
            lambda: stage_scores(nc, held, m),
            lambda: stage_mix(nc, held, m, mix),
            lambda: stage_inverse(nc, held, m, 'proj', mix=mix),
            lambda: stage_factors(nc, held, m, 'proj'),
            lambda: stage_attended(nc, held, m),
            lambda: stage_mixer(nc, held, m, 1),
            lambda: stage_inverse(nc, held, m, 'mix1', ins=ins),
            lambda: stage_mixer(nc, held, m, 2),
            lambda: stage_inverse(nc, held, m, 'mix2'),
            lambda: stage_factors(nc, held, m, 'mix2'),
            lambda: stage_residual(nc, held, m, ins),
            lambda: stage_normed(nc, held, m, ins),
            lambda: stage_attention(nc, held, m),
            lambda: stage_router(nc, held, m, ins),
            lambda: stage_experts(nc, held, m, out),
        ]
        for i, stage in enumerate(stages[:upto]):
            if i == 8:
                nc.clear_and_free_semaphores(held)
                held.clear()
                nc.all_engine_barrier()
            stage()


NAMES = ['x'] + SCALARS + [
    'L0_conv_key_w', 'L0_conv_key_skip_w', 'L0_conv_key_skip_b', 'L0_conv_query_w', 'L0_conv_query_skip_w',
    'L0_conv_query_skip_b', 'L0_conv_value_w', 'L0_conv_value_skip_w', 'L0_conv_value_skip_b', 'L0_conv_proj_w',
    'L0_conv_proj_skip_w', 'L0_conv_mixer_w1', 'L0_conv_mixer_w2', 'L1_attn_rotation_params',
    'L1_attn_entangle_params', 'L1_attn_Wq', 'L1_attn_Wk', 'L1_attn_Wv', 'L1_ffn_router_w', 'L1_ffn_router_b',
    'L1_ffn_expert_w', 'L1_ffn_expert_b']


def kernel(**inputs):
    import concourse.bacc as bacc
    from concourse.bass_utils import run_bass_kernel_spmd

    nc = bacc.Bacc("TRN2", target_bir_lowering=False, num_devices=1)
    arrays, ins = {}, {}
    for name in NAMES:
        a = np.ascontiguousarray(inputs[name])
        arrays[f"in_{name}"] = a
        ins[name] = nc.dram_tensor(f"in_{name}", a.shape, mybir.dt.from_np(a.dtype), kind="ExternalInput").ap()
    table, where = tables()
    arrays["tables"] = table
    const = nc.dram_tensor("tables", table.shape, F32, kind="ExternalInput").ap()
    out = nc.dram_tensor("result", inputs['x'].shape, F32, kind="ExternalOutput").ap()
    build(nc, ins, const, where, out)
    got = run_bass_kernel_spmd(nc, [arrays], core_ids=[0])
    return got.results[0]["result"]
```
